# Optimizing a Trainium2 kernel written in Bass

```python
import numpy as np
import jax
import jax.numpy as jnp

def _softmax(x, axis=-1):
    return jax.nn.softmax(x, axis=axis)

def _gelu(x):
    return jax.nn.gelu(x, approximate=True)

def _silu(x):
    return jax.nn.silu(x)

def _sigmoid(x):
    return jax.nn.sigmoid(x)

def _layernorm(x, axis=-1, eps=1e-05):
    m = jnp.mean(x, axis=axis, keepdims=True)
    v = jnp.var(x, axis=axis, keepdims=True)
    return (x - m) / jnp.sqrt(v + eps)

def _scatter_add(tgt, idx, src, axis=0):
    return tgt.at[idx].add(src)

def _segment_sum(src, seg, n):
    return jax.ops.segment_sum(src, seg, n)
kernel_name = 'mk_decoder_preln_d1_seqx_r4_80fc40'

def setup_inputs(seed: int=0):
    np.random.seed(seed)
    _w = jnp.asarray

    def _rec_inputs():
        import jax
        import jax.numpy as jnp
        _rk = jax.random.key(seed)
        x = 7.22e-05 + 1 * jax.random.normal(jax.random.fold_in(_rk, 1), (8, 256, 512), jnp.float32)
        _lenS = 256 - jax.random.randint(jax.random.fold_in(_rk, 7), (8,), 0, max(1, 256 // 4) + 1, jnp.int32)
        _lenS2 = 256 - jax.random.randint(jax.random.fold_in(_rk, 8), (8,), 0, max(1, 256 // 4) + 1, jnp.int32)
        _ctx_512P = jax.random.normal(jax.random.fold_in(_rk, 11), (8, 16, 128), jnp.float32)
        _ctx_512c = jax.random.dirichlet(jax.random.fold_in(_rk, 511), 0.3 * jnp.ones((16,), jnp.float32), (8, 256))
        _ctx_512t = jnp.einsum('bsk,bkd->bsd', _ctx_512c, _ctx_512P)
        _ctx_512t = _ctx_512t * jax.lax.rsqrt(jnp.mean(jnp.square(_ctx_512t)) + 1e-12) * 0.953939
        ctx_512 = -0.000514642 + 1.00011 * (_ctx_512t + 0.3 * jax.random.normal(jax.random.fold_in(_rk, 611), (8, 256, 128), jnp.float32))
        return (x, ctx_512)
    x, ctx_512 = _rec_inputs()

    def _L0_attn_setup():
        import jax, jax.numpy as jnp
        import numpy as np
        DIM = 512
        N_HEADS = 16
        N_KV_HEADS = 4
        WINDOW = 128
        GLOBAL = 64

        def alibi_slopes(num_heads):
            closest_pow2 = 2.0 ** np.floor(np.log2(num_heads))
            base = 2.0 ** (-2.0 ** (-(np.log2(closest_pow2) - 3.0)))
            powers = np.arange(1, 1 + num_heads, dtype=np.float32)
            return jnp.asarray(base ** powers, dtype=jnp.float32)

        def window_allowed(seq_len):
            i = jnp.arange(seq_len)[:, None]
            j = jnp.arange(seq_len)[None, :]
            inside = (j >= i - WINDOW // 2) & (j <= i + WINDOW // 2)
            glob = (i < GLOBAL) | (j < GLOBAL)
            return inside | glob
        key = jax.random.key(seed)
        k1, k2, k3, k4 = jax.random.split(key, 4)
        B, S, D = (2, 512, DIM)
        kv_feat = 2 * D * N_KV_HEADS // N_HEADS
        std = 0.02
        x = jax.random.normal(k1, (B, S, D), dtype=jnp.float32)
        Wq = jax.random.normal(k2, (D, D), dtype=jnp.float32) * std
        Wkv = jax.random.normal(k3, (D, kv_feat), dtype=jnp.float32) * std
        Wo = jax.random.normal(k4, (D, D), dtype=jnp.float32) * std
        bo = jnp.zeros((D,), dtype=jnp.float32)
        return {'x': x, 'Wq': Wq, 'Wkv': Wkv, 'Wo': Wo, 'bo': bo}
    _L0_attn_all = _L0_attn_setup()
    _L0_attn_in = {k: v for k, v in _L0_attn_all.items() if k in ('Wq', 'Wkv', 'Wo', 'bo')}
    del _L0_attn_all

    def _L0_xattn_setup():
        import jax, jax.numpy as jnp
        import numpy as np
        import math
        NUM_Q_HEADS = 32
        NUM_KV_HEADS = 8
        key = jax.random.key(seed)
        k1, k2, k3 = jax.random.split(key, 3)
        B, S, E = (2, 512, 512)
        kv_E = NUM_KV_HEADS * (E // NUM_Q_HEADS)
        q = jax.random.normal(k1, (B, S, E), dtype=jnp.float32)
        k = jax.random.normal(k2, (B, S, kv_E), dtype=jnp.float32)
        v = jax.random.normal(k3, (B, S, kv_E), dtype=jnp.float32)
        return {'q': q, 'k': k, 'v': v}
    _L0_xattn_all = _L0_xattn_setup()
    _L0_xattn_in = {k: v for k, v in _L0_xattn_all.items() if k in ()}
    del _L0_xattn_all

    def _L0_ffn_setup():
        import jax, jax.numpy as jnp
        import numpy as np
        E = 32
        K = 4
        G = 4
        TG = 2
        H = 512
        F = 256
        FS = 512
        SCALE = 2.0
        B, S = (2, 256)
        N = B * S
        CAP = 2 * (N * K // E)

        def _gate(x, gate_w, gate_bias):
            logits = x @ gate_w.T
            scores = jax.nn.sigmoid(logits)
            sc = scores + gate_bias
            n = x.shape[0]
            grp = sc.reshape(n, G, E // G)
            group_scores = jax.lax.top_k(grp, 2)[0].sum(-1)
            _, gidx = jax.lax.top_k(group_scores, TG)
            gmask = jnp.zeros((n, G), sc.dtype).at[jnp.arange(n)[:, None], gidx].set(1.0)
            smask = jnp.repeat(gmask, E // G, axis=1)
            tmp = jnp.where(smask > 0, sc, 0.0)
            _, topk_idx = jax.lax.top_k(tmp, K)
            topk_w = jnp.take_along_axis(scores, topk_idx, axis=1)
            topk_w = topk_w / (topk_w.sum(-1, keepdims=True) + 1e-20)
            return (topk_idx, topk_w * SCALE)

        def _moe(x, topk_idx, topk_w, w1, w2, w3):
            n = x.shape[0]
            flat_e = topk_idx.reshape(-1)
            oh = jax.nn.one_hot(flat_e, E, dtype=jnp.int32)
            pos = (jnp.cumsum(oh, axis=0) * oh).sum(-1) - 1
            keep = pos < CAP
            slot = jnp.where(keep, pos, CAP)
            x_rep = jnp.repeat(x, K, axis=0)
            buf = jnp.zeros((E, CAP, H), x.dtype).at[flat_e, slot].set(x_rep, mode='drop')
            h = jax.nn.silu(jnp.einsum('ech,ehf->ecf', buf, w1)) * jnp.einsum('ech,ehf->ecf', buf, w3)
            ob = jnp.einsum('ecf,efh->ech', h, w2)
            y = ob[flat_e, jnp.minimum(slot, CAP - 1)]
            y = jnp.where(keep[:, None], y, 0.0)
            return (y.reshape(n, K, H) * topk_w[:, :, None]).sum(1)
        key = jax.random.key(seed)
        ks = jax.random.split(key, 9)
        w = 0.02
        return {'hidden_states': jax.random.normal(ks[0], (B, S, H), jnp.float32), 'gate_w': jax.random.normal(ks[1], (E, H), jnp.float32) * w, 'gate_bias': jax.random.normal(ks[2], (E,), jnp.float32) * w, 'w1': jax.random.normal(ks[3], (E, H, F), jnp.float32) * w, 'w2': jax.random.normal(ks[4], (E, F, H), jnp.float32) * w, 'w3': jax.random.normal(ks[5], (E, H, F), jnp.float32) * w, 'shared_gate': jax.random.normal(ks[6], (H, FS), jnp.float32) * w, 'shared_up': jax.random.normal(ks[7], (H, FS), jnp.float32) * w, 'shared_down': jax.random.normal(ks[8], (FS, H), jnp.float32) * w}
    _L0_ffn_all = _L0_ffn_setup()
    _L0_ffn_in = {k: v for k, v in _L0_ffn_all.items() if k in ('gate_w', 'gate_bias', 'w1', 'w2', 'w3', 'shared_gate', 'shared_up', 'shared_down')}
    del _L0_ffn_all
    return {'x': x, 'ctx_512': ctx_512, 'L0_attn_Wq': _L0_attn_in['Wq'], 'L0_attn_Wkv': _L0_attn_in['Wkv'], 'L0_attn_Wo': _L0_attn_in['Wo'], 'L0_attn_bo': _L0_attn_in['bo'], 'L0_ffn_gate_w': _L0_ffn_in['gate_w'], 'L0_ffn_gate_bias': _L0_ffn_in['gate_bias'], 'L0_ffn_w1': _L0_ffn_in['w1'], 'L0_ffn_w2': _L0_ffn_in['w2'], 'L0_ffn_w3': _L0_ffn_in['w3'], 'L0_ffn_shared_gate': _L0_ffn_in['shared_gate'], 'L0_ffn_shared_up': _L0_ffn_in['shared_up'], 'L0_ffn_shared_down': _L0_ffn_in['shared_down']}

def reference(x, ctx_512, L0_attn_Wq, L0_attn_Wkv, L0_attn_Wo, L0_attn_bo, L0_ffn_gate_w, L0_ffn_gate_bias, L0_ffn_w1, L0_ffn_w2, L0_ffn_w3, L0_ffn_shared_gate, L0_ffn_shared_up, L0_ffn_shared_down):
    import jax
    import jax.numpy as jnp

    def _L0_attn_ref(x, Wq, Wkv, Wo, bo):
        import jax, jax.numpy as jnp
        import numpy as np
        DIM = 512
        N_HEADS = 16
        N_KV_HEADS = 4
        WINDOW = 128
        GLOBAL = 64

        def alibi_slopes(num_heads):
            closest_pow2 = 2.0 ** np.floor(np.log2(num_heads))
            base = 2.0 ** (-2.0 ** (-(np.log2(closest_pow2) - 3.0)))
            powers = np.arange(1, 1 + num_heads, dtype=np.float32)
            return jnp.asarray(base ** powers, dtype=jnp.float32)

        def window_allowed(seq_len):
            i = jnp.arange(seq_len)[:, None]
            j = jnp.arange(seq_len)[None, :]
            inside = (j >= i - WINDOW // 2) & (j <= i + WINDOW // 2)
            glob = (i < GLOBAL) | (j < GLOBAL)
            return inside | glob
        B, S, D = x.shape
        H, KVH = (N_HEADS, N_KV_HEADS)
        hd = D // H
        r = H // KVH
        cw = jax.nn.sigmoid(jnp.sum(jnp.abs(x), axis=-1, keepdims=True))
        q = jnp.dot(x * cw, Wq)
        kv = jnp.dot(x, Wkv)
        k, v = jnp.split(kv, 2, axis=-1)
        q = q.reshape(B, S, H, hd).transpose(0, 2, 1, 3)
        k = k.reshape(B, S, KVH, hd).transpose(0, 2, 1, 3)
        v = v.reshape(B, S, KVH, hd).transpose(0, 2, 1, 3)
        k = jnp.repeat(k, r, axis=1)
        v = jnp.repeat(v, r, axis=1)
        scale = 1.0 / jnp.sqrt(jnp.float32(hd))
        qk = jnp.einsum('bhid,bhjd->bhij', q, k) * scale
        pos = jnp.arange(S)
        dist = -jnp.abs(pos[:, None] - pos[None, :]).astype(jnp.float32)
        qk = qk + alibi_slopes(H)[None, :, None, None] * dist[None, None, :, :]
        allowed = window_allowed(S)
        qk = jnp.where(allowed[None, None, :, :], -1000000000.0, qk)
        attn = jax.nn.softmax(qk, axis=-1)
        out = jnp.einsum('bhij,bhjd->bhid', attn, v)
        out = out.transpose(0, 2, 1, 3).reshape(B, S, D)
        return jnp.dot(out, Wo) + bo

    def _L0_xattn_ref(q, k, v):
        import jax, jax.numpy as jnp
        import numpy as np
        import math
        NUM_Q_HEADS = 32
        NUM_KV_HEADS = 8
        B, S, E = q.shape
        H, KV = (NUM_Q_HEADS, NUM_KV_HEADS)
        D = E // H
        G = H // KV
        scale = math.sqrt(D)
        qh = q.reshape(B, S, KV, G, D).transpose(0, 2, 3, 1, 4)
        kh = k.reshape(B, S, KV, D).transpose(0, 2, 1, 3)
        vh = v.reshape(B, S, KV, D).transpose(0, 2, 1, 3)
        scores = jnp.einsum('bkgsd,bktd->bkgst', qh, kh) / scale
        weights = jax.nn.softmax(scores, axis=-1)
        out = jnp.einsum('bkgst,bktd->bkgsd', weights, vh)
        return out.transpose(0, 3, 1, 2, 4).reshape(B, S, E)

    def _L0_ffn_ref(hidden_states, gate_w, gate_bias, w1, w2, w3, shared_gate, shared_up, shared_down):
        import jax, jax.numpy as jnp
        import numpy as np
        E = 32
        K = 4
        G = 4
        TG = 2
        H = 512
        F = 256
        FS = 512
        SCALE = 2.0
        B, S = (2, 256)
        N = B * S
        CAP = 2 * (N * K // E)

        def _gate(x, gate_w, gate_bias):
            logits = x @ gate_w.T
            scores = jax.nn.sigmoid(logits)
            sc = scores + gate_bias
            n = x.shape[0]
            grp = sc.reshape(n, G, E // G)
            group_scores = jax.lax.top_k(grp, 2)[0].sum(-1)
            _, gidx = jax.lax.top_k(group_scores, TG)
            gmask = jnp.zeros((n, G), sc.dtype).at[jnp.arange(n)[:, None], gidx].set(1.0)
            smask = jnp.repeat(gmask, E // G, axis=1)
            tmp = jnp.where(smask > 0, sc, 0.0)
            _, topk_idx = jax.lax.top_k(tmp, K)
            topk_w = jnp.take_along_axis(scores, topk_idx, axis=1)
            topk_w = topk_w / (topk_w.sum(-1, keepdims=True) + 1e-20)
            return (topk_idx, topk_w * SCALE)

        def _moe(x, topk_idx, topk_w, w1, w2, w3):
            n = x.shape[0]
            flat_e = topk_idx.reshape(-1)
            oh = jax.nn.one_hot(flat_e, E, dtype=jnp.int32)
            pos = (jnp.cumsum(oh, axis=0) * oh).sum(-1) - 1
            keep = pos < CAP
            slot = jnp.where(keep, pos, CAP)
            x_rep = jnp.repeat(x, K, axis=0)
            buf = jnp.zeros((E, CAP, H), x.dtype).at[flat_e, slot].set(x_rep, mode='drop')
            h = jax.nn.silu(jnp.einsum('ech,ehf->ecf', buf, w1)) * jnp.einsum('ech,ehf->ecf', buf, w3)
            ob = jnp.einsum('ecf,efh->ech', h, w2)
            y = ob[flat_e, jnp.minimum(slot, CAP - 1)]
            y = jnp.where(keep[:, None], y, 0.0)
            return (y.reshape(n, K, H) * topk_w[:, :, None]).sum(1)
        b, s, h = hidden_states.shape
        x = hidden_states.reshape(-1, h)
        topk_idx, topk_w = _gate(x, gate_w, gate_bias)
        out = _moe(x, topk_idx, topk_w, w1, w2, w3)
        shared = jax.nn.silu(x @ shared_gate) * (x @ shared_up) @ shared_down
        return (out + shared).reshape(b, s, h)
    x = x + _L0_attn_ref(_layernorm(x, axis=-1), L0_attn_Wq, L0_attn_Wkv, L0_attn_Wo, L0_attn_bo)
    x = x + _L0_xattn_ref(_layernorm(x, axis=-1), ctx_512, ctx_512)
    x = x + _L0_ffn_ref(_layernorm(x, axis=-1), L0_ffn_gate_w, L0_ffn_gate_bias, L0_ffn_w1, L0_ffn_w2, L0_ffn_w3, L0_ffn_shared_gate, L0_ffn_shared_up, L0_ffn_shared_down)
    return x

_drawn_inputs = setup_inputs


def setup_inputs(seed=0):
    import zlib

    import numpy as np

    out = dict(_drawn_inputs(seed))
    spreads = {'L0_attn_bo': (0.0, 0.1)}
    factors = {'L0_attn_Wq': 7.25,
     'L0_ffn_gate_w': 3.149,
     'L0_ffn_gate_bias': 5.347,
     'L0_ffn_w1': 3.076,
     'L0_ffn_w2': 3.01,
     'L0_ffn_w3': 3.004}
    for name, (base, spread) in spreads.items():
        noise = np.random.default_rng([zlib.crc32(name.encode()), seed]).standard_normal(out[name].shape)
        drawn = base * np.exp(spread * noise) if base else spread * noise
        out[name] = jnp.asarray(drawn.astype(out[name].dtype))
    for name, factor in factors.items():
        out[name] = (out[name] * factor).astype(out[name].dtype)
    return out
```

```python
import numpy as np
import concourse.bass as bass
from concourse import mybir
from contextlib import ExitStack

F32 = mybir.dt.float32
F32R = mybir.dt.float32r
BF16 = mybir.dt.bfloat16
U32 = mybir.dt.uint32
ALU = mybir.AluOpType
ACT = mybir.ActivationFunctionType
AX = mybir.AxisListType

P = 128
B, S, D = 8, 256, 512
N = B * S
NT = N // P
DC = D // P
H, KVH, HD = 16, 4, 32
REP = H // KVH
GLOB, HALF = 64, 64
SQ = S - GLOB
XH, XKV, XD = 32, 8, 16
XREP = XH // XKV
NE, TOPK, F, CAP = 32, 4, 256, 128
GRP = 4
EPG = NE // GRP
EPS = 1e-5
NEG = -1e30
SPLIT_ROWS = 3 * HD
ALIBI_ROWS = 4
SHIFT_ROWS = 2
XSPLIT_ROWS = 6 * XD
EU = 4
NB = 512
ABSENT = 65535
TANH_HALF = 0.5


def _round_bits(a, bits):
    a = np.asarray(a, np.float64)
    m, e = np.frexp(a)
    return np.ldexp(np.rint(m * 2.0 ** bits) / 2.0 ** bits, e).astype(np.float32)


def constants():
    p = np.arange(P)
    upper = np.where(p[None, :] > p[:, None], 0.0, NEG).astype(np.float32)
    masks = np.stack([np.tile(upper, (1, 4)), np.tile(upper.T, (1, 4))], 1)
    tri = (p[:, None] < p[None, :]).astype(np.float32)
    mats = np.concatenate([np.eye(P, dtype=np.float32), tri], 1)
    slope = ((2.0 ** -0.5) ** np.arange(1, H + 1)).astype(np.float32)
    i = np.arange(GLOB, S).astype(np.float32)
    lift = slope[:, None] * i[None, :]
    s_hi = _round_bits(slope, 12)
    l_hi = _round_bits(lift, 12)
    wide = np.ones((1, SQ), np.float32)
    q_rows = np.stack([-s_hi[:, None] * wide, -(slope - s_hi)[:, None] * wide, l_hi, lift - l_hi])
    k_rows = np.ones((SHIFT_ROWS + ALIBI_ROWS, 2, KVH, P), np.float32)
    far, near = np.arange(P, S), np.arange(GLOB, GLOB + P)
    k_rows[0:2, 0] = far
    k_rows[0:2, 1] = -near.astype(np.float32)
    k_rows[2:4, 1] = -1.0
    first = (np.arange(GRP)[None, :] < np.arange(GRP)[:, None]).astype(np.float32).reshape(-1)
    iota = np.tile(np.arange(NE, dtype=np.float32), (P, 1))
    small = np.concatenate([np.tile(first, (P, 1)), iota], 1)
    token = (np.arange(NT)[None, :] * P + p[:, None]).astype(np.uint32)
    slots = np.zeros((NE * CAP, 2), np.uint32)
    slots[:, 0] = ABSENT
    return {"c_masks": masks, "c_mats": mats, "c_qrows": q_rows.astype(np.float32), "c_krows": k_rows,
            "c_small": small, "c_token": token, "c_slots": slots}


def build(nc, x, ctx, wq, wkv, wo, bo, gw, gb, w1, w2, w3, sg, su, sd,
          c_masks, c_mats, c_qrows, c_krows, c_small, c_token, c_slots, out):
    st = ExitStack()

    def sb(name, shape, dt=F32):
        return st.enter_context(nc.sbuf_tensor(name, shape, dt))

    def ps(name, cols):
        return st.enter_context(nc.psum_tensor(name, [P, cols], F32))

    def sem(name):
        return st.enter_context(nc.semaphore(name))

    def dram(name, shape, dt=F32):
        return nc.dram_tensor(name, shape, dt, kind="Internal").ap()

    with st:
        kd = dram("kd", [2, P, S])
        qd = dram("qd", [2, D, SQ])
        kxd = dram("kxd", [3, P, S], BF16)
        qxd = dram("qxd", [3, D, S], BF16)
        xnd = dram("xnd", [N, D])
        slot_table = dram("slot_table", [NE * CAP, 2], U32)

        res = sb("res", [P, NT * D])
        xt3 = sb("xt3", [P, DC, N])
        gw_s = sb("gw_s", [P, DC, NE])
        ident = sb("ident", [P, P])
        identb = sb("identb", [P, P], BF16)
        trib = sb("trib", [P, P], BF16)
        onesb = sb("onesb", [P, P], BF16)
        ones = sb("ones", [P, P])
        masks = sb("masks", [P, 2, 4 * P], BF16)
        small = sb("small", [P, GRP * GRP + NE])
        first = small[:, 0:GRP * GRP].rearrange("p (a b) -> p a b", a=GRP)
        iota = small[:, GRP * GRP:]
        token = sb("token", [P, NT], U32)
        gb_s = sb("gb_s", [P, NE])
        bo_s = sb("bo_s", [P, D])
        qs = sb("qs", [P, H, SQ], F32R)
        ks = sb("ks", [P, 2, KVH, P], F32R)
        mall = sb("mall", [P, NT * NE], BF16)
        idall = sb("idall", [P, NT * TOPK])
        scall = sb("scall", [P, NT * TOPK])

        ARENA = 27 * 1024
        arena = sb("arena", [P, ARENA])
        top = [0]

        def place(cols, shape=None, dt=F32):
            a = arena[:, top[0]:top[0] + cols]
            top[0] += cols
            assert top[0] <= ARENA, top[0]
            if dt is not F32:
                a = a.bitcast(dt)
            return a

        wq_s = place(DC * D).rearrange("p (c n) -> p c n", c=DC)
        wkv_s = place(DC * 2 * P).rearrange("p (c n) -> p c n", c=DC)
        wo_s = place(DC * D).rearrange("p (c n) -> p c n", c=DC)
        xn = place(2 * D)
        xt = place(DC * S).rearrange("p (c n) -> p c n", c=DC)
        ctx_s = place(2 * P)
        cwb = place(S)
        dg = place(2 * P)
        kh, kl = place(S, dt=F32R), place(S, dt=F32R)
        vs = place(3 * P).rearrange("p (s n) -> p s n", s=3)
        at = place(DC * S).rearrange("p (c n) -> p c n", c=DC)
        ox_at = top[0]
        qf = place(DC * SQ).rearrange("p (c n) -> p c n", c=DC)
        qh = place(DC * SQ, dt=F32R).rearrange("p (c n) -> p c n", c=DC)
        ql = place(DC * SQ, dt=F32R).rearrange("p (c n) -> p c n", c=DC)
        ox = arena[:, ox_at:ox_at + XKV * S]
        xr = place(DC * S)
        xp = [place(DC * S // 2, dt=BF16) for _ in range(3)]
        kr = place(S)
        kp = [place(S // 2, dt=BF16) for _ in range(3)]
        qxs = place(XH * S // 2, dt=BF16).rearrange("p (h n) -> p h n", h=XH)
        kxs = place(XKV * S // 2, dt=BF16).rearrange("p (h n) -> p h n", h=XKV)
        vx = place(2 * XKV * 2 * XD).rearrange("p (t h c) -> p t h c", t=2, h=XKV)
        ex_at = top[0]
        ex = [place(1024) for _ in range(3)]
        e4 = [arena[:, ex_at + 512 * n:ex_at + 512 * n + 512] for n in range(4)]
        tmp = place(D)
        attention_top = top[0]
        nxh, nxl = sb("nxh", [XH, S], BF16), sb("nxl", [XH, S], BF16)
        nmx = sb("nmx", [H, SQ])
        nmh, nml = sb("nmh", [H, SQ], F32R), sb("nml", [H, SQ], F32R)
        junk = tmp
        bnst = sb("bnst", [P, 2, 6])
        mv = sb("mv", [P, 2, 2])
        rstd = sb("rstd", [P, 2])
        power = sb("power", [P, 2])
        asum = sb("asum", [P, 2])
        mx = sb("mx", [P, 2 * H])
        mxx = sb("mxx", [P, 2 * XH])
        rd = sb("rd", [P, SQ])
        rx = sb("rx", [P, XH])
        gl = sb("gl", [NE, S])
        sc = sb("sc", [P, 2, NE])
        scb = sb("scb", [P, 2, NE])
        m8 = sb("m8", [P, 2, GRP, 8])
        gs = sb("gs", [P, 2, GRP])
        gt = sb("gt", [P, 2, GRP, GRP])
        eq = sb("eq", [P, 2, GRP, GRP])
        sel = sb("sel", [P, 2, GRP])
        v8 = sb("v8", [P, 2, 8])
        i8 = sb("i8", [P, 2, 8], U32)
        idf = sb("idf", [P, 2, TOPK])
        oh = sb("oh", [P, 2, TOPK, NE])
        ohs = sb("ohs", [P, 2, TOPK, NE])

        sd_s = arena[:, ARENA - DC * D:].rearrange("p (c n) -> p c n", c=DC)
        assert attention_top <= ARENA - DC * D
        top[0] = 0
        sg_s = place(DC * D).rearrange("p (c n) -> p c n", c=DC)
        su_s = place(DC * D).rearrange("p (c n) -> p c n", c=DC)
        top[0] = ring_at = 6 * 1024
        h13 = [place(DC * 2 * F).rearrange("p (c n) -> p c n", c=DC) for _ in range(EU)]
        h2 = [place(2 * D).rearrange("p (c n) -> p c n", c=2) for _ in range(EU)]
        ht_sh = place(DC * NB).rearrange("p (c n) -> p c n", c=DC)
        th_sh, ga_sh = place(NB), place(NB)
        top[0] -= DC * NB + 2 * NB
        xgt = [place(D).rearrange("p (c n) -> p c n", c=DC) for r in range(2)]
        th_e = [place(F) for r in range(2)]
        he = [place(F) for r in range(2)]
        hte = [place(2 * P).rearrange("p (c n) -> p c n", c=2) for r in range(2)]
        ye = [place(D) for r in range(2)]
        assert top[0] <= attention_top
        top[0] = ring_at
        big_oh = place(NT * TOPK * NE).rearrange("p (t k e) -> p t k e", t=NT, k=TOPK)
        big_pr = place(NT * TOPK * NE).rearrange("p (t k e) -> p t k e", t=NT, k=TOPK)
        cum = [place(NT * NE) for _ in range(2)]
        pos = place(NT * NE)
        posk, drop, slot, tot, wgt = (place(NT * TOPK) for _ in range(5))
        slot_u = place(NT * TOPK, dt=U32)
        top[0] = attention_top
        xg = [place(D) for _ in range(2)]
        assert top[0] <= ARENA - DC * D
        iw = [sb(f"iw{r}", [P, 2], U32) for r in range(EU)]
        si = sb("si", [P, TOPK], U32)
        sdat = sb("sdat", [P, TOPK, 2], U32)

        pt, pa, pb, po = ps("pt", 1024), ps("pa", 1024), ps("pb", 1024), ps("po", 1024)
        quad = [pa[:, 0:512], pa[:, 512:1024], pb[:, 0:512], pb[:, 512:1024]]
        duo = [pa, pb]
        pv = [po[:, 0:512], po[:, 512:1024]]

        names = """const_in const_moved const_ready clear x_in w_in ffn_in ctx_in
            ln_stats ln_rstd xn1 abs_sum diag x_t xt_ready cw_t cwb_ready k_t k_split v_t v_ready q_t q_split
            bo_added kd_out ks_in qd_out qs_in s_unit s_max m_t m_rows shift_in st_unit e_ready pv_done at_ready
            wo_done x1 xn2 c_t c_hi c_rem c_mid c_split vx_ready kxd_out kxs_in n_t n_hi n_rem n_mid n_split
            qxd_out qxs_in xs_unit x_max xm_t x_rows xshift_in xst_unit xe_ready xpv_done ox_ready xo_t x2 xn3
            xnd_out t3_t xt3_ready g_mm gl_ready g_t th_ready sc_read route dve
            m_count pos_ready slot_ready init_out si_ready sc_out table_ready
            sh_gu sh_th sh_h sh_down res_final base_out
            xe_t xe_tr up_done th_done h_done ht_t ht_ready down_done y_ready""".split()
        s = {n: sem(n) for n in names}
        iw_in = [sem(f"iw_in{r}") for r in range(EU)]
        wg_in = [sem(f"wg_in{r}") for r in range(EU)]
        xg_in = [sem(f"xg_in{r}") for r in range(2)]
        y_out = sem("y_out")
        block = st.enter_context(nc.Block())

        def tile(b, t, n=1):
            return res[:, bass.ds(b * (2 * D) + t * D, n * D)]

        def peeled(engine, count):
            def run(body):
                body(0)
                with engine.Fori(1, count) as i:
                    body(i)
            return run

        wait_register = {}

        def hold(engine, semaphore, count):
            if isinstance(count, int):
                engine.wait_ge(semaphore, count)
                return
            if engine.engine not in wait_register:
                wait_register[engine.engine] = engine.alloc_register("wait_count")
            engine.reg_mov(wait_register[engine.engine], count)
            engine.wait_ge(s["const_ready"], 1)
            engine.wait_ge(semaphore, wait_register[engine.engine])

        @block.sync
        def _(sp):
            def go(dst, src, signal):
                sp.dma_start(dst, src).then_inc(s[signal], 16)

            go(res[:, :].rearrange("p (t d) -> p t d", t=NT), x.rearrange("b (u p) d -> p (b u) d", p=P), "x_in")
            go(xn[:, 0:2 * P], c_mats, "const_in")
            go(xr[:, 0:1024].rearrange("p (a n) -> p a n", a=2), c_masks, "const_in")
            go(small[:], c_small, "const_in")
            go(token[:], c_token, "const_in")
            go(gb_s[:], gb.rearrange("(o n) -> o n", o=1).broadcast_to([P, NE]), "const_in")
            go(bo_s[:], bo.rearrange("(o n) -> o n", o=1).broadcast_to([P, D]), "const_in")
            go(arena[96:102, ex_at:ex_at + 2 * KVH * P].rearrange("p (a h n) -> p a h n", a=2, h=KVH), c_krows,
               "const_in")
            go(arena[96:100, 0:H * SQ].rearrange("p (h n) -> p h n", h=H), c_qrows, "const_in")
            sp.wait_ge(s["const_moved"], 1)
            for dst, src in ((wq_s, wq), (wkv_s, wkv), (wo_s, wo), (gw_s[:], gw)):
                go(dst, src.rearrange("(c p) n -> p c n", p=P), "w_in")
            go(sd_s, sd.rearrange("(c p) n -> p c n", p=P), "ffn_in")
            go(slot_table, c_slots, "init_out")

            @peeled(sp, B)
            def _(b):
                hold(sp, s["c_split"], b)
                hold(sp, s["vx_ready"], b)
                go(ctx_s.rearrange("p (t n) -> p t n", t=2),
                   ctx[bass.ds(b, 1)].rearrange("o (t p) n -> p (o t) n", p=P), "ctx_in")
                hold(sp, s["k_split"], b + 1)
                go(kd[0], kh.bitcast(F32), "kd_out")
                go(kd[1], kl.bitcast(F32), "kd_out")
                hold(sp, s["kd_out"], b * 32 + 32)
                for n, part in enumerate((0, 1, 0)):
                    for blk, j0 in enumerate((P, GLOB)):
                        go(ks[n * HD:n * HD + HD, blk].bitcast(F32),
                           kd[part].rearrange("(g d) t -> d g t", d=HD)[:, :, j0:j0 + P], "ks_in")
                hold(sp, s["q_split"], b + 1)
                go(qd[0].rearrange("(c p) t -> p c t", p=P), qh.bitcast(F32), "qd_out")
                go(qd[1].rearrange("(c p) t -> p c t", p=P), ql.bitcast(F32), "qd_out")
                hold(sp, s["qd_out"], b * 32 + 32)
                for n, part in enumerate((0, 0, 1)):
                    go(qs[n * HD:n * HD + HD].bitcast(F32), qd[part].rearrange("(h d) t -> d h t", d=HD), "qs_in")
                hold(sp, s["c_split"], b + 1)
                for n in range(3):
                    go(kxd[n], kp[n], "kxd_out")
                hold(sp, s["kxd_out"], b * 48 + 48)
                for n, part in enumerate((0, 1, 0, 1, 2, 0)):
                    go(kxs[n * XD:n * XD + XD], kxd[part].rearrange("(g d) t -> d g t", d=XD), "kxs_in")
                hold(sp, s["m_rows"], b + 1)
                go(qs[100:101].bitcast(F32), nmh[:].bitcast(F32), "shift_in")
                go(qs[101:102].bitcast(F32), nml[:].bitcast(F32), "shift_in")
                hold(sp, s["n_split"], b + 1)
                for n in range(3):
                    go(qxd[n].rearrange("(c p) t -> p c t", p=P), xp[n].rearrange("p (c t) -> p c t", c=DC),
                       "qxd_out")
                hold(sp, s["qxd_out"], b * 48 + 48)
                for n, part in enumerate((0, 0, 1, 1, 0, 2)):
                    go(qxs[n * XD:n * XD + XD], qxd[part].rearrange("(h d) t -> d h t", d=XD), "qxs_in")
                hold(sp, s["x_rows"], b + 1)
                go(qxs[96:97], nxh[:], "xshift_in")
                go(qxs[97:98], nxl[:], "xshift_in")
                hold(sp, s["xn3"], b + 1)
                go(xnd[bass.ds(b * S, S)].rearrange("(t p) d -> p t d", p=P), xn.rearrange("p (t d) -> p t d", t=2),
                   "xnd_out")

            sp.wait_ge(s["wo_done"], B)
            for dst, src in ((sg_s, sg), (su_s, su)):
                go(dst, src.rearrange("(c p) n -> p c n", p=P), "ffn_in")

            @peeled(sp, N // NB)
            def _(n):
                hold(sp, s["res_final"], n * 4 + 4)
                go(out.rearrange("b (u p) d -> p (b u) d", p=P)[:, bass.ds(n * 4, 4)],
                   res[:, bass.ds(n * 4 * D, 4 * D)].rearrange("p (t d) -> p t d", t=4), "base_out")
            sp.wait_ge(s["sc_out"], NT * TOPK * 16)
            @peeled(sp, NE // EU)
            def _(i):
                for r in range(EU):
                    hold(sp, s["down_done"], i * EU)
                    e = i * EU + r
                    sp.dma_start(iw[r][:], slot_table[bass.ds(e * CAP, CAP)]).then_inc(iw_in[r], 16)
                    w13 = h13[r].rearrange("p c (a f) -> p c a f", a=2)
                    sp.dma_start(w13[:, :, 0], w1[bass.ds(e, 1)].rearrange("o (p c) f -> p (o c) f", c=DC)
                                 ).then_inc(wg_in[r], 16)
                    sp.dma_start(w13[:, :, 1], w3[bass.ds(e, 1)].rearrange("o (p c) f -> p (o c) f", c=DC)
                                 ).then_inc(wg_in[r], 16)
                    sp.dma_start(h2[r], w2[bass.ds(e, 1)].rearrange("o (p c) d -> p (o c) d", c=2)
                                 ).then_inc(wg_in[r], 16)
                hold(sp, y_out, i * (EU * 16) + EU * 16)
            sp.wait_ge(s["base_out"], N // NB * 16)
            sp.wait_ge(s["xnd_out"], B * 16)

        @block.gpsimd
        def _(pool):
            def norm_scale(count):
                pool.wait_ge(s["ln_stats"], count)
                nc.gpsimd.tensor_tensor(rstd[:], mv[:, :, 1], power[:], ALU.pow).then_inc(s["ln_rstd"], 1)

            pool.wait_ge(s["x_in"], 16)
            nc.gpsimd.memset(ones[:], 1.0)
            nc.gpsimd.memset(onesb[:], 1.0)
            nc.gpsimd.memset(vx, 1.0)
            for r in range(2):
                op = nc.gpsimd.memset(xg[r], 0.0)
            op.then_inc(s["clear"], 1)
            pool.wait_ge(s["clear"], 1)
            nc.gpsimd.memset(kxs[96:98], 1.0).then_inc(s["clear"], 1)
            pool.wait_ge(s["clear"], 2)
            pool.wait_ge(s["const_moved"], 1)
            nc.gpsimd.memset(power[:], -0.5).then_inc(s["const_ready"], 1)
            @peeled(pool, B)
            def _(b):
                norm_scale(b * 3 + 1)
                pool.wait_ge(s["xn1"], b + 1)
                for t in range(2):
                    op = nc.gpsimd.tensor_tensor(tile(b, t), tile(b, t), bo_s[:], ALU.add)
                op.then_inc(s["bo_added"], 1)
                norm_scale(b * 3 + 2)
                norm_scale(b * 3 + 3)

            pool.wait_ge(s["slot_ready"], 1)
            pool.wait_ge(s["init_out"], 16)
            @peeled(pool, NT)
            def _(t):
                pool.wait_ge(s["sc_out"], t * (TOPK * 16))
                nc.gpsimd.tensor_copy(si[:], slot_u[:, bass.ds(t * TOPK, TOPK)])
                nc.gpsimd.tensor_copy(sdat[:, :, 0], token[:, bass.ds(t, 1)].broadcast_to([P, TOPK]))
                nc.gpsimd.tensor_copy(sdat[:, :, 1].bitcast(F32), wgt[:, bass.ds(t * TOPK, TOPK)]
                                      ).then_inc(s["si_ready"], 1)
                hold(pool, s["si_ready"], t + 1)
                for k in range(TOPK):
                    nc.gpsimd.indirect_dma_start(
                        slot_table, bass.IndirectOffsetOnAxis(ap=si[:, k:k + 1], axis=0), sdat[:, k, :], None,
                        bounds_check=NE * CAP - 1, oob_is_err=False).then_inc(s["sc_out"], 16)

            pool.wait_ge(s["base_out"], N // NB * 16)
            pool.wait_ge(s["xnd_out"], B * 16)

            flat = out.rearrange("b s d -> (b s) d")

            def gather(i, r):
                hold(pool, iw_in[r], i * 16 + 16)
                if r < 2:
                    hold(pool, s["xe_t"], i * EU)
                else:
                    hold(pool, s["xe_t"], i * EU + r - 1)
                nc.gpsimd.indirect_dma_start(xg[r % 2], None, xnd, bass.IndirectOffsetOnAxis(ap=iw[r][:, 0:1], axis=0),
                                             bounds_check=N - 1, oob_is_err=False).then_inc(xg_in[r % 2], 16)

            @peeled(pool, NE // EU)
            def _(i):
                gather(i, 0)
                gather(i, 1)
                for r in range(EU):
                    if r + 2 < EU:
                        gather(i, r + 2)
                    hold(pool, s["y_ready"], i * EU + r + 1)
                    hold(pool, y_out, i * (EU * 16) + r * 16)
                    nc.gpsimd.indirect_dma_start(flat, bass.IndirectOffsetOnAxis(ap=iw[r][:, 0:1], axis=0), ye[r % 2],
                                                 None, bounds_check=N - 1, oob_is_err=False,
                                                 compute_op=ALU.add).then_inc(y_out, 16)
                hold(pool, y_out, i * (EU * 16) + EU * 16)

        @block.scalar
        def _(act):
            def copy(dst, src, signal, func=ACT.Copy, **kw):
                nc.scalar.activation(dst, src, func, **kw).then_inc(s[signal], 1)

            act.wait_ge(s["const_in"], 8 * 16)
            nc.scalar.activation(ident[:], xn[:, 0:P], ACT.Copy)
            nc.scalar.activation(identb[:], xn[:, 0:P], ACT.Copy)
            nc.scalar.activation(trib[:], xn[:, P:2 * P], ACT.Copy)
            nc.scalar.activation(masks[:], xr[:, 0:1024].rearrange("p (a n) -> p a n", a=2), ACT.Copy)
            nc.scalar.activation(ks[96:102], arena[96:102, ex_at:ex_at + 2 * KVH * P].rearrange(
                "p (a h n) -> p a h n", a=2, h=KVH), ACT.Copy)
            nc.scalar.activation(qs[96:100], arena[96:100, 0:H * SQ].rearrange("p (h n) -> p h n", h=H), ACT.Copy
                                 ).then_inc(s["const_moved"], 1)

            @peeled(act, B)
            def _(b):
                act.wait_ge(s["xn1"], b + 1)
                for t in range(2):
                    copy(junk, xn[:, t * D:t * D + D], "abs_sum", ACT.Abs, accum_out=asum[:, t:t + 1])
                    act.wait_ge(s["abs_sum"], b * 3 + t + 1)
                copy(asum[:], asum[:], "abs_sum", ACT.Exp, scale=-1.0)
                act.wait_ge(s["x_t"], b + 1)
                copy(xt, pt[:].rearrange("p (c n) -> p c n", c=DC), "xt_ready")
                act.wait_ge(s["cw_t"], b + 1)
                copy(cwb, pv[0][:, 0:S], "cwb_ready", scale=float(HD) ** -0.5)
                act.wait_ge(s["v_t"], b + 1)
                copy(vs, pb[:, 0:3 * P].rearrange("p (s n) -> p s n", s=3), "v_ready")
                act.wait_ge(s["ctx_in"], b * 16 + 16)
                copy(vx[:, :, :, 0:XD], ctx_s.rearrange("p (t h c) -> p t h c", t=2, h=XKV), "vx_ready")
                act.wait_ge(s["c_t"], b + 1)
                copy(kp[0], pv[1][:, 0:S], "c_hi")
                act.wait_ge(s["c_rem"], b + 1)
                copy(kp[1], kr, "c_mid")
                for u in range(8):
                    act.wait_ge(s["st_unit"], b * 8 + u + 1)
                    if u >= 4:
                        act.wait_ge(s["pv_done"], b * 4 + (u - 4) // 2 + 1)
                    copy(e4[u % 4], quad[u % 4], "e_ready", ACT.Exp)
                act.wait_ge(s["n_t"], b + 1)
                copy(xp[0], pt[:], "n_hi")
                act.wait_ge(s["n_rem"], b + 1)
                copy(xp[1], xr, "n_mid")
                for u in range(16):
                    act.wait_ge(s["xst_unit"], b * 16 + u + 1)
                    if u >= 3:
                        act.wait_ge(s["xpv_done"], b * 16 + u - 2)
                    copy(ex[u % 3], duo[u % 2][:], "xe_ready", ACT.Exp, scale=float(XD) ** -0.5)
                    if u % 4 == 1 and u > 4:
                        pair = u // 4 - 1
                        act.wait_ge(s["xpv_done"], b * 16 + pair * 4 + 4)
                        copy(ox[:, pair * 512:pair * 512 + 512], pv[pair % 2], "ox_ready")
                act.wait_ge(s["xpv_done"], b * 16 + 16)
                copy(ox[:, 3 * 512:4 * 512], pv[1], "ox_ready")
                act.wait_ge(s["t3_t"], b + 1)
                copy(xt3[:, :, bass.ds(b * S, S)], pt[:].rearrange("p (c n) -> p c n", c=DC), "xt3_ready")
                act.wait_ge(s["g_mm"], b + 1)
                copy(gl[:], pv[0][0:NE, 0:S], "gl_ready")
                act.wait_ge(s["g_t"], b + 1)
                act.wait_ge(s["sc_read"], b)
                copy(sc[:], pv[1][:, 0:2 * NE].rearrange("p (t e) -> p t e", t=2), "th_ready", ACT.Tanh, scale=0.5)

            @peeled(act, N // NB)
            def _(n):
                for m in range(DC):
                    act.wait_ge(s["sh_gu"], n * DC + m + 1)
                    act.wait_ge(s["sh_h"], n * DC + m)
                    copy(th_sh, duo[m % 2][:, 0:NB], "sh_th", ACT.Tanh, scale=0.5)

            @peeled(act, NE // EU)
            def _(i):
                for r in range(EU + 1):
                    if r < EU:
                        act.wait_ge(s["xe_t"], i * EU + r + 1)
                        if r >= 2:
                            act.wait_ge(s["up_done"], i * EU + r - 1)
                        copy(xgt[r % 2], pt[:, r % 2 * 512:r % 2 * 512 + 512].rearrange("p (c n) -> p c n", c=DC),
                             "xe_tr")
                    if r > 0:
                        q = r - 1
                        act.wait_ge(s["up_done"], i * EU + q + 1)
                        if q >= 2:
                            act.wait_ge(s["h_done"], i * EU + q - 1)
                        copy(th_e[q % 2], quad[q % 2][:, 0:F], "th_done", ACT.Tanh, scale=0.5)
                        act.wait_ge(s["ht_t"], i * EU + q + 1)
                        if q >= 2:
                            act.wait_ge(s["down_done"], i * EU + q - 1)
                        copy(hte[q % 2], pv[q % 2][:, 0:2 * P].rearrange("p (c n) -> p c n", c=2), "ht_ready")

        @block.vector
        def _(dve):
            v = nc.vector
            chain = {"base": 0, "n": 0}

            def link(ins):
                chain["n"] += 1
                ins.then_inc(s["dve"], 1)
                hold(dve, s["dve"], chain["base"] + chain["n"])

            def norm(b, count, signal):
                for t in range(2):
                    link(v.bn_stats(bnst[:, t, :], tile(b, t)))
                for t in range(2):
                    op = v.bn_aggr(mv[:, t, :], bnst[:, t, :])
                link(op)
                v.tensor_scalar(mv[:, :, 1], mv[:, :, 1], EPS, None, ALU.add).then_inc(s["ln_stats"], 1)
                dve.wait_ge(s["ln_rstd"], count)
                dve.wait_ge(s["ln_stats"], count)
                for t in range(2):
                    op = v.tensor_scalar(xn[:, t * D:t * D + D], tile(b, t), mv[:, t, 0:1], rstd[:, t:t + 1],
                                         ALU.subtract, ALU.mult)
                op.then_inc(s[signal], 1)

            dve.wait_ge(s["x_in"], 16)
            dve.wait_ge(s["const_ready"], 1)
            STEPS = 48
            @peeled(dve, B)
            def _(b):
                chain["base"], chain["n"] = b * STEPS, 0
                hold(dve, s["t3_t"], b)
                hold(dve, s["xnd_out"], b * 16)
                norm(b, b * 3 + 1, "xn1")
                dve.wait_ge(s["abs_sum"], b * 3 + 3)
                link(v.tensor_scalar(asum[:], asum[:], 1.0, None, ALU.add))
                link(v.reciprocal(asum[:], asum[:]))
                for t in range(2):
                    op = v.tensor_scalar(dg[:, t * P:t * P + P], ident[:], asum[:, t:t + 1], None, ALU.mult)
                op.then_inc(s["diag"], 1)
                dve.wait_ge(s["k_t"], b + 1)
                dve.wait_ge(s["kd_out"], b * 32)
                link(v.tensor_copy(kh, pv[0][:, S:2 * S]))
                v.tensor_tensor(kl, pv[0][:, S:2 * S], kh.bitcast(F32), ALU.subtract).then_inc(s["k_split"], 1)
                dve.wait_ge(s["q_t"], b + 1)
                dve.wait_ge(s["cwb_ready"], b + 1)
                dve.wait_ge(s["xo_t"], b * 2)
                link(v.tensor_tensor(qf, pa[:].rearrange("p (c n) -> p c n", c=DC)[:, :, 0:SQ],
                                     cwb[:, GLOB:S].unsqueeze(1).broadcast_to([P, DC, SQ]), ALU.mult))
                link(v.tensor_copy(qh, qf))
                v.tensor_tensor(ql, qf, qh.bitcast(F32), ALU.subtract).then_inc(s["q_split"], 1)
                dve.wait_ge(s["c_hi"], b + 1)
                v.tensor_tensor(kr, pv[1][:, 0:S], kp[0], ALU.subtract).then_inc(s["c_rem"], 1)
                dve.wait_ge(s["c_mid"], b + 1)
                dve.wait_ge(s["c_rem"], b + 1)
                v.tensor_tensor(kp[2], kr, kp[1], ALU.subtract).then_inc(s["c_split"], 1)
                for u in range(8):
                    g, blk = u // 2, u % 2
                    dve.wait_ge(s["s_unit"], b * 8 + u + 1)
                    v.reduce_max(mx[:, blk * H + g * 4:blk * H + g * 4 + 4],
                                 quad[u % 4].rearrange("p (h n) -> p h n", h=4), AX.X).then_inc(s["s_max"], 1)
                dve.wait_ge(s["m_t"], b + 1)
                dve.wait_ge(s["shift_in"], b * 32)
                link(v.tensor_scalar(nmx[:], pt[0:H, 0:SQ], -1.0, None, ALU.mult))
                link(v.scalar_tensor_tensor(nmx[:, P - GLOB:P], pt[0:H, 256:256 + GLOB], -1.0, nmx[:, P - GLOB:P],
                                            ALU.mult, ALU.min))
                link(v.tensor_scalar(nmx[:, P:SQ], pt[0:H, 256 + GLOB:256 + P], -1.0, None, ALU.mult))
                link(v.tensor_copy(nmh[:], nmx[:]))
                v.tensor_tensor(nml[:], nmx[:], nmh[:].bitcast(F32), ALU.subtract).then_inc(s["m_rows"], 1)
                for g in range(KVH):
                    dve.wait_ge(s["pv_done"], b * 4 + g + 1)
                    link(v.reciprocal(rd[:], pv[g % 2][:, S + GLOB:2 * S]))
                    link(v.tensor_tensor(at[:, g, GLOB:S], pv[g % 2][:, GLOB:S], rd[:], ALU.mult))
                    v.tensor_scalar(at[:, g, 0:GLOB], pv[g % 2][:, 0:GLOB], 1.0 / S, None, ALU.mult
                                    ).then_inc(s["at_ready"], 1)
                dve.wait_ge(s["wo_done"], b + 1)
                dve.wait_ge(s["bo_added"], b + 1)
                v.tensor_tensor(tile(b, 0, 2), tile(b, 0, 2), pt[:], ALU.add).then_inc(s["x1"], 1)
                hold(dve, s["x1"], b + 1)
                norm(b, b * 3 + 2, "xn2")
                dve.wait_ge(s["n_hi"], b + 1)
                v.tensor_tensor(xr, pt[:], xp[0], ALU.subtract).then_inc(s["n_rem"], 1)
                dve.wait_ge(s["n_mid"], b + 1)
                dve.wait_ge(s["n_rem"], b + 1)
                v.tensor_tensor(xp[2], xr, xp[1], ALU.subtract).then_inc(s["n_split"], 1)
                for u in range(16):
                    kv, t = u // 2, u % 2
                    dve.wait_ge(s["xs_unit"], b * 16 + u + 1)
                    v.reduce_max(mxx[:, t * XH + kv * 4:t * XH + kv * 4 + 4],
                                 duo[u % 2][:].rearrange("p (h n) -> p h n", h=4), AX.X).then_inc(s["x_max"], 1)
                dve.wait_ge(s["xm_t"], b + 1)
                dve.wait_ge(s["xshift_in"], b * 32)
                link(v.tensor_scalar(nxh[:], pt[0:XH, 0:S], -1.0, None, ALU.mult))
                v.scalar_tensor_tensor(nxl[:], pt[0:XH, 0:S], -1.0, nxh[:], ALU.mult, ALU.subtract
                                       ).then_inc(s["x_rows"], 1)
                for t in range(2):
                    dve.wait_ge(s["xo_t"], b * 2 + t + 1)
                    o = (pt, pa)[t][:].rearrange("p (h c) -> p h c", h=XH)
                    link(v.reciprocal(rx[:], o[:, :, XD]))
                    link(v.tensor_tensor(tmp.rearrange("p (h c) -> p h c", h=XH), o[:, :, 0:XD],
                                         rx[:].unsqueeze(2).broadcast_to([P, XH, XD]), ALU.mult))
                    v.tensor_tensor(tile(b, t), tile(b, t), tmp, ALU.add).then_inc(s["x2"], 1)
                    hold(dve, s["x2"], b * 2 + t + 1)
                norm(b, b * 3 + 3, "xn3")
                dve.wait_ge(s["th_ready"], b + 1)
                link(v.tensor_scalar(sc[:], sc[:], 0.5, 0.5, ALU.mult, ALU.add))
                link(v.tensor_tensor(scb[:], sc[:], gb_s[:].unsqueeze(1).broadcast_to([P, 2, NE]), ALU.add))
                for t in range(2):
                    for g in range(GRP):
                        op = v.max(m8[:, t, g, :], scb[:, t, g * EPG:g * EPG + EPG])
                link(op)
                link(v.tensor_tensor(gs[:], m8[:, :, :, 0], m8[:, :, :, 1], ALU.add))
                other = gs[:].unsqueeze(2).broadcast_to([P, 2, GRP, GRP])
                own = gs[:].unsqueeze(3).broadcast_to([P, 2, GRP, GRP])
                v.tensor_tensor(gt[:], other, own, ALU.is_gt)
                link(v.tensor_tensor(eq[:], other, own, ALU.is_equal))
                link(v.tensor_tensor(eq[:], eq[:], first.unsqueeze(1).broadcast_to([P, 2, GRP, GRP]), ALU.mult))
                link(v.tensor_tensor(gt[:], gt[:], eq[:], ALU.add))
                link(v.reduce_sum(sel[:], gt[:], AX.X))
                link(v.tensor_scalar(sel[:], sel[:], 1.5, None, ALU.is_lt))
                link(v.tensor_tensor(scb[:].rearrange("p t (g e) -> p t g e", g=GRP),
                                     scb[:].rearrange("p t (g e) -> p t g e", g=GRP),
                                     sel[:].unsqueeze(3).broadcast_to([P, 2, GRP, EPG]), ALU.mult))
                for t in range(2):
                    link(v.max(v8[:, t, :], scb[:, t, :]))
                    link(v.max_index(i8[:, t, :], v8[:, t, :], scb[:, t, :]))
                link(v.tensor_copy(idf[:], i8[:, :, 0:TOPK]))
                v.tensor_copy(idall[:, bass.ds(b * 2 * TOPK, 2 * TOPK)], idf[:].rearrange("p t k -> p (t k)"))
                link(v.tensor_tensor(oh[:], iota.unsqueeze(1).unsqueeze(1).broadcast_to([P, 2, TOPK, NE]),
                                     idf[:].unsqueeze(3).broadcast_to([P, 2, TOPK, NE]), ALU.is_equal))
                with nc.allow_low_precision(reason="each sum is 0 or 1"):
                    v.reduce_sum(mall[:, bass.ds(b * 2 * NE, 2 * NE)], oh[:].rearrange("p t k e -> p t e k"), AX.X)
                v.tensor_tensor(ohs[:], oh[:], sc[:].unsqueeze(2).broadcast_to([P, 2, TOPK, NE]), ALU.mult
                                ).then_inc(s["sc_read"], 1)
                dve.wait_ge(s["sc_read"], b + 1)
                link(v.reduce_sum(scall[:, bass.ds(b * 2 * TOPK, 2 * TOPK)], ohs[:], AX.X))
                assert chain["n"] == STEPS, chain["n"]

            chain["base"], chain["n"] = B * STEPS, 0
            v.tensor_copy(tmp[:, 0:1], tmp[:, 0:1]).then_inc(s["route"], 1)
            dve.wait_ge(s["m_count"], 1)
            link(v.tensor_copy(cum[0], pv[1]))
            for n, d in enumerate((1, 2, 4, 8)):
                a, c = cum[n % 2], cum[(n + 1) % 2]
                v.tensor_copy(c[:, 0:d * NE], a[:, 0:d * NE])
                link(v.tensor_tensor(c[:, d * NE:], a[:, d * NE:], a[:, 0:(NT - d) * NE], ALU.add))
            link(v.tensor_copy(pos[:, 0:NE], pv[0][:, 0:NE]))
            link(v.tensor_tensor(pos[:, NE:], pv[0][:, NE:], cum[0][:, 0:(NT - 1) * NE], ALU.add))
            idv = idall[:].rearrange("p (t k) -> p t k", t=NT)
            link(v.tensor_tensor(big_oh, iota.unsqueeze(1).unsqueeze(1).broadcast_to([P, NT, TOPK, NE]),
                                 idv.unsqueeze(3).broadcast_to([P, NT, TOPK, NE]), ALU.is_equal))
            link(v.tensor_tensor(big_pr, big_oh, pos.rearrange("p (t e) -> p t e", t=NT).unsqueeze(2).broadcast_to(
                [P, NT, TOPK, NE]), ALU.mult))
            link(v.reduce_sum(posk, big_pr.rearrange("p t k e -> p (t k) e"), AX.X))
            link(v.tensor_scalar(drop, posk, CAP - 0.5, 1e6, ALU.is_gt, ALU.mult))
            link(v.scalar_tensor_tensor(slot, idall[:], float(CAP), posk, ALU.mult, ALU.add))
            link(v.tensor_tensor(slot, slot, drop, ALU.add))
            link(v.tensor_copy(slot_u, slot))
            scv = scall[:].rearrange("p (t k) -> p t k", t=NT)
            link(v.reduce_sum(tot[:, 0:NT], scv, AX.X))
            link(v.tensor_scalar(tot[:, 0:NT], tot[:, 0:NT], 1e-20, None, ALU.add))
            link(v.reciprocal(tot[:, 0:NT], tot[:, 0:NT]))
            v.scalar_tensor_tensor(wgt.rearrange("p (t k) -> p t k", t=NT), scv, 2.0,
                                   tot[:, 0:NT].unsqueeze(2).broadcast_to([P, NT, TOPK]), ALU.mult, ALU.mult
                                   ).then_inc(s["slot_ready"], 1)

            @peeled(dve, N // NB)
            def _(n):
                for m in range(DC):
                    dve.wait_ge(s["sh_th"], n * DC + m + 1)
                    dve.wait_ge(s["sh_down"], n * 4)
                    chain2 = v.scalar_tensor_tensor(ga_sh, th_sh, 1.0, duo[m % 2][:, 0:NB], ALU.add, ALU.mult)
                    chain2.then_inc(s["route"], 1)
                    dve.wait_ge(s["route"], n * DC + m + 2)
                    v.scalar_tensor_tensor(ht_sh[:, m, :], ga_sh, 0.5, duo[m % 2][:, NB:2 * NB], ALU.mult, ALU.mult
                                           ).then_inc(s["sh_h"], 1)
                for t in range(4):
                    dve.wait_ge(s["sh_down"], n * 4 + t + 1)
                    cols = res[:, bass.ds(n * (4 * D) + t * D, D)]
                    v.tensor_tensor(cols, cols, pt[:, t % 2 * D:t % 2 * D + D], ALU.add).then_inc(s["res_final"], 1)

            @peeled(dve, NE // EU)
            def _(i):
                for r in range(EU + 1):
                    if r < EU:
                        dve.wait_ge(s["th_done"], i * EU + r + 1)
                        if r >= 2:
                            dve.wait_ge(s["ht_t"], i * EU + r - 1)
                        v.scalar_tensor_tensor(th_e[r % 2], th_e[r % 2], 1.0, quad[r % 2][:, 0:F], ALU.add, ALU.mult
                                               ).then_inc(s["table_ready"], 1)
                        dve.wait_ge(s["table_ready"], i * EU + r + 1)
                        v.scalar_tensor_tensor(he[r % 2], th_e[r % 2], 0.5, quad[r % 2][:, F:2 * F], ALU.mult,
                                               ALU.mult).then_inc(s["h_done"], 1)
                    if r > 0:
                        q = r - 1
                        dve.wait_ge(s["down_done"], i * EU + q + 1)
                        if q >= 2:
                            dve.wait_ge(y_out, i * (EU * 16) + (q - 1) * 16)
                        else:
                            dve.wait_ge(y_out, i * (EU * 16))
                        v.tensor_scalar(ye[q % 2], quad[2 + q % 2], iw[q][:, 1:2].bitcast(F32), None, ALU.mult
                                        ).then_inc(s["y_ready"], 1)

        @block.tensor
        def _(pe):
            mm, tr = nc.tensor.matmul, nc.tensor.transpose

            def transpose_norm(signal):
                for t in range(2):
                    for c in range(DC):
                        op = tr(pt[:, c * S + t * P:c * S + t * P + P], xn[:, t * D + c * P:t * D + c * P + P], ident[:])
                op.then_inc(s[signal], 1)

            pe.wait_ge(s["const_ready"], 1)
            pe.wait_ge(s["w_in"], 4 * 16)
            @peeled(pe, B)
            def _(b):
                pe.wait_ge(s["xn1"], b + 1)
                pe.wait_ge(s["xt3_ready"], b)
                transpose_norm("x_t")
                pe.wait_ge(s["diag"], b + 1)
                pe.wait_ge(s["gl_ready"], b)
                for t in range(2):
                    op = mm(pv[0][:, t * P:t * P + P], ones[:], dg[:, t * P:t * P + P], start=True, stop=True)
                op.then_inc(s["cw_t"], 1)
                pe.wait_ge(s["xt_ready"], b + 1)
                pe.wait_ge(s["cwb_ready"], b + 1)
                for c in range(DC):
                    op = mm(pv[0][:, S:2 * S], wkv_s[:, c, 0:P], xt[:, c, :], start=c == 0, stop=c == DC - 1)
                op.then_inc(s["k_t"], 1)
                for ch in range(DC):
                    for c in range(DC):
                        op = mm(pa[:, ch * S:ch * S + SQ], wq_s[:, c, ch * P:ch * P + P], xt[:, c, GLOB:S],
                                start=c == 0, stop=c == DC - 1)
                op.then_inc(s["q_t"], 1)
                for n, t0 in enumerate((0, P, GLOB)):
                    for c in range(DC):
                        op = mm(pb[:, n * P:n * P + P], xt[:, c, t0:t0 + P], wkv_s[:, c, P:2 * P],
                                start=c == 0, stop=c == DC - 1)
                op.then_inc(s["v_t"], 1)
                pe.wait_ge(s["ctx_in"], b * 16 + 16)
                pe.wait_ge(s["th_ready"], b)
                for t in range(2):
                    op = tr(pv[1][:, t * P:t * P + P], ctx_s[:, t * P:t * P + P], ident[:])
                op.then_inc(s["c_t"], 1)

                pe.wait_ge(s["ks_in"], b * 96 + 96)
                pe.wait_ge(s["qs_in"], b * 48 + 48)
                pe.wait_ge(s["v_ready"], b + 1)
                rows = SPLIT_ROWS + ALIBI_ROWS
                for u in range(8):
                    g, blk = u // 2, u % 2
                    if u >= 4:
                        pe.wait_ge(s["s_max"], b * 8 + u - 3)
                    mm(quad[u % 4], identb[:], masks[:, blk, :], start=True, stop=False)
                    for h in range(4):
                        op = mm(quad[u % 4][:, h * P:h * P + P], qs[0:rows, g * 4 + h, blk * GLOB:blk * GLOB + P],
                                ks[0:rows, blk, g, :], start=False, stop=h == 3)
                    op.then_inc(s["s_unit"], 1)
                pe.wait_ge(s["s_max"], b * 8 + 8)
                tr(pt[0:H, 0:P], mx[:, 0:H], ident[:])
                tr(pt[0:H, 256:256 + P], mx[:, H:2 * H], ident[:]).then_inc(s["m_t"], 1)

                pe.wait_ge(s["shift_in"], b * 32 + 32)
                rows += SHIFT_ROWS

                def keyed(u):
                    g, blk = u // 2, u % 2
                    if u >= 4:
                        pe.wait_ge(s["e_ready"], b * 8 + u - 3)
                    mm(quad[u % 4], identb[:], masks[:, 1 - blk, :], start=True, stop=False)
                    mm(quad[u % 4], ks[0:rows, blk, g, :], qs[0:rows, g * 4:g * 4 + 4, blk * GLOB:blk * GLOB + P],
                       start=False, stop=True).then_inc(s["st_unit"], 1)

                def weigh(g):
                    pe.wait_ge(s["e_ready"], b * 8 + 2 * g + 2)
                    if g >= 2:
                        pe.wait_ge(s["at_ready"], b * 4 + g - 1)
                    o = pv[g % 2]
                    far, near = (e4[(2 * g + n) % 4].rearrange("p (h n) -> p h n", h=4) for n in range(2))
                    vals = slice(g * HD, g * HD + HD)
                    for kind in range(6):
                        for h in range(4):
                            q = o[h * HD:h * HD + HD]
                            at_ = (0, h * HD)
                            kw = dict(start=kind == 0, stop=kind == 5, skip_group_check=True, tile_position=at_)
                            if kind == 0:
                                op = mm(q[:, 0:GLOB], vs[:, 0, vals], ones[:, 0:GLOB], **kw)
                            elif kind == 1:
                                op = mm(q[:, 0:GLOB], vs[:, 1, vals], ones[:, 0:GLOB], **kw)
                            elif kind == 2:
                                op = mm(q[:, GLOB:GLOB + P], vs[:, 1, vals], far[:, h, :], **kw)
                            elif kind == 3:
                                op = mm(q[:, P:S], vs[:, 2, vals], near[:, h, :], **kw)
                            elif kind == 4:
                                op = mm(q[:, S + GLOB:S + GLOB + P], ones[:, 0:HD], far[:, h, :], **kw)
                            else:
                                op = mm(q[:, S + P:2 * S], ones[:, 0:HD], near[:, h, :], **kw)
                    op.then_inc(s["pv_done"], 1)

                for u in range(4):
                    keyed(u)
                pe.wait_ge(s["c_split"], b + 1)
                for g in range(KVH):
                    weigh(g)
                    if g < 2:
                        keyed(4 + 2 * g)
                        keyed(5 + 2 * g)
                pe.wait_ge(s["at_ready"], b * 4 + 4)
                for t in range(2):
                    for g in range(DC):
                        op = mm(pt[:, t * D:t * D + D], at[:, g, t * P:t * P + P], wo_s[:, g, :],
                                start=g == 0, stop=g == DC - 1)
                op.then_inc(s["wo_done"], 1)

                pe.wait_ge(s["xn2"], b + 1)
                transpose_norm("n_t")
                pe.wait_ge(s["kxs_in"], b * 96 + 96)
                pe.wait_ge(s["qxs_in"], b * 96 + 96)
                for u in range(16):
                    kv, t = u // 2, u % 2
                    if u >= 2:
                        pe.wait_ge(s["x_max"], b * 16 + u - 1)
                    for h in range(4):
                        op = mm(duo[u % 2][:, h * S:h * S + S], qxs[0:XSPLIT_ROWS, kv * 4 + h, t * P:t * P + P],
                                kxs[0:XSPLIT_ROWS, kv, :], start=True, stop=True)
                    op.then_inc(s["xs_unit"], 1)
                pe.wait_ge(s["x_max"], b * 16 + 16)
                for t in range(2):
                    op = tr(pt[0:XH, t * P:t * P + P], mxx[:, t * XH:t * XH + XH], ident[:])
                op.then_inc(s["xm_t"], 1)
                pe.wait_ge(s["xshift_in"], b * 32 + 32)
                pe.wait_ge(s["vx_ready"], b + 1)
                rows = XSPLIT_ROWS + SHIFT_ROWS

                def xkeyed(u):
                    kv, t = u // 2, u % 2
                    if u >= 2:
                        pe.wait_ge(s["xe_ready"], b * 16 + u - 1)
                    for h in range(2):
                        op = mm(duo[u % 2][:, h * 512:h * 512 + 512], kxs[0:rows, kv, t * P:t * P + P],
                                qxs[0:rows, kv * 4 + 2 * h:kv * 4 + 2 * h + 2, :], start=True, stop=True)
                    op.then_inc(s["xst_unit"], 1)

                def xweigh(u):
                    kv, t = u // 2, u % 2
                    pe.wait_ge(s["xe_ready"], b * 16 + u + 1)
                    if u >= 8 and u % 4 == 0:
                        pe.wait_ge(s["ox_ready"], b * 4 + u // 4 - 1)
                    for h in range(4):
                        op = mm(pv[kv // 2 % 2][h * 32:h * 32 + 32, kv % 2 * S:kv % 2 * S + S], vx[:, t, kv, :],
                                ex[u % 3][:, h * S:h * S + S], start=t == 0, stop=t == 1, tile_position=(0, h * 32))
                    op.then_inc(s["xpv_done"], 1)

                for u in range(16):
                    xkeyed(u)
                    if u > 0:
                        xweigh(u - 1)
                xweigh(15)
                pe.wait_ge(s["ox_ready"], b * 4 + 4)
                for t in range(2):
                    for kv in range(XKV):
                        op = tr((pt, pa)[t][:, kv * P:kv * P + P], ox[:, kv * S + t * P:kv * S + t * P + P], ident[:])
                    op.then_inc(s["xo_t"], 1)

                pe.wait_ge(s["xn3"], b + 1)
                transpose_norm("t3_t")
                pe.wait_ge(s["xt3_ready"], b + 1)
                for c in range(DC):
                    op = mm(pv[0][0:NE, 0:S], gw_s[:, c, :], xt3[:, c, bass.ds(b * S, S)], start=c == 0,
                            stop=c == DC - 1)
                op.then_inc(s["g_mm"], 1)
                hold(pe, s["gl_ready"], b + 1)
                for t in range(2):
                    op = tr(pv[1][:, t * NE:t * NE + NE], gl[:, t * P:t * P + P], ident[0:NE, 0:NE])
                op.then_inc(s["g_t"], 1)

            pe.wait_ge(s["route"], 1)
            mm(pv[0], trib[:], mall[:], start=True, stop=True)
            mm(pv[1], onesb[:], mall[:], start=True, stop=True).then_inc(s["m_count"], 1)

            pe.wait_ge(s["ffn_in"], 3 * 16)
            @peeled(pe, N // NB)
            def _(n):
                for m in range(DC):
                    if m < 2:
                        pe.wait_ge(s["sh_h"], n * DC)
                    else:
                        pe.wait_ge(s["sh_h"], n * DC + m - 1)
                    for half, w in enumerate((sg_s, su_s)):
                        for c in range(DC):
                            op = mm(duo[m % 2][:, half * NB:half * NB + NB], w[:, c, m * P:m * P + P],
                                    xt3[:, c, bass.ds(n * NB, NB)], start=c == 0, stop=c == DC - 1)
                    op.then_inc(s["sh_gu"], 1)
                pe.wait_ge(s["sh_h"], n * DC + DC)
                for t in range(4):
                    if t < 2:
                        pe.wait_ge(s["res_final"], n * 4)
                    else:
                        pe.wait_ge(s["res_final"], n * 4 + t - 1)
                    for c in range(DC):
                        op = mm(pt[:, t % 2 * D:t % 2 * D + D], ht_sh[:, c, t * P:t * P + P], sd_s[:, c, :],
                                start=c == 0, stop=c == DC - 1)
                    op.then_inc(s["sh_down"], 1)

            pe.wait_ge(s["res_final"], N // NB * 4)
            pe.wait_ge(s["slot_ready"], 1)
            @peeled(pe, NE // EU)
            def _(i):
                def bring(r):
                    pe.wait_ge(xg_in[r % 2], i * (EU // 2 * 16) + r // 2 * 16 + 16)
                    pe.wait_ge(s["xe_tr"], i * EU + max(r - 1, 0))
                    for c in range(DC):
                        op = tr(pt[:, r % 2 * 512 + c * P:r % 2 * 512 + c * P + P],
                                xg[r % 2].rearrange("p (n c) -> p c n", c=DC)[:, c, :], ident[:])
                    op.then_inc(s["xe_t"], 1)

                def down(r):
                    pe.wait_ge(s["ht_ready"], i * EU + r + 1)
                    pe.wait_ge(s["y_ready"], i * EU + max(r - 1, 0))
                    for c in range(2):
                        op = mm(quad[2 + r % 2], hte[r % 2][:, c, :], h2[r][:, c, :], start=c == 0, stop=c == 1)
                    op.then_inc(s["down_done"], 1)

                bring(0)
                for r in range(EU):
                    pe.wait_ge(wg_in[r], i * 48 + 48)
                    pe.wait_ge(s["xe_tr"], i * EU + r + 1)
                    pe.wait_ge(s["h_done"], i * EU + max(r - 1, 0))
                    for c in range(DC):
                        op = mm(quad[r % 2], xgt[r % 2][:, c, :], h13[r][:, c, :], start=c == 0, stop=c == DC - 1)
                    op.then_inc(s["up_done"], 1)
                    if r + 1 < EU:
                        bring(r + 1)
                    if r > 0:
                        down(r - 1)
                    pe.wait_ge(s["h_done"], i * EU + r + 1)
                    pe.wait_ge(s["ht_ready"], i * EU + max(r - 1, 0))
                    for c in range(2):
                        op = tr(pv[r % 2][:, c * P:c * P + P], he[r % 2].rearrange("p (n c) -> p c n", c=2)[:, c, :],
                                ident[:])
                    op.then_inc(s["ht_t"], 1)
                down(EU - 1)


_INS = ["x", "ctx_512", "L0_attn_Wq", "L0_attn_Wkv", "L0_attn_Wo", "L0_attn_bo", "L0_ffn_gate_w", "L0_ffn_gate_bias",
        "L0_ffn_w1", "L0_ffn_w2", "L0_ffn_w3", "L0_ffn_shared_gate", "L0_ffn_shared_up", "L0_ffn_shared_down"]


def kernel(**inputs):
    import numpy as _np
    import concourse.bacc as _bacc
    from concourse import mybir as _mybir
    from concourse.bass_utils import run_bass_kernel_spmd as _run

    nc = _bacc.Bacc("TRN2", target_bir_lowering=False, num_devices=1)
    arrays, args = {}, []
    given = {n: _np.asarray(inputs[n]) for n in _INS}
    given["L0_ffn_gate_w"] = given["L0_ffn_gate_w"].T
    given.update(constants())
    for name, a in given.items():
        a = _np.ascontiguousarray(a)
        arrays[f"in_{name}"] = a
        args.append(nc.dram_tensor(f"in_{name}", a.shape, _mybir.dt.from_np(a.dtype), kind="ExternalInput").ap())
    o = nc.dram_tensor("out_0", (B, S, D), _mybir.dt.float32, kind="ExternalOutput").ap()
    build(nc, *args, o)
    r = _run(nc, [arrays], core_ids=[0])
    return r.results[0]["out_0"]
```

```python
import numpy as np
import concourse.bass as bass
from concourse import mybir
from contextlib import ExitStack

F32 = mybir.dt.float32
F32R = mybir.dt.float32r
BF16 = mybir.dt.bfloat16
U32 = mybir.dt.uint32
ALU = mybir.AluOpType
ACT = mybir.ActivationFunctionType
AX = mybir.AxisListType

P = 128
B, S, D = 8, 256, 512
N = B * S
NT = N // P
DC = D // P
H, KVH, HD = 16, 4, 32
REP = H // KVH
GLOB, HALF = 64, 64
SQ = S - GLOB
XH, XKV, XD = 32, 8, 16
XREP = XH // XKV
NE, TOPK, F, CAP = 32, 4, 256, 128
GRP = 4
EPG = NE // GRP
EPS = 1e-5
NEG = -1e30
SPLIT_ROWS = 3 * HD
ALIBI_ROWS = 4
SHIFT_ROWS = 2
XSPLIT_ROWS = 6 * XD
EU = 4
NB = 512
ABSENT = 65535
LOOP_STEPS = 55


def _round_bits(a, bits):
    a = np.asarray(a, np.float64)
    m, e = np.frexp(a)
    return np.ldexp(np.rint(m * 2.0 ** bits) / 2.0 ** bits, e).astype(np.float32)


def constants():
    p = np.arange(P)
    upper = np.where(p[None, :] > p[:, None], 0.0, NEG).astype(np.float32)
    masks = np.stack([np.tile(upper, (1, 4)), np.tile(upper.T, (1, 4))], 1)
    tri = (p[:, None] < p[None, :]).astype(np.float32)
    mats = np.concatenate([np.eye(P, dtype=np.float32), tri], 1)
    slope = ((2.0 ** -0.5) ** np.arange(1, H + 1)).astype(np.float32)
    i = np.arange(GLOB, S).astype(np.float32)
    lift = slope[:, None] * i[None, :]
    s_hi = _round_bits(slope, 12)
    l_hi = _round_bits(lift, 12)
    wide = np.ones((1, SQ), np.float32)
    q_rows = np.stack([-s_hi[:, None] * wide, -(slope - s_hi)[:, None] * wide, l_hi, lift - l_hi])
    k_rows = np.ones((SHIFT_ROWS + ALIBI_ROWS, 2, KVH, P), np.float32)
    far, near = np.arange(P, S), np.arange(GLOB, GLOB + P)
    k_rows[0:2, 0] = far
    k_rows[0:2, 1] = -near.astype(np.float32)
    k_rows[2:4, 1] = -1.0
    first = (np.arange(GRP)[None, :] < np.arange(GRP)[:, None]).astype(np.float32).reshape(-1)
    iota = np.tile(np.arange(NE, dtype=np.float32), (P, 1))
    small = np.concatenate([np.tile(first, (P, 1)), iota], 1)
    token = (np.arange(NT)[None, :] * P + p[:, None]).astype(np.uint32)
    slots = np.zeros((NE * CAP, 2), np.uint32)
    slots[:, 0] = ABSENT
    return {"c_masks": masks, "c_mats": mats, "c_qrows": q_rows.astype(np.float32), "c_krows": k_rows,
            "c_small": small, "c_token": token, "c_slots": slots}


def build(nc, x, ctx, wq, wkv, wo, bo, gw, gb, w1, w2, w3, sg, su, sd,
          c_masks, c_mats, c_qrows, c_krows, c_small, c_token, c_slots, out):
    st = ExitStack()

    def sb(name, shape, dt=F32):
        return st.enter_context(nc.sbuf_tensor(name, shape, dt))

    def ps(name, cols):
        return st.enter_context(nc.psum_tensor(name, [P, cols], F32))

    def sem(name):
        return st.enter_context(nc.semaphore(name))

    def dram(name, shape, dt=F32):
        return nc.dram_tensor(name, shape, dt, kind="Internal").ap()

    with st:
        kd = dram("kd", [2, P, S])
        qd = dram("qd", [2, D, SQ])
        kxd = dram("kxd", [3, P, S], BF16)
        qxd = dram("qxd", [3, D, S], BF16)
        xnd = dram("xnd", [N, D])
        slot_table = dram("slot_table", [NE * CAP, 2], U32)

        res = sb("res", [P, NT * D])
        xt3 = sb("xt3", [P, DC, N])
        gw_s = sb("gw_s", [P, DC, NE])
        ident = sb("ident", [P, P])
        identb = sb("identb", [P, P], BF16)
        trib = sb("trib", [P, P], BF16)
        onesb = sb("onesb", [P, P], BF16)
        ones = sb("ones", [P, P])
        masks = sb("masks", [P, 2, 4 * P], BF16)
        small = sb("small", [P, GRP * GRP + NE])
        first = small[:, 0:GRP * GRP].rearrange("p (a b) -> p a b", a=GRP)
        iota = small[:, GRP * GRP:]
        token = sb("token", [P, NT], U32)
        gb_s = sb("gb_s", [P, NE])
        bo_s = sb("bo_s", [P, D])
        qs = sb("qs", [P, H, SQ], F32R)
        ks = sb("ks", [P, 2, KVH, P], F32R)

        ARENA = 27 * 1024
        arena = sb("arena", [P, ARENA])
        top = [0]

        def place(cols, dt=F32):
            a = arena[:, top[0]:top[0] + cols]
            top[0] += cols
            assert top[0] <= ARENA, top[0]
            if dt is not F32:
                a = a.bitcast(dt)
            return a

        wq_s = place(DC * D).rearrange("p (c n) -> p c n", c=DC)
        wkv_s = place(DC * 2 * P).rearrange("p (c n) -> p c n", c=DC)
        wo_s = place(DC * D).rearrange("p (c n) -> p c n", c=DC)
        xn1, xn2, xn3 = place(2 * D), place(2 * D), place(2 * D)
        xt_at = top[0]
        xt = place(DC * S).rearrange("p (c n) -> p c n", c=DC)
        ctx_s = place(2 * P)
        cwb = place(S)
        dg = place(2 * P)
        kh, kl = place(S, dt=F32R), place(S, dt=F32R)
        vt = place(S)
        vs = place(3 * P).rearrange("p (s n) -> p s n", s=3)
        at = place(DC * S).rearrange("p (c n) -> p c n", c=DC)
        ox_at = top[0]
        qf = place(DC * SQ).rearrange("p (c n) -> p c n", c=DC)
        qh = place(DC * SQ, dt=F32R).rearrange("p (c n) -> p c n", c=DC)
        ql = place(DC * SQ, dt=F32R).rearrange("p (c n) -> p c n", c=DC)
        ox = arena[:, ox_at:ox_at + XKV * S]
        xr_at = top[0]
        xr = place(DC * S)
        xp = [place(DC * S // 2, dt=BF16) for _ in range(3)]
        kr = place(S)
        kp = [place(S // 2, dt=BF16) for _ in range(3)]
        qxs = place(XH * S // 2, dt=BF16).rearrange("p (h n) -> p h n", h=XH)
        kxs = place(XKV * S // 2, dt=BF16).rearrange("p (h n) -> p h n", h=XKV)
        vx = place(2 * XKV * 2 * XD).rearrange("p (t h c) -> p t h c", t=2, h=XKV)
        ex_at = top[0]
        ex = [place(512) for _ in range(4)]
        e4 = [arena[:, a:a + 512] for a in (xt_at, xt_at + 512, xr_at, xr_at + 512)]
        tmp, junk = place(D // 2), place(D)
        attention_top = top[0]
        nxh, nxl = sb("nxh", [XH, S], BF16), sb("nxl", [XH, S], BF16)
        nmx = sb("nmx", [H, SQ])
        nmh, nml = sb("nmh", [H, SQ], F32R), sb("nml", [H, SQ], F32R)
        stats = {n: (sb(f"bnst{n}", [P, 2, 6]), sb(f"mv{n}", [P, 2, 2]), sb(f"rstd{n}", [P, 2])) for n in (1, 2, 3)}
        power = sb("power", [P, 2])
        asum = sb("asum", [P, 2])
        mx = sb("mx", [P, 2 * H])
        mxx = sb("mxx", [P, 2 * XH])
        rd = sb("rd", [P, SQ])
        rx = sb("rx", [P, XH // 2])
        gl = sb("gl", [NE, S])
        sc = sb("sc", [P, 2, NE])
        scb = sb("scb", [P, 2, NE])
        m8 = sb("m8", [P, 2, GRP, 8])
        gs = sb("gs", [P, 2, GRP])
        gt = sb("gt", [P, 2, GRP, GRP])
        eq = sb("eq", [P, 2, GRP, GRP])
        sel = sb("sel", [P, 2, GRP])
        v8 = sb("v8", [P, 2, 8])
        i8 = sb("i8", [P, 2, 8], U32)
        idf = sb("idf", [P, 2, TOPK])
        oh = sb("oh", [P, 2, TOPK, NE])
        ohs = sb("ohs", [P, 2, TOPK, NE])
        chosen = sb("chosen", [P, 2 * NE], BF16)
        seen = sb("seen", [P, NE])
        pos = sb("pos", [P, 2, NE])
        sck, posk, drop, slot, wgt = (sb(n, [P, 2, TOPK]) for n in ("sck", "posk", "drop", "slot", "wgt"))
        tot = sb("tot", [P, 2])
        slot_u = sb("slot_u", [P, 2 * TOPK], U32)
        sdat = sb("sdat", [P, 2 * TOPK, 2], U32)

        top[0] = 0
        sg_s = place(DC * D).rearrange("p (c n) -> p c n", c=DC)
        su_s = place(DC * D).rearrange("p (c n) -> p c n", c=DC)
        sd_s = place(DC * D).rearrange("p (c n) -> p c n", c=DC)
        h13 = [place(DC * 2 * F).rearrange("p (c n) -> p c n", c=DC) for _ in range(EU)]
        h2 = [place(2 * D).rearrange("p (c n) -> p c n", c=2) for _ in range(EU)]
        ht_sh = place(DC * NB).rearrange("p (c n) -> p c n", c=DC)
        th_sh, ga_sh = place(NB), place(NB)
        top[0] -= DC * NB + 2 * NB
        xgt = [place(D).rearrange("p (c n) -> p c n", c=DC) for r in range(2)]
        th_e = [place(F) for r in range(2)]
        he = [place(F) for r in range(2)]
        hte = [place(2 * P).rearrange("p (c n) -> p c n", c=2) for r in range(2)]
        ye = [place(D) for r in range(2)]
        assert top[0] <= attention_top
        top[0] = attention_top
        xg = [place(D) for _ in range(2)]
        iw = [sb(f"iw{r}", [P, 2], U32) for r in range(EU)]

        pt, qa, qx, va, vb = ps("pt", 1024), ps("qa", 1024), ps("qx", 1024), ps("va", 512), ps("vb", 512)
        abank = [qa[:, 0:512], qa[:, 512:1024]]
        xbank = [qx[:, 0:512], qx[:, 512:1024]]
        quad = abank + xbank
        duo = [qa, qx]
        pv = [va[:, :], vb[:, :]]

        names = """const_in const_moved const_ready clear x_in w_in ffn_in ctx_in
            ln1_stats ln2_stats ln3_stats ln1_rstd ln2_rstd ln3_rstd xn1 xn2 xn3 abs_sum diag x_t xt_ready cw_t
            cwb_ready k_t k_split vt_t vt_ready v_t v_ready q_t q_split
            bo_added kd_out ks_in qd_out qs_in s_unit s_max m_t m_rows shift_in st_unit e_ready pv_done at_ready
            wo_done x1 c_t c_hi c_rem c_mid c_split vx_ready kxd_out kxs_in n_t n_hi n_rem n_mid n_split
            qxd_out qxs_in xs_unit x_max xm_t x_rows xshift_in xst_unit xe_ready xpv_done ox_ready xo_t x2
            xnd_out t3_t xt3_ready g_mm gl_ready g_t th_ready chosen dve
            pos_t slot_ready sdat_ready init_out sc_out
            sh_gu sh_th sh_ga sh_h sh_down res_final base_out
            xe_t xe_tr up_done th_done ga_done h_done ht_t ht_ready down_done y_ready""".split()
        s = {n: sem(n) for n in names}
        iw_in = [sem(f"iw_in{r}") for r in range(EU)]
        wg_in = [sem(f"wg_in{r}") for r in range(EU)]
        xg_in = [sem(f"xg_in{r}") for r in range(2)]
        y_out = sem("y_out")
        block = st.enter_context(nc.Block())

        def tile(b, t, n=1):
            return res[:, bass.ds(b * (2 * D) + t * D, n * D)]

        def peeled(engine, count):
            def run(body):
                body(0)
                with engine.Fori(1, count) as i:
                    body(i)
            return run

        def pipelined(engine):
            def run(body):
                body(0, a=True, x=False, g=False, n=True)
                body(1, a=True, x=True, g=False, n=True)
                body(2, a=True, x=True, g=True, n=True)
                with engine.Fori(3, B - 1) as k:
                    body(k, a=True, x=True, g=True, n=True)
                body(B - 1, a=True, x=True, g=True, n=False)
                body(B, a=False, x=True, g=True, n=False)
                body(B + 1, a=False, x=False, g=True, n=False)
            return run

        def expert_rounds(engine):
            def run(body):
                body(0, True, False)
                with engine.Fori(1, NE // EU - 1) as i:
                    body(i, False, False)
                body(NE // EU - 1, False, True)
            return run

        wait_register = {}

        def hold(engine, semaphore, count):
            if isinstance(count, int):
                engine.wait_ge(semaphore, count)
                return
            if engine.engine not in wait_register:
                wait_register[engine.engine] = engine.alloc_register("wait_count")
            engine.reg_mov(wait_register[engine.engine], count)
            engine.wait_ge(s["const_ready"], 1)
            engine.wait_ge(semaphore, wait_register[engine.engine])

        def tile(b, t, n=1):
            return res[:, bass.ds(b * (2 * D) + t * D, n * D)]

        XU = 32
        AU = 8

        @block.sync
        def _(sp):
            def go(dst, src, signal):
                sp.dma_start(dst, src).then_inc(s[signal], 16)

            go(res[:, :].rearrange("p (t d) -> p t d", t=NT), x.rearrange("b (u p) d -> p (b u) d", p=P), "x_in")
            go(xn3[:, 0:2 * P], c_mats, "const_in")
            go(xr[:, 0:1024].rearrange("p (a n) -> p a n", a=2), c_masks, "const_in")
            go(small[:], c_small, "const_in")
            go(token[:], c_token, "const_in")
            go(gb_s[:], gb.rearrange("(o n) -> o n", o=1).broadcast_to([P, NE]), "const_in")
            go(bo_s[:], bo.rearrange("(o n) -> o n", o=1).broadcast_to([P, D]), "const_in")
            go(arena[96:102, ex_at:ex_at + 2 * KVH * P].rearrange("p (a h n) -> p a h n", a=2, h=KVH), c_krows,
               "const_in")
            go(arena[96:100, 0:H * SQ].rearrange("p (h n) -> p h n", h=H), c_qrows, "const_in")
            sp.wait_ge(s["const_moved"], 1)
            for dst, src in ((wkv_s, wkv), (wq_s, wq), (wo_s, wo), (gw_s[:], gw)):
                go(dst, src.rearrange("(c p) n -> p c n", p=P), "w_in")
            go(slot_table, c_slots, "init_out")

            @pipelined(sp)
            def _(k, a, x, g, n):
                if a:
                    hold(sp, s["c_t"], k)
                    hold(sp, s["vx_ready"], k)
                    go(ctx_s.rearrange("p (t n) -> p t n", t=2),
                       ctx[bass.ds(k, 1)].rearrange("o (t p) n -> p (o t) n", p=P), "ctx_in")
                    hold(sp, s["k_split"], k + 1)
                    go(kd[0], kh.bitcast(F32), "kd_out")
                    go(kd[1], kl.bitcast(F32), "kd_out")
                    hold(sp, s["kd_out"], k * 32 + 32)
                    for m, part in enumerate((0, 1, 0)):
                        for blk, j0 in enumerate((P, GLOB)):
                            go(ks[m * HD:m * HD + HD, blk].bitcast(F32),
                               kd[part].rearrange("(g d) t -> d g t", d=HD)[:, :, j0:j0 + P], "ks_in")
                    hold(sp, s["q_split"], k + 1)
                    go(qd[0].rearrange("(c p) t -> p c t", p=P), qh.bitcast(F32), "qd_out")
                    go(qd[1].rearrange("(c p) t -> p c t", p=P), ql.bitcast(F32), "qd_out")
                    hold(sp, s["qd_out"], k * 32 + 32)
                    for m, part in enumerate((0, 0, 1)):
                        go(qs[m * HD:m * HD + HD].bitcast(F32), qd[part].rearrange("(h d) t -> d h t", d=HD), "qs_in")
                    hold(sp, s["c_split"], k + 1)
                    hold(sp, s["kxs_in"], k * 96)
                    for m in range(3):
                        go(kxd[m], kp[m], "kxd_out")
                if x:
                    hold(sp, s["x_rows"], k)
                    go(qxs[96:97], nxh[:], "xshift_in")
                    go(qxs[97:98], nxl[:], "xshift_in")
                if a:
                    hold(sp, s["m_rows"], k + 1)
                    go(qs[100:101].bitcast(F32), nmh[:].bitcast(F32), "shift_in")
                    go(qs[101:102].bitcast(F32), nml[:].bitcast(F32), "shift_in")
                    hold(sp, s["n_split"], k + 1)
                    hold(sp, s["qxs_in"], k * 96)
                    for m in range(3):
                        go(qxd[m].rearrange("(c p) t -> p c t", p=P), xp[m].rearrange("p (c t) -> p c t", c=DC),
                           "qxd_out")
                    hold(sp, s["kxd_out"], k * 48 + 48)
                    hold(sp, s["qxd_out"], k * 48 + 48)
                    hold(sp, s["xst_unit"], k * XU)
                    for m, part in enumerate((0, 1, 0, 1, 2, 0)):
                        go(kxs[m * XD:m * XD + XD], kxd[part].rearrange("(g d) t -> d g t", d=XD), "kxs_in")
                    for m, part in enumerate((0, 0, 1, 1, 0, 2)):
                        go(qxs[m * XD:m * XD + XD], qxd[part].rearrange("(h d) t -> d h t", d=XD), "qxs_in")
                if x:
                    hold(sp, s["xn3"], k)
                    go(xnd[bass.ds(k * S - S, S)].rearrange("(t p) d -> p t d", p=P),
                       xn3.rearrange("p (t d) -> p t d", t=2), "xnd_out")

            sp.wait_ge(s["wo_done"], B)
            for dst, src in ((sg_s, sg), (su_s, su), (sd_s, sd)):
                go(dst, src.rearrange("(c p) n -> p c n", p=P), "ffn_in")
            sp.wait_ge(s["t3_t"], B)
            sp.wait_ge(s["xnd_out"], B * 16)

            @peeled(sp, NE // EU)
            def _(i):
                for r in range(EU):
                    if not isinstance(i, int):
                        hold(sp, s["down_done"], i * EU + (r + 1 - EU))
                    e = i * EU + r
                    w13 = h13[r].rearrange("p c (a f) -> p c a f", a=2)
                    sp.dma_start(w13[:, :, 0], w1[bass.ds(e, 1)].rearrange("o (p c) f -> p (o c) f", c=DC)
                                 ).then_inc(wg_in[r], 16)
                    sp.dma_start(w13[:, :, 1], w3[bass.ds(e, 1)].rearrange("o (p c) f -> p (o c) f", c=DC)
                                 ).then_inc(wg_in[r], 16)
                    sp.dma_start(h2[r], w2[bass.ds(e, 1)].rearrange("o (p c) d -> p (o c) d", c=2)
                                 ).then_inc(wg_in[r], 16)

        @block.gpsimd
        def _(pool):
            def norm_scale(n, count):
                pool.wait_ge(s[f"ln{n}_stats"], count)
                nc.gpsimd.tensor_tensor(stats[n][2][:], stats[n][1][:, :, 1], power[:], ALU.pow
                                        ).then_inc(s[f"ln{n}_rstd"], 1)

            nc.gpsimd.memset(ones[:], 1.0)
            nc.gpsimd.memset(onesb[:], 1.0)
            nc.gpsimd.memset(seen[:], 0.0)
            nc.gpsimd.memset(vx, 1.0)
            for r in range(2):
                op = nc.gpsimd.memset(xg[r], 0.0)
            op.then_inc(s["clear"], 1)
            pool.wait_ge(s["clear"], 1)
            nc.gpsimd.memset(kxs[96:98], 1.0).then_inc(s["clear"], 1)
            pool.wait_ge(s["clear"], 2)
            pool.wait_ge(s["const_moved"], 1)
            nc.gpsimd.memset(power[:], -0.5).then_inc(s["const_ready"], 1)
            pool.wait_ge(s["const_ready"], 1)
            norm_scale(1, 1)

            @pipelined(pool)
            def _(k, a, x, g, n):
                if a:
                    pool.wait_ge(s["xn1"], k + 1)
                    for t in range(2):
                        op = nc.gpsimd.tensor_tensor(tile(k, t), tile(k, t), bo_s[:], ALU.add)
                    op.then_inc(s["bo_added"], 1)
                    norm_scale(2, k + 1)
                if n:
                    norm_scale(1, k + 2)
                if x:
                    norm_scale(3, k)
                if g:
                    pool.wait_ge(s["slot_ready"], k - 1)
                    if isinstance(k, int) and k == 2:
                        pool.wait_ge(s["init_out"], 16)
                    nc.gpsimd.tensor_copy(sdat[:, :, 0].rearrange("p (t k) -> p t k", t=2),
                                          token[:, bass.ds(k * 2 - 4, 2)].unsqueeze(2).broadcast_to([P, 2, TOPK])
                                          ).then_inc(s["sdat_ready"], 1)
                    hold(pool, s["sdat_ready"], k - 1)
                    for c in range(2 * TOPK):
                        nc.gpsimd.indirect_dma_start(
                            slot_table, bass.IndirectOffsetOnAxis(ap=slot_u[:, c:c + 1], axis=0), sdat[:, c, :], None,
                            bounds_check=NE * CAP - 1, oob_is_err=False).then_inc(s["sc_out"], 16)

            pool.wait_ge(s["sc_out"], B * 2 * TOPK * 16)
            pool.wait_ge(s["xnd_out"], B * 16)

            def load_slots(i, r):
                pool.dma_start(iw[r % EU][:], slot_table[bass.ds(i * (EU * CAP) + r * CAP, CAP)]
                               ).then_inc(iw_in[r % EU], 16)

            def gather(i, r):
                hold(pool, iw_in[r % EU], i * 16 + r // EU * 16 + 16)
                nc.gpsimd.indirect_dma_start(
                    xg[r % 2], None, xnd, bass.IndirectOffsetOnAxis(ap=iw[r % EU][:, 0:1], axis=0),
                    bounds_check=N - 1, oob_is_err=False).then_inc(xg_in[r % 2], 16)

            for r in range(3):
                load_slots(0, r)
            for r in range(2):
                gather(0, r)

            @peeled(pool, N // NB)
            def _(n):
                hold(pool, s["res_final"], n * 4 + 4)
                pool.dma_start(out.rearrange("b (u p) d -> p (b u) d", p=P)[:, bass.ds(n * 4, 4)],
                               res[:, bass.ds(n * 4 * D, 4 * D)].rearrange("p (t d) -> p t d", t=4)
                               ).then_inc(s["base_out"], 16)
            pool.wait_ge(s["base_out"], N // NB * 16)
            flat = out.rearrange("b s d -> (b s) d")

            @expert_rounds(pool)
            def _(i, first, last):
                for r in range(EU):
                    if not last or r + 2 < EU:
                        hold(pool, s["xe_t"], i * EU + r + 1)
                        gather(i, r + 2)
                    hold(pool, s["y_ready"], i * EU + r + 1)
                    hold(pool, y_out, i * (EU * 16) + r * 16)
                    nc.gpsimd.indirect_dma_start(flat, bass.IndirectOffsetOnAxis(ap=iw[r][:, 0:1], axis=0), ye[r % 2],
                                                 None, bounds_check=N - 1, oob_is_err=False,
                                                 compute_op=ALU.add).then_inc(y_out, 16)
                    if not last or r + 3 < EU:
                        load_slots(i, r + 3)
            pool.wait_ge(y_out, NE * 16)

        @block.scalar
        def _(act):
            def copy(dst, src, signal, func=ACT.Copy, **kw):
                nc.scalar.activation(dst, src, func, **kw).then_inc(s[signal], 1)

            def token_sums(b):
                act.wait_ge(s["xn1"], b + 1)
                for t in range(2):
                    copy(junk, xn1[:, t * D:t * D + D], "abs_sum", ACT.Abs, accum_out=asum[:, t:t + 1])
                    act.wait_ge(s["abs_sum"], b * 3 + t + 1)
                copy(asum[:], asum[:], "abs_sum", ACT.Exp, scale=-1.0)

            act.wait_ge(s["const_in"], 8 * 16)
            nc.scalar.activation(ident[:], xn3[:, 0:P], ACT.Copy)
            nc.scalar.activation(identb[:], xn3[:, 0:P], ACT.Copy)
            nc.scalar.activation(trib[:], xn3[:, P:2 * P], ACT.Copy)
            nc.scalar.activation(masks[:], xr[:, 0:1024].rearrange("p (a n) -> p a n", a=2), ACT.Copy)
            nc.scalar.activation(ks[96:102], arena[96:102, ex_at:ex_at + 2 * KVH * P].rearrange(
                "p (a h n) -> p a h n", a=2, h=KVH), ACT.Copy)
            nc.scalar.activation(qs[96:100], arena[96:100, 0:H * SQ].rearrange("p (h n) -> p h n", h=H), ACT.Copy
                                 ).then_inc(s["const_moved"], 1)
            act.wait_ge(s["const_ready"], 1)
            token_sums(0)

            @pipelined(act)
            def _(k, a, x, g, n):
                if g:
                    act.wait_ge(s["t3_t"], k - 1)
                    copy(xt3[:, :, bass.ds(k * S - 2 * S, S)], pt[:].rearrange("p (c n) -> p c n", c=DC), "xt3_ready")
                if a:
                    act.wait_ge(s["cw_t"], k + 1)
                    copy(cwb, va[:, 0:S], "cwb_ready", scale=float(HD) ** -0.5)
                    act.wait_ge(s["x_t"], k + 1)
                    copy(xt, pt[:].rearrange("p (c n) -> p c n", c=DC), "xt_ready")
                if g:
                    act.wait_ge(s["g_mm"], k - 1)
                    copy(gl[:], vb[0:NE, 0:S], "gl_ready")
                    act.wait_ge(s["g_t"], k - 1)
                    copy(sc[:], vb[:, S:S + 2 * NE].rearrange("p (t e) -> p t e", t=2), "th_ready", ACT.Tanh,
                         scale=0.5)
                if a:
                    act.wait_ge(s["v_t"], k + 1)
                    copy(vs, va[:, 0:3 * P].rearrange("p (s n) -> p s n", s=3), "v_ready")
                    act.wait_ge(s["c_t"], k + 1)
                    copy(kp[0], va[:, 0:S], "c_hi")
                    act.wait_ge(s["c_rem"], k + 1)
                    copy(kp[1], kr, "c_mid")

                def cross(v):
                    act.wait_ge(s["xst_unit"], k * XU - XU + v + 1)
                    if v >= 4:
                        act.wait_ge(s["xpv_done"], k * XU - XU + v - 3)
                    copy(ex[v % 4], xbank[v % 2], "xe_ready", ACT.Exp, scale=float(XD) ** -0.5)
                    if v % 8 == 1 and v > 8:
                        pair_out(v // 8 - 1)

                def pair_out(pair):
                    act.wait_ge(s["xpv_done"], k * XU - XU + pair * 8 + 8)
                    copy(ox[:, pair * 512:pair * 512 + 512], vb[:, :], "ox_ready")

                for j in range(AU):
                    if x:
                        cross(2 * j)
                    if a:
                        act.wait_ge(s["st_unit"], k * AU + j + 1)
                        if j >= 4:
                            act.wait_ge(s["pv_done"], k * KVH + (j - 4) // 2 + 1)
                        copy(e4[j % 4], abank[j % 2], "e_ready", ACT.Exp)
                    if x:
                        cross(2 * j + 1)
                if x:
                    for v in range(16, XU):
                        cross(v)
                if a:
                    act.wait_ge(s["n_t"], k + 1)
                    copy(xp[0], pt[:], "n_hi")
                if x:
                    pair_out(3)
                if a:
                    act.wait_ge(s["n_rem"], k + 1)
                    copy(xp[1], xr, "n_mid")
                    act.wait_ge(s["ctx_in"], k * 16 + 16)
                    copy(vx[:, :, :, 0:XD], ctx_s.rearrange("p (t h c) -> p t h c", t=2, h=XKV), "vx_ready")
                if n:
                    token_sums(k + 1)

            @peeled(act, N // NB)
            def _(n):
                for m in range(DC):
                    act.wait_ge(s["sh_gu"], n * DC + m + 1)
                    act.wait_ge(s["sh_h"], n * DC + m)
                    copy(th_sh, duo[m % 2][:, 0:NB], "sh_th", ACT.Tanh, scale=0.5)

            def tokens_out(i, r):
                act.wait_ge(s["xe_t"], i * EU + r + 1)
                copy(xgt[r % 2], pt[:, r % 2 * 512:r % 2 * 512 + 512].rearrange("p (c n) -> p c n", c=DC), "xe_tr")

            tokens_out(0, 0)

            @expert_rounds(act)
            def _(i, first, last):
                for r in range(EU):
                    act.wait_ge(s["up_done"], i * EU + r + 1)
                    if not first or r >= 2:
                        act.wait_ge(s["h_done"], i * EU + r - 1)
                    copy(th_e[r % 2], quad[r % 2][:, 0:F], "th_done", ACT.Tanh, scale=0.5)
                    if not last or r + 1 < EU:
                        tokens_out(i, r + 1)
                    act.wait_ge(s["ht_t"], i * EU + r + 1)
                    if not first or r >= 2:
                        act.wait_ge(s["down_done"], i * EU + r - 1)
                    copy(hte[r % 2], pv[r % 2][:, 0:2 * P].rearrange("p (c n) -> p c n", c=2), "ht_ready")

        @block.vector
        def _(dve):
            v_ = nc.vector
            chain = {"base": 0, "n": 0}

            def link(ins):
                chain["n"] += 1
                ins.then_inc(s["dve"], 1)
                hold(dve, s["dve"], chain["base"] + chain["n"])

            def norm(n, b, dst):
                bnst, mv, rstd = stats[n]
                for t in range(2):
                    op = v_.bn_stats(bnst[:, t, :], tile(b, t))
                link(op)
                for t in range(2):
                    op = v_.bn_aggr(mv[:, t, :], bnst[:, t, :])
                link(op)
                v_.tensor_scalar(mv[:, :, 1], mv[:, :, 1], EPS, None, ALU.add).then_inc(s[f"ln{n}_stats"], 1)
                dve.wait_ge(s[f"ln{n}_rstd"], b + 1)
                for t in range(2):
                    op = v_.tensor_scalar(dst[:, t * D:t * D + D], tile(b, t), mv[:, t, 0:1], rstd[:, t:t + 1],
                                          ALU.subtract, ALU.mult)
                op.then_inc(s[f"xn{n}"], 1)

            def token_weights(b):
                dve.wait_ge(s["abs_sum"], b * 3 + 3)
                link(v_.tensor_scalar(asum[:], asum[:], 1.0, None, ALU.add))
                link(v_.reciprocal(asum[:], asum[:]))
                for t in range(2):
                    op = v_.tensor_scalar(dg[:, t * P:t * P + P], ident[:], asum[:, t:t + 1], None, ALU.mult)
                op.then_inc(s["diag"], 1)

            def choose():
                link(v_.tensor_scalar(sc[:], sc[:], 0.5, 0.5, ALU.mult, ALU.add))
                link(v_.tensor_tensor(scb[:], sc[:], gb_s[:].unsqueeze(1).broadcast_to([P, 2, NE]), ALU.add))
                for t in range(2):
                    for q in range(GRP):
                        op = v_.max(m8[:, t, q, :], scb[:, t, q * EPG:q * EPG + EPG])
                link(op)
                link(v_.tensor_tensor(gs[:], m8[:, :, :, 0], m8[:, :, :, 1], ALU.add))
                other = gs[:].unsqueeze(2).broadcast_to([P, 2, GRP, GRP])
                own = gs[:].unsqueeze(3).broadcast_to([P, 2, GRP, GRP])
                v_.tensor_tensor(gt[:], other, own, ALU.is_gt)
                link(v_.tensor_tensor(eq[:], other, own, ALU.is_equal))
                link(v_.tensor_tensor(eq[:], eq[:], first_in.unsqueeze(1).broadcast_to([P, 2, GRP, GRP]), ALU.mult))
                link(v_.tensor_tensor(gt[:], gt[:], eq[:], ALU.add))
                link(v_.reduce_sum(sel[:], gt[:], AX.X))
                link(v_.tensor_scalar(sel[:], sel[:], 1.5, None, ALU.is_lt))
                by_group = scb[:].rearrange("p t (g e) -> p t g e", g=GRP)
                link(v_.tensor_tensor(by_group, by_group, sel[:].unsqueeze(3).broadcast_to([P, 2, GRP, EPG]),
                                      ALU.mult))
                for t in range(2):
                    op = v_.max(v8[:, t, :], scb[:, t, :])
                link(op)
                for t in range(2):
                    op = v_.max_index(i8[:, t, :], v8[:, t, :], scb[:, t, :])
                link(op)
                link(v_.tensor_copy(idf[:], i8[:, :, 0:TOPK]))
                link(v_.tensor_tensor(oh[:], iota.unsqueeze(1).unsqueeze(1).broadcast_to([P, 2, TOPK, NE]),
                                      idf[:].unsqueeze(3).broadcast_to([P, 2, TOPK, NE]), ALU.is_equal))
                with nc.allow_low_precision(reason="each sum is 0 or 1"):
                    v_.reduce_sum(chosen[:].rearrange("p (t e) -> p t e", t=2), oh[:].rearrange(
                        "p t k e -> p t e k"), AX.X).then_inc(s["chosen"], 1)
                link(v_.tensor_tensor(ohs[:], oh[:], sc[:].unsqueeze(2).broadcast_to([P, 2, TOPK, NE]), ALU.mult))
                link(v_.reduce_sum(sck[:], ohs[:], AX.X))
                link(v_.reduce_sum(tot[:], sck[:], AX.X))
                link(v_.tensor_scalar(tot[:], tot[:], 1e-20, None, ALU.add))
                link(v_.reciprocal(tot[:], tot[:]))
                link(v_.scalar_tensor_tensor(wgt[:], sck[:], 2.0, tot[:].unsqueeze(2).broadcast_to([P, 2, TOPK]),
                                             ALU.mult, ALU.mult))

            def take_slots(k):
                dve.wait_ge(s["pos_t"], k - 1)
                hold(dve, s["sc_out"], k * (2 * TOPK * 16) - 4 * TOPK * 16)
                count = xbank[0]
                link(v_.tensor_tensor(pos[:], count[:, 0:2 * NE].rearrange("p (t e) -> p t e", t=2),
                                      seen[:].unsqueeze(1).broadcast_to([P, 2, NE]), ALU.add))
                v_.tensor_tensor(seen[:], seen[:], count[:, 2 * NE:3 * NE], ALU.add)
                link(v_.tensor_tensor(ohs[:], oh[:], pos[:].unsqueeze(2).broadcast_to([P, 2, TOPK, NE]), ALU.mult))
                link(v_.reduce_sum(posk[:], ohs[:], AX.X))
                link(v_.tensor_scalar(drop[:], posk[:], CAP - 0.5, 1e6, ALU.is_gt, ALU.mult))
                link(v_.scalar_tensor_tensor(slot[:], idf[:], float(CAP), posk[:], ALU.mult, ALU.add))
                link(v_.tensor_tensor(slot[:], slot[:], drop[:], ALU.add))
                v_.tensor_copy(sdat[:, :, 1].bitcast(F32), wgt[:].rearrange("p t k -> p (t k)"))
                v_.tensor_copy(slot_u[:], slot[:].rearrange("p t k -> p (t k)")).then_inc(s["slot_ready"], 1)

            first_in = first
            dve.wait_ge(s["x_in"], 16)
            dve.wait_ge(s["const_ready"], 1)
            norm(1, 0, xn1)
            token_weights(0)
            steps = {}

            @pipelined(dve)
            def _(k, a, x, g, n):
                if isinstance(k, int):
                    if "loop" in steps:
                        chain.update(base=steps.pop("loop") + (B - 4) * LOOP_STEPS, n=0)
                    else:
                        chain.update(base=chain["base"] + chain["n"], n=0)
                else:
                    steps["loop"] = chain["base"] + chain["n"]
                    chain.update(base=k * LOOP_STEPS + (steps["loop"] - 3 * LOOP_STEPS), n=0)
                if g:
                    dve.wait_ge(s["th_ready"], k - 1)
                    hold(dve, s["pos_t"], k - 2)
                    choose()
                if a:
                    dve.wait_ge(s["k_t"], k + 1)
                    dve.wait_ge(s["kd_out"], k * 32)
                    v_.tensor_copy(vt, va[:, S:2 * S]).then_inc(s["vt_ready"], 1)
                    link(v_.tensor_copy(kh, va[:, 0:S]))
                    v_.tensor_tensor(kl, va[:, 0:S], kh.bitcast(F32), ALU.subtract).then_inc(s["k_split"], 1)

                def queries():
                    dve.wait_ge(s["q_t"], k + 1)
                    dve.wait_ge(s["cwb_ready"], k + 1)
                    link(v_.tensor_tensor(qf, qa[:].rearrange("p (c n) -> p c n", c=DC)[:, :, 0:SQ],
                                          cwb[:, GLOB:S].unsqueeze(1).broadcast_to([P, DC, SQ]), ALU.mult))
                    link(v_.tensor_copy(qh, qf))
                    v_.tensor_tensor(ql, qf, qh.bitcast(F32), ALU.subtract).then_inc(s["q_split"], 1)

                def context_rem():
                    dve.wait_ge(s["c_hi"], k + 1)
                    v_.tensor_tensor(kr, va[:, 0:S], kp[0], ALU.subtract).then_inc(s["c_rem"], 1)

                def context_low():
                    dve.wait_ge(s["c_mid"], k + 1)
                    v_.tensor_tensor(kp[2], kr, kp[1], ALU.subtract).then_inc(s["c_split"], 1)

                if x:
                    for v in range(XU):
                        kv, t, half = v // 4, v // 2 % 2, v % 2
                        dve.wait_ge(s["xs_unit"], k * XU - XU + v + 1)
                        col = t * XH + kv * 4 + half * 2
                        v_.reduce_max(mxx[:, col:col + 2], xbank[v % 2].rearrange("p (h n) -> p h n", h=2), AX.X
                                      ).then_inc(s["x_max"], 1)
                        if a:
                            if v == 12:
                                queries()
                            elif v == 20:
                                context_rem()
                            elif v == 24:
                                context_low()
                    dve.wait_ge(s["xm_t"], k)
                    dve.wait_ge(s["xshift_in"], k * 32 - 32)
                    link(v_.tensor_scalar(nxh[:], vb[0:XH, 0:S], -1.0, None, ALU.mult))
                    v_.scalar_tensor_tensor(nxl[:], vb[0:XH, 0:S], -1.0, nxh[:], ALU.mult, ALU.subtract
                                            ).then_inc(s["x_rows"], 1)
                else:
                    if a:
                        queries()
                        context_rem()
                        context_low()
                if a:
                    for u in range(AU):
                        q, blk = u // 2, u % 2
                        dve.wait_ge(s["s_unit"], k * AU + u + 1)
                        v_.reduce_max(mx[:, blk * H + q * 4:blk * H + q * 4 + 4],
                                      abank[u % 2].rearrange("p (h n) -> p h n", h=4), AX.X).then_inc(s["s_max"], 1)
                    dve.wait_ge(s["m_t"], k + 1)
                    dve.wait_ge(s["shift_in"], k * 32)
                    link(v_.tensor_scalar(nmx[:, 0:P], pt[0:H, 0:P], -1.0, None, ALU.mult))
                    link(v_.scalar_tensor_tensor(nmx[:, P - GLOB:P], pt[0:H, 256:256 + GLOB], -1.0,
                                                 nmx[:, P - GLOB:P], ALU.mult, ALU.min))
                    link(v_.tensor_scalar(nmx[:, P:SQ], pt[0:H, 256 + GLOB:256 + P], -1.0, None, ALU.mult))
                    link(v_.tensor_copy(nmh[:], nmx[:]))
                    v_.tensor_tensor(nml[:], nmx[:], nmh[:].bitcast(F32), ALU.subtract).then_inc(s["m_rows"], 1)
                    for q in range(KVH):
                        dve.wait_ge(s["pv_done"], k * KVH + q + 1)
                        link(v_.reciprocal(rd[:], va[:, S + GLOB:2 * S]))
                        v_.tensor_tensor(at[:, q, GLOB:S], va[:, GLOB:S], rd[:], ALU.mult)
                        v_.tensor_scalar(at[:, q, 0:GLOB], va[:, 0:GLOB], 1.0 / S, None, ALU.mult
                                         ).then_inc(s["at_ready"], 1)
                    dve.wait_ge(s["wo_done"], k + 1)
                    dve.wait_ge(s["bo_added"], k + 1)
                    link(v_.tensor_tensor(tile(k, 0, 2), tile(k, 0, 2), pt[:], ALU.add))
                    norm(2, k, xn2)
                if n:
                    norm(1, k + 1, xn1)
                if a:
                    dve.wait_ge(s["n_hi"], k + 1)
                    v_.tensor_tensor(xr, pt[:], xp[0], ALU.subtract).then_inc(s["n_rem"], 1)
                    dve.wait_ge(s["n_mid"], k + 1)
                    v_.tensor_tensor(xp[2], xr, xp[1], ALU.subtract).then_inc(s["n_split"], 1)
                if g:
                    take_slots(k)
                if n:
                    token_weights(k + 1)
                if x:
                    for w in range(4):
                        t, half = w // 2, w % 2
                        dve.wait_ge(s["xo_t"], k * 4 - 4 + w + 1)
                        o = pt[:, half * 512:half * 512 + 512].rearrange("p (h c) -> p h c", h=XH // 2)
                        link(v_.reciprocal(rx[:], o[:, :, XD]))
                        link(v_.tensor_tensor(tmp.rearrange("p (h c) -> p h c", h=XH // 2), o[:, :, 0:XD],
                                              rx[:].unsqueeze(2).broadcast_to([P, XH // 2, XD]), ALU.mult))
                        cols = res[:, bass.ds(k * (2 * D) + (t * D + half * (D // 2) - 2 * D), D // 2)]
                        v_.tensor_tensor(cols, cols, tmp, ALU.add).then_inc(s["x2"], 1)
                        hold(dve, s["x2"], k * 4 - 4 + w + 1)
                    hold(dve, s["xnd_out"], k * 16 - 16)
                    norm(3, k - 1, xn3)
                if not isinstance(k, int):
                    assert chain["n"] == LOOP_STEPS, chain["n"]

            @peeled(dve, N // NB)
            def _(n):
                dve.wait_ge(s["sh_down"], n * 4)
                for m in range(DC):
                    dve.wait_ge(s["sh_th"], n * DC + m + 1)
                    v_.scalar_tensor_tensor(ga_sh, th_sh, 1.0, duo[m % 2][:, 0:NB], ALU.add, ALU.mult
                                            ).then_inc(s["sh_ga"], 1)
                    dve.wait_ge(s["sh_ga"], n * DC + m + 1)
                    v_.scalar_tensor_tensor(ht_sh[:, m, :], ga_sh, 0.5, duo[m % 2][:, NB:2 * NB], ALU.mult, ALU.mult
                                            ).then_inc(s["sh_h"], 1)
                for t in range(4):
                    dve.wait_ge(s["sh_down"], n * 4 + t + 1)
                    cols = res[:, bass.ds(n * (4 * D) + t * D, D)]
                    v_.tensor_tensor(cols, cols, pt[:, t % 2 * D:t % 2 * D + D], ALU.add).then_inc(s["res_final"], 1)

            def weigh_out(i, r):
                dve.wait_ge(s["down_done"], i * EU + r + 1)
                if isinstance(i, int) and i * EU + r < 2:
                    pass
                else:
                    dve.wait_ge(y_out, i * (EU * 16) + (r - 1) * 16)
                v_.tensor_scalar(ye[r % 2], quad[2 + r % 2], iw[r % EU][:, 1:2].bitcast(F32), None, ALU.mult
                                 ).then_inc(s["y_ready"], 1)

            @expert_rounds(dve)
            def _(i, first, last):
                for r in range(EU):
                    dve.wait_ge(s["th_done"], i * EU + r + 1)
                    if not first or r >= 2:
                        dve.wait_ge(s["ht_t"], i * EU + r - 1)
                    v_.scalar_tensor_tensor(th_e[r % 2], th_e[r % 2], 1.0, quad[r % 2][:, 0:F], ALU.add, ALU.mult
                                            ).then_inc(s["ga_done"], 1)
                    dve.wait_ge(s["ga_done"], i * EU + r + 1)
                    v_.scalar_tensor_tensor(he[r % 2], th_e[r % 2], 0.5, quad[r % 2][:, F:2 * F], ALU.mult,
                                            ALU.mult).then_inc(s["h_done"], 1)
                    if not first or r > 0:
                        weigh_out(i, r - 1)
                if last:
                    weigh_out(i, EU - 1)

        @block.tensor
        def _(pe):
            mm, tr = nc.tensor.matmul, nc.tensor.transpose

            def transpose_norm(src, signal):
                for t in range(2):
                    for c in range(DC):
                        op = tr(pt[:, c * S + t * P:c * S + t * P + P], src[:, t * D + c * P:t * D + c * P + P],
                                ident[:])
                op.then_inc(s[signal], 1)

            pe.wait_ge(s["const_ready"], 1)

            @pipelined(pe)
            def _(k, a, x, g, n):
                if g:
                    pe.wait_ge(s["xn3"], k - 1)
                    pe.wait_ge(s["x2"], k * 4 - 4)
                    transpose_norm(xn3, "t3_t")
                if a:
                    pe.wait_ge(s["diag"], k + 1)
                    pe.wait_ge(s["at_ready"], k * KVH)
                    for t in range(2):
                        op = mm(va[:, t * P:t * P + P], ones[:], dg[:, t * P:t * P + P], start=True, stop=True)
                    op.then_inc(s["cw_t"], 1)
                if g:
                    pe.wait_ge(s["xt3_ready"], k - 1)
                if a:
                    pe.wait_ge(s["xn1"], k + 1)
                    pe.wait_ge(s["n_rem"], k)
                    transpose_norm(xn1, "x_t")
                if g:
                    if isinstance(k, int) and k == 2:
                        pe.wait_ge(s["w_in"], 4 * 16)
                    for c in range(DC):
                        op = mm(vb[0:NE, 0:S], gw_s[:, c, :], xt3[:, c, bass.ds(k * S - 2 * S, S)], start=c == 0,
                                stop=c == DC - 1)
                    op.then_inc(s["g_mm"], 1)
                if a:
                    if isinstance(k, int) and k == 0:
                        pe.wait_ge(s["w_in"], 4 * 16)
                    pe.wait_ge(s["xt_ready"], k + 1)
                    pe.wait_ge(s["cwb_ready"], k + 1)
                    for half in range(2):
                        for c in range(DC):
                            op = mm(va[:, half * S:half * S + S], wkv_s[:, c, half * P:half * P + P], xt[:, c, :],
                                    start=c == 0, stop=c == DC - 1)
                    op.then_inc(s["k_t"], 1)
                if g:
                    hold(pe, s["gl_ready"], k - 1)
                    for t in range(2):
                        op = tr(vb[:, S + t * NE:S + t * NE + NE], gl[:, t * P:t * P + P], ident[0:NE, 0:NE])
                    op.then_inc(s["g_t"], 1)

                def queries(ch):
                    if ch == 0:
                        pe.wait_ge(s["e_ready"], k * AU)
                    for c in range(DC):
                        op = mm(qa[:, ch * S:ch * S + SQ], wq_s[:, c, ch * P:ch * P + P], xt[:, c, GLOB:S],
                                start=c == 0, stop=c == DC - 1)
                    if ch == DC - 1:
                        op.then_inc(s["q_t"], 1)

                def values():
                    pe.wait_ge(s["vt_ready"], k + 1)
                    pe.wait_ge(s["k_split"], k + 1)
                    for m, t0 in enumerate((0, P, GLOB)):
                        op = tr(va[:, m * P:m * P + P], vt[:, t0:t0 + P], ident[:])
                    op.then_inc(s["v_t"], 1)

                def context():
                    pe.wait_ge(s["v_ready"], k + 1)
                    pe.wait_ge(s["ctx_in"], k * 16 + 16)
                    for t in range(2):
                        op = tr(va[:, t * P:t * P + P], ctx_s[:, t * P:t * P + P], ident[:])
                    op.then_inc(s["c_t"], 1)

                if x:
                    pe.wait_ge(s["kxs_in"], k * 96)
                    pe.wait_ge(s["qxs_in"], k * 96)
                    for v in range(XU):
                        kv, t, half = v // 4, v // 2 % 2, v % 2
                        if v >= 2:
                            pe.wait_ge(s["x_max"], k * XU - XU + v - 1)
                        for h in range(2):
                            op = mm(xbank[v % 2][:, h * S:h * S + S],
                                    qxs[0:XSPLIT_ROWS, kv * 4 + half * 2 + h, t * P:t * P + P],
                                    kxs[0:XSPLIT_ROWS, kv, :], start=True, stop=True)
                        op.then_inc(s["xs_unit"], 1)
                        if a:
                            if v in (1, 4, 7, 10):
                                queries(v // 3)
                            elif v == 14:
                                values()
                            elif v == 17:
                                context()
                    pe.wait_ge(s["x_max"], k * XU)
                    if g:
                        pe.wait_ge(s["th_ready"], k - 1)
                    for t in range(2):
                        op = tr(vb[0:XH, t * P:t * P + P], mxx[:, t * XH:t * XH + XH], ident[:])
                    op.then_inc(s["xm_t"], 1)
                else:
                    if a:
                        for ch in range(DC):
                            queries(ch)
                        values()
                        context()
                if a:
                    pe.wait_ge(s["ks_in"], k * 96 + 96)
                    pe.wait_ge(s["qs_in"], k * 48 + 48)
                    rows = SPLIT_ROWS + ALIBI_ROWS
                    for u in range(AU):
                        q, blk = u // 2, u % 2
                        if u >= 2:
                            pe.wait_ge(s["s_max"], k * AU + u - 1)
                        mm(abank[u % 2], identb[:], masks[:, blk, :], start=True, stop=False)
                        for h in range(4):
                            op = mm(abank[u % 2][:, h * P:h * P + P], qs[0:rows, q * 4 + h, blk * GLOB:blk * GLOB + P],
                                    ks[0:rows, blk, q, :], start=False, stop=h == 3)
                        op.then_inc(s["s_unit"], 1)
                    pe.wait_ge(s["s_max"], k * AU + AU)
                    tr(pt[0:H, 0:P], mx[:, 0:H], ident[:])
                    tr(pt[0:H, 256:256 + P], mx[:, H:2 * H], ident[:]).then_inc(s["m_t"], 1)

                def xkeyed(v):
                    kv, t, half = v // 4, v // 2 % 2, v % 2
                    if v >= 2:
                        pe.wait_ge(s["xe_ready"], k * XU - XU + v - 1)
                    h = kv * 4 + half * 2
                    mm(xbank[v % 2], kxs[0:XSPLIT_ROWS + SHIFT_ROWS, kv, t * P:t * P + P],
                       qxs[0:XSPLIT_ROWS + SHIFT_ROWS, h:h + 2, :], start=True, stop=True).then_inc(s["xst_unit"], 1)

                def xweigh(v):
                    kv, t, half = v // 4, v // 2 % 2, v % 2
                    pe.wait_ge(s["xe_ready"], k * XU - XU + v + 1)
                    if v >= 8 and v % 8 == 0:
                        pe.wait_ge(s["ox_ready"], k * 4 - 4 + v // 8)
                    for h in range(2):
                        at_ = (half * 2 + h) * 32
                        op = mm(vb[at_:at_ + 32, kv % 2 * S:kv % 2 * S + S], vx[:, t, kv, :],
                                ex[v % 4][:, h * S:h * S + S], start=t == 0, stop=t == 1, tile_position=(0, at_))
                    op.then_inc(s["xpv_done"], 1)

                def cross(v):
                    xkeyed(v)
                    if v >= 2:
                        xweigh(v - 2)

                def keyed(u):
                    q, blk = u // 2, u % 2
                    if u >= 2:
                        pe.wait_ge(s["e_ready"], k * AU + u - 1)
                    rows = SPLIT_ROWS + ALIBI_ROWS + SHIFT_ROWS
                    mm(abank[u % 2], identb[:], masks[:, 1 - blk, :], start=True, stop=False)
                    mm(abank[u % 2], ks[0:rows, blk, q, :], qs[0:rows, q * 4:q * 4 + 4, blk * GLOB:blk * GLOB + P],
                       start=False, stop=True).then_inc(s["st_unit"], 1)

                def weigh(q):
                    pe.wait_ge(s["e_ready"], k * AU + 2 * q + 2)
                    if q >= 1:
                        pe.wait_ge(s["at_ready"], k * KVH + q)
                    far, near = (e4[(2 * q + m) % 4].rearrange("p (h n) -> p h n", h=4) for m in range(2))
                    vals = slice(q * HD, q * HD + HD)
                    for kind in range(6):
                        for h in range(4):
                            o = va[h * HD:h * HD + HD]
                            kw = dict(start=kind == 0, stop=kind == 5, skip_group_check=True,
                                      tile_position=(0, h * HD))
                            if kind == 0:
                                op = mm(o[:, 0:GLOB], vs[:, 0, vals], ones[:, 0:GLOB], **kw)
                            elif kind == 1:
                                op = mm(o[:, 0:GLOB], vs[:, 1, vals], ones[:, 0:GLOB], **kw)
                            elif kind == 2:
                                op = mm(o[:, GLOB:GLOB + P], vs[:, 1, vals], far[:, h, :], **kw)
                            elif kind == 3:
                                op = mm(o[:, P:S], vs[:, 2, vals], near[:, h, :], **kw)
                            elif kind == 4:
                                op = mm(o[:, S + GLOB:S + GLOB + P], ones[:, 0:HD], far[:, h, :], **kw)
                            else:
                                op = mm(o[:, S + P:2 * S], ones[:, 0:HD], near[:, h, :], **kw)
                    op.then_inc(s["pv_done"], 1)

                def project(t):
                    for q in range(DC):
                        op = mm(pt[:, t * D:t * D + D], at[:, q, t * P:t * P + P], wo_s[:, q, :],
                                start=q == 0, stop=q == DC - 1)
                    if t == 1:
                        op.then_inc(s["wo_done"], 1)

                if x:
                    pe.wait_ge(s["xshift_in"], k * 32)
                    pe.wait_ge(s["vx_ready"], k)
                for j in range(AU):
                    if x:
                        cross(2 * j)
                    if a:
                        if j == 0:
                            pe.wait_ge(s["shift_in"], k * 32 + 32)
                            pe.wait_ge(s["c_rem"], k + 1)
                        keyed(j)
                    if x:
                        cross(2 * j + 1)
                    if a and j % 2 == 0 and j >= 2:
                        weigh(j // 2 - 1)
                if a:
                    weigh(3)
                if x:
                    for v in range(16, 20):
                        cross(v)
                if a:
                    pe.wait_ge(s["at_ready"], k * KVH + KVH)
                    project(0)
                if x:
                    cross(20)
                    cross(21)
                if a:
                    project(1)
                if x:
                    for v in range(22, XU):
                        cross(v)
                if a:
                    pe.wait_ge(s["xn2"], k + 1)
                    transpose_norm(xn2, "n_t")
                if x:
                    xweigh(XU - 2)
                    xweigh(XU - 1)
                if g:
                    pe.wait_ge(s["chosen"], k - 1)
                    count = xbank[0]
                    mm(count[:, 0:2 * NE], trib[:], chosen[:], start=True, stop=False, skip_group_check=True)
                    mm(count[:, NE:2 * NE], onesb[:], chosen[:, 0:NE], start=False, stop=False, skip_group_check=True)
                    mm(count[:, 2 * NE:3 * NE], onesb[:], chosen[:, 0:NE], start=False, stop=False,
                       skip_group_check=True)
                    mm(count[:, 2 * NE:3 * NE], onesb[:], chosen[:, NE:2 * NE], start=False, stop=True,
                       skip_group_check=True).then_inc(s["pos_t"], 1)
                if x:
                    pe.wait_ge(s["ox_ready"], k * 4)
                    if a:
                        pe.wait_ge(s["n_rem"], k + 1)
                    for w in range(4):
                        t, half = w // 2, w % 2
                        if w >= 2:
                            pe.wait_ge(s["x2"], k * 4 - 4 + w - 1)
                        for m in range(4):
                            kv = half * 4 + m
                            op = tr(pt[:, half * 512 + m * P:half * 512 + m * P + P],
                                    ox[:, kv * S + t * P:kv * S + t * P + P], ident[:])
                        op.then_inc(s["xo_t"], 1)

            pe.wait_ge(s["ffn_in"], 3 * 16)
            pe.wait_ge(s["slot_ready"], B)

            @peeled(pe, N // NB)
            def _(n):
                for m in range(DC):
                    pe.wait_ge(s["sh_h"], n * DC + max(m - 1, 0))
                    for half, w in enumerate((sg_s, su_s)):
                        for c in range(DC):
                            op = mm(duo[m % 2][:, half * NB:half * NB + NB], w[:, c, m * P:m * P + P],
                                    xt3[:, c, bass.ds(n * NB, NB)], start=c == 0, stop=c == DC - 1)
                    op.then_inc(s["sh_gu"], 1)
                pe.wait_ge(s["sh_h"], n * DC + DC)
                for t in range(4):
                    pe.wait_ge(s["res_final"], n * 4 + max(t - 1, 0))
                    for c in range(DC):
                        op = mm(pt[:, t % 2 * D:t % 2 * D + D], ht_sh[:, c, t * P:t * P + P], sd_s[:, c, :],
                                start=c == 0, stop=c == DC - 1)
                    op.then_inc(s["sh_down"], 1)

            def bring(i, r):
                pe.wait_ge(xg_in[r % 2], i * (EU // 2 * 16) + r // 2 * 16 + 16)
                if not (isinstance(i, int) and i * EU + r < 2):
                    pe.wait_ge(s["xe_tr"], i * EU + r - 1)
                for c in range(DC):
                    op = tr(pt[:, r % 2 * 512 + c * P:r % 2 * 512 + c * P + P],
                            xg[r % 2].rearrange("p (n c) -> p c n", c=DC)[:, c, :], ident[:])
                op.then_inc(s["xe_t"], 1)

            def down(i, r):
                pe.wait_ge(s["ht_ready"], i * EU + r + 1)
                if not (isinstance(i, int) and i * EU + r < 2):
                    pe.wait_ge(s["y_ready"], i * EU + r - 1)
                for c in range(2):
                    op = mm(quad[2 + r % 2], hte[r % 2][:, c, :], h2[r % EU][:, c, :], start=c == 0, stop=c == 1)
                op.then_inc(s["down_done"], 1)

            pe.wait_ge(s["res_final"], N // NB * 4)
            bring(0, 0)

            @expert_rounds(pe)
            def _(i, first, last):
                for r in range(EU):
                    pe.wait_ge(wg_in[r], i * 48 + 48)
                    pe.wait_ge(s["xe_tr"], i * EU + r + 1)
                    if not first or r >= 2:
                        pe.wait_ge(s["h_done"], i * EU + r - 1)
                    for c in range(DC):
                        op = mm(quad[r % 2], xgt[r % 2][:, c, :], h13[r][:, c, :], start=c == 0, stop=c == DC - 1)
                    op.then_inc(s["up_done"], 1)
                    if not last or r + 1 < EU:
                        bring(i, r + 1)
                    if not first or r > 0:
                        down(i, r - 1)
                    pe.wait_ge(s["h_done"], i * EU + r + 1)
                    if not first or r >= 2:
                        pe.wait_ge(s["ht_ready"], i * EU + r - 1)
                    for c in range(2):
                        op = tr(pv[r % 2][:, c * P:c * P + P], he[r % 2].rearrange("p (n c) -> p c n", c=2)[:, c, :],
                                ident[:])
                    op.then_inc(s["ht_t"], 1)
                if last:
                    down(i, EU - 1)


_INS = ["x", "ctx_512", "L0_attn_Wq", "L0_attn_Wkv", "L0_attn_Wo", "L0_attn_bo", "L0_ffn_gate_w", "L0_ffn_gate_bias",
        "L0_ffn_w1", "L0_ffn_w2", "L0_ffn_w3", "L0_ffn_shared_gate", "L0_ffn_shared_up", "L0_ffn_shared_down"]


def kernel(**inputs):
    import numpy as _np
    import concourse.bacc as _bacc
    from concourse import mybir as _mybir
    from concourse.bass_utils import run_bass_kernel_spmd as _run

    nc = _bacc.Bacc("TRN2", target_bir_lowering=False, num_devices=1)
    arrays, args = {}, []
    given = {n: _np.asarray(inputs[n]) for n in _INS}
    given["L0_ffn_gate_w"] = given["L0_ffn_gate_w"].T
    given.update(constants())
    for name, a in given.items():
        a = _np.ascontiguousarray(a)
        arrays[f"in_{name}"] = a
        args.append(nc.dram_tensor(f"in_{name}", a.shape, _mybir.dt.from_np(a.dtype), kind="ExternalInput").ap())
    o = nc.dram_tensor("out_0", (B, S, D), _mybir.dt.float32, kind="ExternalOutput").ap()
    build(nc, *args, o)
    r = _run(nc, [arrays], core_ids=[0])
    return r.results[0]["out_0"]
```

```python
import numpy as np
import concourse.bass as bass
from concourse import mybir
from contextlib import ExitStack

F32 = mybir.dt.float32
F32R = mybir.dt.float32r
BF16 = mybir.dt.bfloat16
U32 = mybir.dt.uint32
ALU = mybir.AluOpType
ACT = mybir.ActivationFunctionType
AX = mybir.AxisListType

P = 128
B, S, D = 8, 256, 512
N = B * S
NT = N // P
DC = D // P
H, KVH, HD = 16, 4, 32
REP = H // KVH
GLOB = 64
SQ = S - GLOB
XH, XKV, XD = 32, 8, 16
XREP = XH // XKV
NE, TOPK, F, CAP = 32, 4, 256, 128
GRP = 4
EPG = NE // GRP
EPS = 1e-5
NEG = -1e30
SPLIT_ROWS = 3 * HD
ALIBI_ROWS = 4
SHIFT_ROWS = 2
XSPLIT_ROWS = 6 * XD
EU = 4
NB = 512
ABSENT = 65535
LOOP_STEPS = 53


def _round_bits(a, bits):
    a = np.asarray(a, np.float64)
    m, e = np.frexp(a)
    return np.ldexp(np.rint(m * 2.0 ** bits) / 2.0 ** bits, e).astype(np.float32)


def constants():
    p = np.arange(P)
    upper = np.where(p[None, :] > p[:, None], 0.0, NEG).astype(np.float32)
    masks = np.stack([np.tile(upper, (1, 4)), np.tile(upper.T, (1, 4))], 1)
    tri = (p[:, None] < p[None, :]).astype(np.float32)
    mats = np.concatenate([np.eye(P, dtype=np.float32), tri], 1)
    slope = ((2.0 ** -0.5) ** np.arange(1, H + 1)).astype(np.float32)
    i = np.arange(GLOB, S).astype(np.float32)
    lift = slope[:, None] * i[None, :]
    s_hi = _round_bits(slope, 12)
    l_hi = _round_bits(lift, 12)
    wide = np.ones((1, SQ), np.float32)
    q_rows = np.stack([-s_hi[:, None] * wide, -(slope - s_hi)[:, None] * wide, l_hi, lift - l_hi])
    k_rows = np.ones((SHIFT_ROWS + ALIBI_ROWS, 2, KVH, P), np.float32)
    far, near = np.arange(P, S), np.arange(GLOB, GLOB + P)
    k_rows[0:2, 0] = far
    k_rows[0:2, 1] = -near.astype(np.float32)
    k_rows[2:4, 1] = -1.0
    first = (np.arange(GRP)[None, :] < np.arange(GRP)[:, None]).astype(np.float32).reshape(-1)
    iota = np.tile(np.arange(NE, dtype=np.float32), (P, 1))
    small = np.concatenate([np.tile(first, (P, 1)), iota], 1)
    token = (np.arange(NT)[None, :] * P + p[:, None]).astype(np.uint32)
    slots = np.zeros((NE * CAP, 2), np.uint32)
    slots[:, 0] = ABSENT
    return {"c_masks": masks, "c_mats": mats, "c_qrows": q_rows.astype(np.float32), "c_krows": k_rows,
            "c_small": small, "c_token": token, "c_slots": slots}


def build(nc, x, ctx, wq, wkv, wo, bo, gw, gb, w1, w2, w3, sg, su, sd,
          c_masks, c_mats, c_qrows, c_krows, c_small, c_token, c_slots, out):
    st = ExitStack()

    def sb(name, shape, dt=F32):
        return st.enter_context(nc.sbuf_tensor(name, shape, dt))

    def ps(name, cols):
        return st.enter_context(nc.psum_tensor(name, [P, cols], F32))

    def sem(name):
        return st.enter_context(nc.semaphore(name))

    def dram(name, shape, dt=F32):
        return nc.dram_tensor(name, shape, dt, kind="Internal").ap()

    with st:
        kd = dram("kd", [2, P, S])
        qd = dram("qd", [2, D, SQ])
        kxd = dram("kxd", [3, P, S], BF16)
        qxd = dram("qxd", [3, D, S], BF16)
        xnd = dram("xnd", [N, D])
        slot_table = dram("slot_table", [NE * CAP, 2], U32)

        res = sb("res", [P, NT * D])
        gw_s = sb("gw_s", [P, DC, NE])
        ident = sb("ident", [P, P])
        identb = sb("identb", [P, P], BF16)
        trib = sb("trib", [P, P], BF16)
        onesb = sb("onesb", [P, P], BF16)
        ones = sb("ones", [P, P])
        masks = sb("masks", [P, 2, 4 * P], BF16)
        small = sb("small", [P, GRP * GRP + NE])
        first = small[:, 0:GRP * GRP].rearrange("p (a b) -> p a b", a=GRP)
        iota = small[:, GRP * GRP:]
        token = sb("token", [P, NT], U32)
        gb_s = sb("gb_s", [P, NE])
        bo_s = sb("bo_s", [P, D])

        qs = sb("qs", [P, H, SQ], F32R)
        ks = sb("ks", [P, 2, KVH, P], F32R)

        ARENA = 27 * 1024
        arena = sb("arena", [P, ARENA + DC * N])
        xt3 = arena[:, ARENA:].rearrange("p (b c n) -> p b c n", b=B, c=DC)
        EARLY = NE // 2
        fetched = arena[:, ARENA - EARLY * D:]
        top = [0]

        def place(cols, dt=F32):
            a = arena[:, top[0]:top[0] + cols]
            top[0] += cols
            assert top[0] <= ARENA, top[0]
            if dt is not F32:
                a = a.bitcast(dt)
            return a

        wq_s = place(DC * D).rearrange("p (c n) -> p c n", c=DC)
        wkv_s = place(DC * 2 * P).rearrange("p (c n) -> p c n", c=DC)
        wo_s = place(DC * D).rearrange("p (c n) -> p c n", c=DC)
        xn1, xn2, xn3 = place(2 * D), place(2 * D), place(2 * D)
        xt_at = top[0]
        xt = place(DC * S).rearrange("p (c n) -> p c n", c=DC)
        ctx_at = top[0]
        ctx_s = place(2 * P)
        cwb = place(S)
        dg = place(2 * P)
        kh, kl = place(S, dt=F32R), place(S, dt=F32R)
        vt = place(S)
        vs = place(3 * P).rearrange("p (s n) -> p s n", s=3)
        at = place(DC * S).rearrange("p (c n) -> p c n", c=DC)
        place(P)
        ox_at = top[0]
        qf = place(DC * SQ).rearrange("p (c n) -> p c n", c=DC)
        qh = place(DC * SQ, dt=F32R).rearrange("p (c n) -> p c n", c=DC)
        ql = place(DC * SQ, dt=F32R).rearrange("p (c n) -> p c n", c=DC)
        ox = arena[:, ox_at:ox_at + XKV * S]
        xr_at = top[0]
        xr = place(DC * S)
        xp = [place(DC * S // 2, dt=BF16) for _ in range(3)]
        kr = place(S)
        kp = [place(S // 2, dt=BF16) for _ in range(3)]
        qxs = place(XH * S // 2, dt=BF16).rearrange("p (h n) -> p h n", h=XH)
        kxs = place(XKV * S // 2, dt=BF16).rearrange("p (h n) -> p h n", h=XKV)
        vx = place(2 * XKV * 2 * XD).rearrange("p (t h c) -> p t h c", t=2, h=XKV)
        ex_at = top[0]
        ex = [place(512) for _ in range(4)]
        e4 = [arena[:, a:a + 512] for a in (xt_at, xt_at + 512, xr_at, xr_at + 512)]
        tmp, junk = place(D), place(D)
        attention_top = top[0]
        nxh, nxl = sb("nxh", [XH, S], BF16), sb("nxl", [XH, S], BF16)
        nmx = sb("nmx", [H, SQ])
        nmh, nml = sb("nmh", [H, SQ], F32R), sb("nml", [H, SQ], F32R)
        stats = {n: (sb(f"bnst{n}", [P, 2, 6]), sb(f"mv{n}", [P, 2, 2]), sb(f"rstd{n}", [P, 2])) for n in (1, 2, 3)}
        shift = {n: sb(f"shift{n}", [P, 2]) for n in (1, 3)}
        power = sb("power", [P, 2])
        asum = sb("asum", [P, 2])
        mx = sb("mx", [P, 2 * H])
        mxx = sb("mxx", [P, 2 * XH])
        rd = sb("rd", [P, SQ])
        rx = sb("rx", [P, XH])
        gl = sb("gl", [NE, S])
        sc = sb("sc", [P, 2, NE])
        scb = sb("scb", [P, 2, NE])
        m8 = sb("m8", [P, 2, GRP, 8])
        gs = sb("gs", [P, 2, GRP])
        gt = sb("gt", [P, 2, GRP, GRP])
        eq = sb("eq", [P, 2, GRP, GRP])
        sel = sb("sel", [P, 2, GRP])
        v8 = sb("v8", [P, 2, 8])
        i8 = sb("i8", [P, 2, 8], U32)
        idf = sb("idf", [P, 2, TOPK])
        oh = sb("oh", [P, 2, TOPK, NE])
        ohs = sb("ohs", [P, 2, TOPK, NE])
        chosen = sb("chosen", [P, 2 * NE], BF16)
        seen = sb("seen", [P, NE])
        pos = sb("pos", [P, 2, NE])
        sck, posk, drop, slot, wgt = (sb(n, [P, 2, TOPK]) for n in ("sck", "posk", "drop", "slot", "wgt"))
        tot = sb("tot", [P, 2])
        slot_u = sb("slot_u", [P, 2 * TOPK], U32)
        sdat = sb("sdat", [P, 2 * TOPK, 2], U32)

        top[0] = 0
        sg_s = place(DC * D).rearrange("p (c n) -> p c n", c=DC)
        su_s = place(DC * D).rearrange("p (c n) -> p c n", c=DC)
        sd_s = place(DC * D).rearrange("p (c n) -> p c n", c=DC)
        h13, h2, ring_at = [], [], []
        for _ in range(EU):
            ring_at.append(top[0])
            h13.append(place(DC * 2 * F).rearrange("p (c n) -> p c n", c=DC))
            h2.append(place(2 * D).rearrange("p (c n) -> p c n", c=2))
        end = top[0]
        top[0] = ring_at[1]
        assert top[0] >= ctx_at
        h13.append(h13.pop(1))
        h2.append(h2.pop(1))
        ht_sh = place(DC * NB).rearrange("p (c n) -> p c n", c=DC)
        th_sh, ga_sh = place(NB), place(NB)
        assert top[0] <= ox_at
        assert top[0] <= end
        top[0] = 0
        xgt = [place(D).rearrange("p (c n) -> p c n", c=DC) for r in range(2)]
        xg = [place(D).rearrange("p (c n) -> p c n", c=DC) for r in range(2)]
        th_e = [place(F) for r in range(2)]
        he = [place(F) for r in range(2)]
        hte = [place(2 * P).rearrange("p (c n) -> p c n", c=2) for r in range(2)]
        ye = [place(D) for r in range(2)]
        assert top[0] <= end <= ARENA - EARLY * D
        add_ids = sb("add_ids", [P, EU], U32)
        iw = sb("iw", [P, NE * 2], U32)

        pt, qa, qx, va, vb = ps("pt", 1024), ps("qa", 1024), ps("qx", 1024), ps("va", 512), ps("vb", 512)
        abank = [qa[:, 0:512], qa[:, 512:1024]]
        xbank = [qx[:, 0:512], qx[:, 512:1024]]
        quad = abank + xbank
        duo = [qa, qx]
        pv = [va[:, :], vb[:, :]]
        xo_bank = [va[:, :], va[:, :], pt[:, :]]

        names = """const_in const_moved const_ready clear x_in w_in ffn_in gate_up_in ctx_in
            ln1_stats ln2_stats ln3_stats ln1_rstd ln2_rstd ln3_rstd ln1_shift ln3_shift xn1 xn2 xn3 abs_sum diag x_t xt_ready cw_t
            cwb_ready k_t k_split vt_ready v_t v_ready q_t q_scaled q_hi q_split
            bo_added kd_out ks_in qd_out qs_in s_unit s_max m_t m_rows shift_in st_unit e_ready pv_done at_ready
            wo_done c_t c_hi c_rem c_mid c_split vx_ready kxd_out kxs_in n_t n_rem n_split
            qxd_out qxs_in xs_unit x_max xm_t x_rows xshift_in xst_unit xe_ready xpv_done ox_ready xo_t x2
            xnd_out t3_t xt3_ready g_mm gl_ready g_t th_ready chosen dve xg_ready iw_in fetch_in add_ids
            pos_t slot_ready sdat_ready init_out sc_out
            sh_gu sh_th sh_ga sh_h sh_down res_final base_out
            xe_t xe_tr up_done th_done ga_done h_done ht_t ht_ready down_done y_ready""".split()
        s = {n: sem(n) for n in names}
        wg_in = [sem(f"wg_in{r}") for r in range(EU)]
        y_out = sem("y_out")
        block = st.enter_context(nc.Block())

        def tile(b, t, n=1):
            return res[:, bass.ds(b * (2 * D) + t * D, n * D)]

        def peeled(engine, count):
            def run(body):
                body(0)
                with engine.Fori(1, count) as i:
                    body(i)
            return run

        def pipelined(engine):
            def run(body):
                body(0, a=True, x=False, g=False, n=True)
                body(1, a=True, x=True, g=False, n=True)
                body(2, a=True, x=True, g=True, n=True)
                with engine.Fori(3, B - 1) as k:
                    body(k, a=True, x=True, g=True, n=True)
                body(B - 1, a=True, x=True, g=True, n=False)
                body(B, a=False, x=True, g=True, n=False)
                body(B + 1, a=False, x=False, g=True, n=False)
            return run

        def expert_rounds(engine):
            def run(body):
                body(0, True, False)
                with engine.Fori(1, NE // EU - 1) as i:
                    body(i, False, False)
                body(NE // EU - 1, False, True)
            return run

        wait_register = {}

        def hold(engine, semaphore, count):
            if isinstance(count, int):
                engine.wait_ge(semaphore, count)
                return
            if engine.engine not in wait_register:
                wait_register[engine.engine] = engine.alloc_register("wait_count")
            engine.reg_mov(wait_register[engine.engine], count)
            engine.wait_ge(s["const_ready"], 1)
            engine.wait_ge(semaphore, wait_register[engine.engine])

        AT_QUERY = (-1, -1, -1, 1)
        AT_CONTEXT, AT_THIRD, AT_LOGITS = 7, 11, 14
        AT_SELF = (23, 25, 27, 29, 30, 31)
        LEAD = 5
        AT_OUT, AT_NORM, AT_FIRST = 19, 23, 28
        XU = 32
        AU = 8

        @block.sync
        def _(sp):
            def go(dst, src, signal):
                sp.dma_start(dst, src).then_inc(s[signal], 16)

            rows, tiles = x.rearrange("b (u p) d -> p (b u) d", p=P), res[:, :].rearrange("p (t d) -> p t d", t=NT)
            go(tiles[:, 0:2], rows[:, 0:2], "x_in")
            go(xn3[:, 0:2 * P], c_mats, "const_in")
            go(xr[:, 0:1024].rearrange("p (a n) -> p a n", a=2), c_masks, "const_in")
            go(small[:], c_small, "const_in")
            go(token[:], c_token, "const_in")
            go(gb_s[:], gb.rearrange("(o n) -> o n", o=1).broadcast_to([P, NE]), "const_in")
            go(bo_s[:], bo.rearrange("(o n) -> o n", o=1).broadcast_to([P, D]), "const_in")
            go(arena[96:102, ex_at:ex_at + 2 * KVH * P].rearrange("p (a h n) -> p a h n", a=2, h=KVH), c_krows,
               "const_in")
            go(arena[96:100, 0:H * SQ].rearrange("p (h n) -> p h n", h=H), c_qrows, "const_in")
            sp.wait_ge(s["const_moved"], 1)
            for dst, src in ((wkv_s, wkv), (wq_s, wq), (wo_s, wo), (gw_s[:], gw)):
                go(dst, src.rearrange("(c p) n -> p c n", p=P), "w_in")
            for u in range(2, NT, 2):
                go(tiles[:, u:u + 2], rows[:, u:u + 2], "x_in")
            go(slot_table, c_slots, "init_out")

            @pipelined(sp)
            def _(k, a, x, g, n):
                if a:
                    hold(sp, s["c_t"], k)
                    hold(sp, s["vx_ready"], k)
                    go(ctx_s.rearrange("p (t n) -> p t n", t=2),
                       ctx[bass.ds(k, 1)].rearrange("o (t p) n -> p (o t) n", p=P), "ctx_in")
                    hold(sp, s["k_split"], k + 1)
                    go(kd[0], kh.bitcast(F32), "kd_out")
                    go(kd[1], kl.bitcast(F32), "kd_out")
                    hold(sp, s["kd_out"], k * 32 + 32)
                    for m, part in enumerate((0, 1, 0)):
                        for blk, j0 in enumerate((P, GLOB)):
                            go(ks[m * HD:m * HD + HD, blk].bitcast(F32),
                               kd[part].rearrange("(g d) t -> d g t", d=HD)[:, :, j0:j0 + P], "ks_in")
                    hold(sp, s["q_split"], k + 1)
                    go(qd[0].rearrange("(c p) t -> p c t", p=P), qh.bitcast(F32), "qd_out")
                    go(qd[1].rearrange("(c p) t -> p c t", p=P), ql.bitcast(F32), "qd_out")
                    hold(sp, s["qd_out"], k * 32 + 32)
                    for m, part in enumerate((0, 0, 1)):
                        go(qs[m * HD:m * HD + HD].bitcast(F32), qd[part].rearrange("(h d) t -> d h t", d=HD), "qs_in")
                    if not n:
                        sp.wait_ge(s["q_t"], B)
                        go(sg_s, sg.rearrange("(c p) n -> p c n", p=P), "gate_up_in")
                    hold(sp, s["c_split"], k + 1)
                    hold(sp, s["kxs_in"], k * 96)
                    for m in range(3):
                        go(kxd[m], kp[m], "kxd_out")
                if g:
                    hold(sp, s["xn3"], k - 1)
                    go(xnd[bass.ds(k * S - 2 * S, S)].rearrange("(t p) d -> p t d", p=P),
                       xn3.rearrange("p (t d) -> p t d", t=2), "xnd_out")
                if x:
                    hold(sp, s["x_rows"], k)
                    go(qxs[96:97], nxh[:], "xshift_in")
                    go(qxs[97:98], nxl[:], "xshift_in")
                if a:
                    hold(sp, s["m_rows"], k + 1)
                    go(qs[100:101].bitcast(F32), nmh[:].bitcast(F32), "shift_in")
                    go(qs[101:102].bitcast(F32), nml[:].bitcast(F32), "shift_in")
                    if not n:
                        sp.wait_ge(s["wo_done"], B * 2)
                        go(su_s, su.rearrange("(c p) n -> p c n", p=P), "gate_up_in")
                    hold(sp, s["n_split"], k + 1)
                    hold(sp, s["qxs_in"], k * 96)
                    for m in range(3):
                        go(qxd[m].rearrange("(c p) t -> p c t", p=P), xp[m].rearrange("p (c t) -> p c t", c=DC),
                           "qxd_out")
                    hold(sp, s["kxd_out"], k * 48 + 48)
                    hold(sp, s["qxd_out"], k * 48 + 48)
                    hold(sp, s["xst_unit"], k * XU)
                    for m, part in enumerate((0, 1, 0, 1, 2, 0)):
                        go(kxs[m * XD:m * XD + XD], kxd[part].rearrange("(g d) t -> d g t", d=XD), "kxs_in")
                    for m, part in enumerate((0, 0, 1, 1, 0, 2)):
                        go(qxs[m * XD:m * XD + XD], qxd[part].rearrange("(h d) t -> d h t", d=XD), "qxs_in")

            go(sd_s, sd.rearrange("(c p) n -> p c n", p=P), "ffn_in")
            sp.wait_ge(s["t3_t"], B)
            sp.wait_ge(s["xnd_out"], B * 16)

            @peeled(sp, NE // EU)
            def _(i):
                for r in range(EU):
                    if not isinstance(i, int):
                        hold(sp, s["down_done"], i * EU + (r + 1 - EU))
                    elif r == EU - 1:
                        sp.wait_ge(s["res_final"], N // NB * 4)
                    e = i * EU + r
                    w13 = h13[r].rearrange("p c (a f) -> p c a f", a=2)
                    sp.dma_start(w13[:, :, 0], w1[bass.ds(e, 1)].rearrange("o (p c) f -> p (o c) f", c=DC)
                                 ).then_inc(wg_in[r], 16)
                    sp.dma_start(w13[:, :, 1], w3[bass.ds(e, 1)].rearrange("o (p c) f -> p (o c) f", c=DC)
                                 ).then_inc(wg_in[r], 16)
                    sp.dma_start(h2[r], w2[bass.ds(e, 1)].rearrange("o (p c) d -> p (o c) d", c=2)
                                 ).then_inc(wg_in[r], 16)

        @block.gpsimd
        def _(pool):
            def norm_scale(n, count):
                pool.wait_ge(s[f"ln{n}_stats"], count)
                nc.gpsimd.tensor_tensor(stats[n][2][:], stats[n][1][:, :, 1], power[:], ALU.pow
                                        ).then_inc(s[f"ln{n}_rstd"], 1)

            def norm_shift(n, count):
                hold(pool, s[f"ln{n}_rstd"], count)
                nc.gpsimd.tensor_tensor(shift[n][:], shift[n][:], stats[n][2][:], ALU.mult
                                        ).then_inc(s[f"ln{n}_shift"], 1)

            nc.gpsimd.memset(ones[:], 1.0)
            nc.gpsimd.memset(onesb[:], 1.0)
            nc.gpsimd.memset(seen[:], 0.0)
            nc.gpsimd.memset(vx, 1.0)
            nc.gpsimd.memset(arena[:, attention_top:ARENA], 0.0).then_inc(s["clear"], 1)
            for n, (place_, value) in enumerate(((qxs[96:P], 0.0), (kxs[96:P], 0.0), (kxs[96:98], 1.0))):
                pool.wait_ge(s["clear"], n + 1)
                nc.gpsimd.memset(place_, value).then_inc(s["clear"], 1)
            pool.wait_ge(s["clear"], 4)
            pool.wait_ge(s["const_moved"], 1)
            nc.gpsimd.memset(power[:], -0.5).then_inc(s["const_ready"], 1)
            pool.wait_ge(s["const_ready"], 1)
            norm_scale(1, 1)
            norm_shift(1, 1)

            @pipelined(pool)
            def _(k, a, x, g, n):
                if a:
                    pool.wait_ge(s["xn1"], k + 1)
                    for t in range(2):
                        op = nc.gpsimd.tensor_tensor(tile(k, t), tile(k, t), bo_s[:], ALU.add)
                    op.then_inc(s["bo_added"], 1)
                if n:
                    norm_scale(1, k + 2)
                    norm_shift(1, k + 2)
                if a:
                    norm_scale(2, k + 1)
                if x:
                    norm_scale(3, k)
                    norm_shift(3, k)
                if g:
                    pool.wait_ge(s["slot_ready"], k - 1)
                    if isinstance(k, int) and k == 2:
                        pool.wait_ge(s["init_out"], 16)
                    nc.gpsimd.tensor_copy(sdat[:, :, 0].rearrange("p (t k) -> p t k", t=2),
                                          token[:, bass.ds(k * 2 - 4, 2)].unsqueeze(2).broadcast_to([P, 2, TOPK])
                                          ).then_inc(s["sdat_ready"], 1)
                    hold(pool, s["sdat_ready"], k - 1)
                    for c in range(2 * TOPK):
                        nc.gpsimd.indirect_dma_start(
                            slot_table, bass.IndirectOffsetOnAxis(ap=slot_u[:, c:c + 1], axis=0), sdat[:, c, :], None,
                            bounds_check=NE * CAP - 1, oob_is_err=False).then_inc(s["sc_out"], 16)

            pool.wait_ge(s["sc_out"], B * 2 * TOPK * 16)
            pool.wait_ge(s["xnd_out"], B * 16)

            pool.wait_ge(s["ks_in"], B * 96)
            pool.wait_ge(s["x2"], B * 3)
            pool.wait_ge(s["slot_ready"], B)
            pool.dma_start(iw[:].rearrange("p (e c) -> p e c", c=2), slot_table.rearrange("(e p) c -> p e c", p=CAP)
                           ).then_inc(s["iw_in"], 16)
            pool.wait_ge(s["iw_in"], 16)

            ids = iw[:].rearrange("p (e c) -> p e c", c=2)

            def fetch(e):
                nc.gpsimd.indirect_dma_start(
                    fetched[:, e * D:e * D + D], None, xnd, bass.IndirectOffsetOnAxis(ap=iw[:, e * 2:e * 2 + 1], axis=0),
                    bounds_check=N - 1, oob_is_err=False).then_inc(s["fetch_in"], 16)

            for e in range(EARLY):
                fetch(e)
            for n in range(N // NB):
                pool.wait_ge(s["sh_gu"], n * DC + DC)
                for r in range(EU):
                    fetch(EARLY + n * EU + r)
                pool.wait_ge(s["res_final"], n * 4 + 4)
                pool.dma_start(out.rearrange("b (u p) d -> p (b u) d", p=P)[:, n * 4:n * 4 + 4],
                               res[:, n * 4 * D:n * 4 * D + 4 * D].rearrange("p (t d) -> p t d", t=4)
                               ).then_inc(s["base_out"], 16)
            pool.wait_ge(s["base_out"], N // NB * 16)
            flat = out.rearrange("b s d -> (b s) d")

            @expert_rounds(pool)
            def _(i, first, last):
                hold(pool, y_out, i * (EU * 16))
                nc.gpsimd.tensor_copy(add_ids[:], ids[:, bass.ds(i * EU, EU), 0]).then_inc(s["add_ids"], 1)
                hold(pool, s["add_ids"], i + 1)
                for r in range(EU):
                    hold(pool, s["y_ready"], i * EU + r + 1)
                    if r > 0:
                        hold(pool, y_out, i * (EU * 16) + r * 16)
                    nc.gpsimd.indirect_dma_start(
                        flat, bass.IndirectOffsetOnAxis(ap=add_ids[:, r:r + 1], axis=0), ye[r % 2], None,
                        bounds_check=N - 1, oob_is_err=False, compute_op=ALU.add).then_inc(y_out, 16)
            pool.wait_ge(y_out, NE * 16)

        @block.scalar
        def _(act):
            def copy(dst, src, signal, func=ACT.Copy, **kw):
                nc.scalar.activation(dst, src, func, **kw).then_inc(s[signal], 1)

            def norm_apply(n, b, dst):
                act.wait_ge(s[f"ln{n}_shift"], b + 1)
                for t in range(2):
                    op = nc.scalar.activation(dst[:, t * D:t * D + D], tile(b, t), ACT.Identity,
                                              bias=shift[n][:, t:t + 1], scale=stats[n][2][:, t:t + 1])
                op.then_inc(s[f"xn{n}"], 1)

            def token_sums(b, part=None):
                for p in range(3) if part is None else [part]:
                    if p == 0:
                        act.wait_ge(s["xn1"], b + 1)
                    if p < 2:
                        copy(junk, xn1[:, p * D:p * D + D], "abs_sum", ACT.Abs, accum_out=asum[:, p:p + 1])
                        act.wait_ge(s["abs_sum"], b * 3 + p + 1)
                    else:
                        copy(asum[:], asum[:], "abs_sum", ACT.Exp, scale=-1.0)

            act.wait_ge(s["const_in"], 8 * 16)
            nc.scalar.activation(ident[:], xn3[:, 0:P], ACT.Copy)
            nc.scalar.activation(identb[:], xn3[:, 0:P], ACT.Copy)
            nc.scalar.activation(trib[:], xn3[:, P:2 * P], ACT.Copy)
            nc.scalar.activation(masks[:], xr[:, 0:1024].rearrange("p (a n) -> p a n", a=2), ACT.Copy)
            nc.scalar.activation(ks[96:102], arena[96:102, ex_at:ex_at + 2 * KVH * P].rearrange(
                "p (a h n) -> p a h n", a=2, h=KVH), ACT.Copy)
            nc.scalar.activation(qs[96:100], arena[96:100, 0:H * SQ].rearrange("p (h n) -> p h n", h=H), ACT.Copy
                                 ).then_inc(s["const_moved"], 1)
            act.wait_ge(s["const_ready"], 1)
            norm_apply(1, 0, xn1)
            token_sums(0)
            act.wait_ge(s["x_t"], 1)
            copy(xt, qa[:].rearrange("p (c n) -> p c n", c=DC), "xt_ready")

            def shared_tanh(n, m, bank):
                act.wait_ge(s["sh_gu"], n * DC + m + 1)
                act.wait_ge(s["sh_h"], n * DC + m)
                copy(th_sh, bank[:, 0:NB], "sh_th", ACT.Tanh, scale=0.5)

            @pipelined(act)
            def _(k, a, x, g, n):
                if a:
                    act.wait_ge(s["cw_t"], k + 1)
                    copy(cwb, qa[:, 0:S], "cwb_ready", scale=float(HD) ** -0.5)
                    act.wait_ge(s["k_t"], k + 1)
                    act.wait_ge(s["kd_out"], k * 32)
                    nc.scalar.activation(kh, va[:, 0:S], ACT.Copy)
                    copy(vt, va[:, S:2 * S], "vt_ready")
                    act.wait_ge(s["q_scaled"], k + 1)
                    copy(qh, qf, "q_hi")
                if g:
                    if not (isinstance(k, int) and k == 2):
                        act.wait_ge(s["xnd_out"], k * 16 - 32)
                    norm_apply(3, k - 2, xn3)
                if a:
                    act.wait_ge(s["v_t"], k + 1)
                    copy(vs, va[:, 0:3 * P].rearrange("p (s n) -> p s n", s=3), "v_ready")
                    act.wait_ge(s["c_t"], k + 1)
                    copy(kp[0], va[:, 0:S], "c_hi")
                    act.wait_ge(s["c_rem"], k + 1)
                    copy(kp[1], kr, "c_mid")
                if g:
                    act.wait_ge(s["t3_t"], k - 1)
                    copy(xt3[:, bass.ds(k - 2, 1)].rearrange("p o c n -> p (o c n)"), pt[:], "xt3_ready")
                    act.wait_ge(s["g_mm"], k - 1)
                    copy(gl[:], vb[0:NE, 0:S], "gl_ready")
                    act.wait_ge(s["g_t"], k - 1)
                    copy(sc[:], vb[:, S:S + 2 * NE].rearrange("p (t e) -> p t e", t=2), "th_ready", ACT.Tanh,
                         scale=0.5)
                if not a:
                    if x:
                        shared_tanh(0, 0, qa)
                        shared_tanh(0, 1, qa)
                    else:
                        shared_tanh(0, 3, qa)

                def cross(v):
                    act.wait_ge(s["xst_unit"], k * XU - XU + v + 1)
                    if v >= 4:
                        act.wait_ge(s["xpv_done"], k * XU - XU + v - 3)
                    copy(ex[v % 4], xbank[v % 2], "xe_ready", ACT.Exp, scale=float(XD) ** -0.5)
                    if v % 8 == 1 and v > 8:
                        pair_out(v // 8 - 1)

                def pair_out(pair):
                    act.wait_ge(s["xpv_done"], k * XU - XU + pair * 8 + 8)
                    copy(ox[:, pair * 512:pair * 512 + 512], vb[:, :], "ox_ready")

                def tokens_out():
                    act.wait_ge(s["x_t"], k + 2)
                    copy(xt, qa[:].rearrange("p (c n) -> p c n", c=DC), "xt_ready")

                if x:
                    for v in range(LEAD):
                        cross(v)
                for j in range(AU):
                    if a:
                        act.wait_ge(s["st_unit"], k * AU + j + 1)
                        if j >= 4:
                            act.wait_ge(s["pv_done"], k * KVH + (j - 4) // 2 + 1)
                        copy(e4[j % 4], abank[j % 2], "e_ready", ACT.Exp)
                    if x:
                        cross(LEAD + j)
                if n and not x:
                    norm_apply(1, k + 1, xn1)
                    token_sums(k + 1)
                if x:
                    for v in range(LEAD + AU, XU):
                        cross(v)
                        if n and v == 15:
                            norm_apply(1, k + 1, xn1)
                        if n and v == 16:
                            token_sums(k + 1, 0)
                            token_sums(k + 1, 1)
                        if n and v == 18:
                            token_sums(k + 1, 2)
                        if n and v == AT_FIRST:
                            tokens_out()
                    pair_out(3)
                    if not a:
                        shared_tanh(0, 2, qa)
                elif n:
                    tokens_out()
                if a:
                    act.wait_ge(s["ctx_in"], k * 16 + 16)
                    copy(vx[:, :, :, 0:XD], ctx_s.rearrange("p (t h c) -> p t h c", t=2, h=XKV), "vx_ready")

            @peeled(act, N // NB)
            def _(n):
                if not isinstance(n, int):
                    for m in range(DC):
                        shared_tanh(n, m, duo[m % 2])

            def tokens_out(i, r):
                act.wait_ge(s["xe_t"], i * EU + r + 1)
                copy(xgt[r % 2], pt[:, r % 2 * 512:r % 2 * 512 + 512].rearrange("p (c n) -> p c n", c=DC), "xe_tr")

            def tokens_in(i, r):
                if not (isinstance(i, int) and i * EU + r < 2):
                    act.wait_ge(s["xe_t"], i * EU + r - 1)
                copy(xg[r % 2], fetched[:, bass.ds((i * EU + r) * D, D)].rearrange("p (n c) -> p c n", c=DC),
                     "xg_ready")

            act.wait_ge(s["fetch_in"], NE * 16)
            tokens_in(0, 0)
            tokens_in(0, 1)
            tokens_out(0, 0)

            @expert_rounds(act)
            def _(i, first, last):
                for r in range(EU):
                    act.wait_ge(s["up_done"], i * EU + r + 1)
                    if not first or r >= 2:
                        act.wait_ge(s["h_done"], i * EU + r - 1)
                    copy(th_e[r % 2], quad[r % 2][:, 0:F], "th_done", ACT.Tanh, scale=0.5)
                    if not last or r + 1 < EU:
                        tokens_out(i, r + 1)
                    if not last or r + 2 < EU:
                        tokens_in(i, r + 2)
                    act.wait_ge(s["ht_t"], i * EU + r + 1)
                    if not first or r >= 2:
                        act.wait_ge(s["down_done"], i * EU + r - 1)
                    copy(hte[r % 2], pv[r % 2][:, 0:2 * P].rearrange("p (c n) -> p c n", c=2), "ht_ready")

        @block.vector
        def _(dve):
            v_ = nc.vector
            chain = {"base": 0, "n": 0}

            def link(ins):
                chain["n"] += 1
                ins.then_inc(s["dve"], 1)
                hold(dve, s["dve"], chain["base"] + chain["n"])

            def norm_tile(n, b, t):
                return v_.bn_stats(stats[n][0][:, t, :], tile(b, t))

            def norm_stats(n):
                bnst, mv, _ = stats[n]
                for t in range(2):
                    op = v_.bn_aggr(mv[:, t, :], bnst[:, t, :])
                link(op)
                if n != 2:
                    v_.tensor_scalar(shift[n][:], mv[:, :, 0], -1.0, None, ALU.mult)
                v_.tensor_scalar(mv[:, :, 1], mv[:, :, 1], EPS, None, ALU.add).then_inc(s[f"ln{n}_stats"], 1)

            def norm_apply(n, b, dst):
                _, mv, rstd = stats[n]
                dve.wait_ge(s[f"ln{n}_rstd"], b + 1)
                for t in range(2):
                    op = v_.tensor_scalar(dst[:, t * D:t * D + D], tile(b, t), mv[:, t, 0:1], rstd[:, t:t + 1],
                                          ALU.subtract, ALU.mult)
                op.then_inc(s[f"xn{n}"], 1)

            def token_weights(b):
                dve.wait_ge(s["abs_sum"], b * 3 + 3)
                link(v_.tensor_scalar(asum[:], asum[:], 1.0, None, ALU.add))
                link(v_.reciprocal(asum[:], asum[:]))
                for t in range(2):
                    op = v_.tensor_scalar(dg[:, t * P:t * P + P], ident[:], asum[:, t:t + 1], None, ALU.mult)
                op.then_inc(s["diag"], 1)

            def choose():
                link(v_.tensor_scalar(sc[:], sc[:], 0.5, 0.5, ALU.mult, ALU.add))
                link(v_.tensor_tensor(scb[:], sc[:], gb_s[:].unsqueeze(1).broadcast_to([P, 2, NE]), ALU.add))
                for t in range(2):
                    for q in range(GRP):
                        op = v_.max(m8[:, t, q, :], scb[:, t, q * EPG:q * EPG + EPG])
                link(op)
                link(v_.tensor_tensor(gs[:], m8[:, :, :, 0], m8[:, :, :, 1], ALU.add))
                other = gs[:].unsqueeze(2).broadcast_to([P, 2, GRP, GRP])
                own = gs[:].unsqueeze(3).broadcast_to([P, 2, GRP, GRP])
                v_.tensor_tensor(gt[:], other, own, ALU.is_gt)
                link(v_.tensor_tensor(eq[:], other, own, ALU.is_equal))
                link(v_.tensor_tensor(eq[:], eq[:], first.unsqueeze(1).broadcast_to([P, 2, GRP, GRP]), ALU.mult))
                link(v_.tensor_tensor(gt[:], gt[:], eq[:], ALU.add))
                link(v_.reduce_sum(sel[:], gt[:], AX.X))
                link(v_.tensor_scalar(sel[:], sel[:], 1.5, None, ALU.is_lt))
                by_group = scb[:].rearrange("p t (g e) -> p t g e", g=GRP)
                link(v_.tensor_tensor(by_group, by_group, sel[:].unsqueeze(3).broadcast_to([P, 2, GRP, EPG]),
                                      ALU.mult))
                for t in range(2):
                    op = v_.max(v8[:, t, :], scb[:, t, :])
                link(op)
                for t in range(2):
                    op = v_.max_index(i8[:, t, :], v8[:, t, :], scb[:, t, :])
                link(op)
                link(v_.tensor_copy(idf[:], i8[:, :, 0:TOPK]))
                link(v_.tensor_tensor(oh[:], iota.unsqueeze(1).unsqueeze(1).broadcast_to([P, 2, TOPK, NE]),
                                      idf[:].unsqueeze(3).broadcast_to([P, 2, TOPK, NE]), ALU.is_equal))
                with nc.allow_low_precision(reason="each sum is 0 or 1"):
                    v_.reduce_sum(chosen[:].rearrange("p (t e) -> p t e", t=2), oh[:].rearrange(
                        "p t k e -> p t e k"), AX.X).then_inc(s["chosen"], 1)
                link(v_.tensor_tensor(ohs[:], oh[:], sc[:].unsqueeze(2).broadcast_to([P, 2, TOPK, NE]), ALU.mult))
                link(v_.reduce_sum(sck[:], ohs[:], AX.X))
                link(v_.reduce_sum(tot[:], sck[:], AX.X))
                link(v_.tensor_scalar(tot[:], tot[:], 1e-20, None, ALU.add))
                link(v_.reciprocal(tot[:], tot[:]))
                link(v_.scalar_tensor_tensor(wgt[:], sck[:], 2.0, tot[:].unsqueeze(2).broadcast_to([P, 2, TOPK]),
                                             ALU.mult, ALU.mult))

            def take_slots(k):
                dve.wait_ge(s["pos_t"], k - 1)
                hold(dve, s["sc_out"], k * (2 * TOPK * 16) - 4 * TOPK * 16)
                count = xbank[0]
                link(v_.tensor_tensor(pos[:], count[:, 0:2 * NE].rearrange("p (t e) -> p t e", t=2),
                                      seen[:].unsqueeze(1).broadcast_to([P, 2, NE]), ALU.add))
                v_.tensor_tensor(seen[:], seen[:], count[:, 2 * NE:3 * NE], ALU.add)
                link(v_.tensor_tensor(ohs[:], oh[:], pos[:].unsqueeze(2).broadcast_to([P, 2, TOPK, NE]), ALU.mult))
                link(v_.reduce_sum(posk[:], ohs[:], AX.X))
                link(v_.tensor_scalar(drop[:], posk[:], CAP - 0.5, 1e6, ALU.is_gt, ALU.mult))
                link(v_.scalar_tensor_tensor(slot[:], idf[:], float(CAP), posk[:], ALU.mult, ALU.add))
                link(v_.tensor_tensor(slot[:], slot[:], drop[:], ALU.add))
                v_.tensor_copy(sdat[:, :, 1].bitcast(F32), wgt[:].rearrange("p t k -> p (t k)"))
                v_.tensor_copy(slot_u[:], slot[:].rearrange("p t k -> p (t k)")).then_inc(s["slot_ready"], 1)

            dve.wait_ge(s["x_in"], 16)
            dve.wait_ge(s["const_ready"], 1)
            norm_tile(1, 0, 0)
            link(norm_tile(1, 0, 1))
            norm_stats(1)
            token_weights(0)
            steps = {}

            def shared_hidden(n, m, bank):
                dve.wait_ge(s["sh_th"], n * DC + m + 1)
                v_.scalar_tensor_tensor(ga_sh, th_sh, 1.0, bank[:, 0:NB], ALU.add, ALU.mult).then_inc(s["sh_ga"], 1)
                dve.wait_ge(s["sh_ga"], n * DC + m + 1)
                v_.scalar_tensor_tensor(ht_sh[:, m, :], ga_sh, 0.5, bank[:, NB:2 * NB], ALU.mult, ALU.mult
                                        ).then_inc(s["sh_h"], 1)

            @pipelined(dve)
            def _(k, a, x, g, n):
                if isinstance(k, int):
                    if "loop" in steps:
                        chain.update(base=steps.pop("loop") + (B - 4) * LOOP_STEPS, n=0)
                    else:
                        chain.update(base=chain["base"] + chain["n"], n=0)
                else:
                    steps["loop"] = chain["base"] + chain["n"]
                    chain.update(base=k * LOOP_STEPS + (steps["loop"] - 3 * LOOP_STEPS), n=0)
                if a:
                    dve.wait_ge(s["vt_ready"], k + 1)
                    v_.tensor_tensor(kl, va[:, 0:S], kh.bitcast(F32), ALU.subtract).then_inc(s["k_split"], 1)

                def queries():
                    dve.wait_ge(s["q_t"], k + 1)
                    dve.wait_ge(s["cwb_ready"], k + 1)
                    v_.tensor_tensor(qf, qa[:].rearrange("p (c n) -> p c n", c=DC)[:, :, 0:SQ],
                                     cwb[:, GLOB:S].unsqueeze(1).broadcast_to([P, DC, SQ]), ALU.mult
                                     ).then_inc(s["q_scaled"], 1)

                def queries_low():
                    dve.wait_ge(s["q_hi"], k + 1)
                    v_.tensor_tensor(ql, qf, qh.bitcast(F32), ALU.subtract).then_inc(s["q_split"], 1)

                def context_rem():
                    dve.wait_ge(s["c_hi"], k + 1)
                    v_.tensor_tensor(kr, va[:, 0:S], kp[0], ALU.subtract).then_inc(s["c_rem"], 1)

                def context_low():
                    dve.wait_ge(s["c_mid"], k + 1)
                    v_.tensor_tensor(kp[2], kr, kp[1], ALU.subtract).then_inc(s["c_split"], 1)

                def self_max(u):
                    q, blk = u // 2, u % 2
                    dve.wait_ge(s["s_unit"], k * AU + u + 1)
                    v_.reduce_max(mx[:, blk * H + q * 4:blk * H + q * 4 + 4],
                                  abank[u % 2].rearrange("p (h n) -> p h n", h=4), AX.X).then_inc(s["s_max"], 1)

                if x:
                    for v in range(XU):
                        kv, t, half = v // 4, v // 2 % 2, v % 2
                        dve.wait_ge(s["xs_unit"], k * XU - XU + v + 1)
                        col = t * XH + kv * 4 + half * 2
                        v_.reduce_max(mxx[:, col:col + 2], xbank[v % 2].rearrange("p (h n) -> p h n", h=2), AX.X
                                      ).then_inc(s["x_max"], 1)
                        if a:
                            if v == AT_QUERY[3] + 1:
                                queries()
                            elif v == AT_QUERY[3] + 3:
                                queries_low()
                            elif v == AT_CONTEXT + 3:
                                context_rem()
                            elif v == AT_CONTEXT + 6:
                                context_low()
                            if v in AT_SELF:
                                self_max(AT_SELF.index(v))
                    if not a:
                        shared_hidden(0, 0, qa)
                    dve.wait_ge(s["xm_t"], k)
                    dve.wait_ge(s["xshift_in"], k * 32 - 32)
                    link(v_.tensor_scalar(nxh[:], vb[0:XH, 0:S], -1.0, None, ALU.mult))
                    v_.scalar_tensor_tensor(nxl[:], vb[0:XH, 0:S], -1.0, nxh[:], ALU.mult, ALU.subtract
                                            ).then_inc(s["x_rows"], 1)
                else:
                    if a:
                        queries()
                        queries_low()
                        context_rem()
                        context_low()
                if a:
                    for u in range(len(AT_SELF) if x else 0, AU):
                        self_max(u)
                    dve.wait_ge(s["m_t"], k + 1)
                    dve.wait_ge(s["shift_in"], k * 32)
                    link(v_.tensor_scalar(nmx[:, 0:P], pt[0:H, 0:P], -1.0, None, ALU.mult))
                    link(v_.scalar_tensor_tensor(nmx[:, P - GLOB:P], pt[0:H, 256:256 + GLOB], -1.0,
                                                 nmx[:, P - GLOB:P], ALU.mult, ALU.min))
                    link(v_.tensor_scalar(nmx[:, P:SQ], pt[0:H, 256 + GLOB:256 + P], -1.0, None, ALU.mult))
                    link(v_.tensor_copy(nmh[:], nmx[:]))
                    v_.tensor_tensor(nml[:], nmx[:], nmh[:].bitcast(F32), ALU.subtract).then_inc(s["m_rows"], 1)
                if g:
                    dve.wait_ge(s["th_ready"], k - 1)
                    hold(dve, s["pos_t"], k - 2)
                    choose()
                if not a:
                    shared_hidden(0, 1 if x else 3, qa)
                if a:
                    for q in range(KVH):
                        dve.wait_ge(s["pv_done"], k * KVH + q + 1)
                        link(v_.reciprocal(rd[:], va[:, S + GLOB:2 * S]))
                        v_.tensor_tensor(at[:, q, GLOB:S], va[:, GLOB:S], rd[:], ALU.mult)
                        v_.tensor_scalar(at[:, q, 0:GLOB], va[:, 0:GLOB], 1.0 / S, None, ALU.mult
                                         ).then_inc(s["at_ready"], 1)
                        if n and q == 0:
                            if isinstance(k, int) and k == 0:
                                dve.wait_ge(s["x_in"], B * 16)
                            norm_tile(1, k + 1, 0)
                        elif n and q == 1:
                            link(norm_tile(1, k + 1, 1))
                        elif n and q == 2:
                            norm_stats(1)
                    dve.wait_ge(s["bo_added"], k + 1)
                    for t in range(2):
                        dve.wait_ge(s["wo_done"], k * 2 + t + 1)
                        link(v_.tensor_tensor(tile(k, t), tile(k, t), qa[:, t * D:t * D + D], ALU.add))
                        op = norm_tile(2, k, t)
                    link(op)
                    norm_stats(2)
                    norm_apply(2, k, xn2)

                def cross_out(w):
                    tiles, half = (1, 0) if w < 2 else (2, 1)
                    dve.wait_ge(s["xo_t"], k * 3 - 3 + w + 1)
                    o = xo_bank[w].rearrange("p (h c) -> p h c", c=2 * XD)
                    heads = tiles * (XH // 2)
                    link(v_.reciprocal(rx[:, 0:heads], o[:, :, XD]))
                    link(v_.tensor_tensor(tmp[:, 0:heads * XD].rearrange("p (h c) -> p h c", c=XD), o[:, :, 0:XD],
                                          rx[:, 0:heads].unsqueeze(2).broadcast_to([P, heads, XD]), ALU.mult))
                    cols = res[:, bass.ds(k * (2 * D) + (w % 2 * D - 2 * D), tiles * D)].rearrange(
                        "p (t d) -> p t d", d=D)[:, :, half * (D // 2):half * (D // 2) + D // 2]
                    v_.tensor_tensor(cols, cols, tmp[:, 0:heads * XD].rearrange("p (t d) -> p t d", t=tiles), ALU.add
                                     ).then_inc(s["x2"], 1)
                    hold(dve, s["x2"], k * 3 - 3 + w + 1)

                if x:
                    cross_out(0)
                if a:
                    dve.wait_ge(s["n_t"], k + 1)
                    link(v_.tensor_copy(xp[0], pt[:]))
                    v_.tensor_tensor(xr, pt[:], xp[0], ALU.subtract).then_inc(s["n_rem"], 1)
                    hold(dve, s["n_rem"], k + 1)
                    link(v_.tensor_copy(xp[1], xr))
                    v_.tensor_tensor(xp[2], xr, xp[1], ALU.subtract).then_inc(s["n_split"], 1)
                if x:
                    cross_out(1)
                if n:
                    token_weights(k + 1)
                if g:
                    take_slots(k)
                if x:
                    cross_out(2)
                    norm_tile(3, k - 1, 0)
                    link(norm_tile(3, k - 1, 1))
                    norm_stats(3)
                    if not a:
                        shared_hidden(0, 2, qa)
                if not isinstance(k, int):
                    assert chain["n"] == LOOP_STEPS, chain["n"]

            @peeled(dve, N // NB)
            def _(n):
                if not isinstance(n, int):
                    dve.wait_ge(s["sh_down"], n * 4)
                    for m in range(DC):
                        shared_hidden(n, m, duo[m % 2])
                for t in range(4):
                    dve.wait_ge(s["sh_down"], n * 4 + t + 1)
                    cols = res[:, bass.ds(n * (4 * D) + t * D, D)]
                    v_.tensor_tensor(cols, cols, pt[:, t % 2 * D:t % 2 * D + D], ALU.add).then_inc(s["res_final"], 1)

            def weigh_out(i, r):
                dve.wait_ge(s["down_done"], i * EU + r + 1)
                if isinstance(i, int) and i * EU + r < 2:
                    pass
                else:
                    dve.wait_ge(y_out, i * (EU * 16) + (r - 1) * 16)
                v_.tensor_scalar(ye[r % 2], quad[2 + r % 2], iw[:, bass.ds((i * EU + r) * 2 + 1, 1)].bitcast(F32), None,
                                 ALU.mult
                                 ).then_inc(s["y_ready"], 1)

            @expert_rounds(dve)
            def _(i, first, last):
                for r in range(EU):
                    dve.wait_ge(s["th_done"], i * EU + r + 1)
                    if not first or r >= 2:
                        dve.wait_ge(s["ht_t"], i * EU + r - 1)
                    v_.scalar_tensor_tensor(th_e[r % 2], th_e[r % 2], 1.0, quad[r % 2][:, 0:F], ALU.add, ALU.mult
                                            ).then_inc(s["ga_done"], 1)
                    dve.wait_ge(s["ga_done"], i * EU + r + 1)
                    v_.scalar_tensor_tensor(he[r % 2], th_e[r % 2], 0.5, quad[r % 2][:, F:2 * F], ALU.mult,
                                            ALU.mult).then_inc(s["h_done"], 1)
                    if not first or r > 0:
                        weigh_out(i, r - 1)
                if last:
                    weigh_out(i, EU - 1)

        @block.tensor
        def _(pe):
            mm, tr = nc.tensor.matmul, nc.tensor.transpose

            def transpose_norm(src, dst, signal, tiles=(0, 1)):
                for t in tiles:
                    for c in range(DC):
                        op = tr(dst[:, c * S + t * P:c * S + t * P + P], src[:, t * D + c * P:t * D + c * P + P],
                                ident[:])
                if 1 in tiles:
                    op.then_inc(s[signal], 1)

            pe.wait_ge(s["const_ready"], 1)
            pe.wait_ge(s["xn1"], 1)
            transpose_norm(xn1, qa, "x_t")

            def shared_gate_up(n, m, bank):
                for half, w in enumerate((sg_s, su_s)):
                    for c in range(DC):
                        op = mm(bank[:, half * NB:half * NB + NB], w[:, c, m * P:m * P + P],
                                xt3[:, bass.ds(n * 2, 2), c, :], start=c == 0, stop=c == DC - 1)
                op.then_inc(s["sh_gu"], 1)

            @pipelined(pe)
            def _(k, a, x, g, n):
                if a:
                    pe.wait_ge(s["diag"], k + 1)
                    pe.wait_ge(s["xt_ready"], k + 1)
                    for t in range(2):
                        op = mm(qa[:, t * P:t * P + P], ones[:], dg[:, t * P:t * P + P], start=True, stop=True)
                    op.then_inc(s["cw_t"], 1)
                    pe.wait_ge(s["at_ready"], k * KVH)
                    if g:
                        pe.wait_ge(s["x2"], k * 3 - 4)
                    if isinstance(k, int) and k == 0:
                        pe.wait_ge(s["w_in"], 4 * 16)
                    for half in range(2):
                        for c in range(DC):
                            op = mm(va[:, half * S:half * S + S], wkv_s[:, c, half * P:half * P + P], xt[:, c, :],
                                    start=c == 0, stop=c == DC - 1)
                    op.then_inc(s["k_t"], 1)

                def third_norm(t):
                    if t == 0:
                        pe.wait_ge(s["xn3"], k - 1)
                        pe.wait_ge(s["x2"], k * 3 - 3)
                    transpose_norm(xn3, pt, "t3_t", (t,))

                def logits(c):
                    if c == 0:
                        pe.wait_ge(s["xt3_ready"], k - 1)
                        pe.wait_ge(s["ox_ready"], k * 4 - 4)
                    op = mm(vb[0:NE, 0:S], gw_s[:, c, :], xt3[:, bass.ds(k - 2, 1), c, :], start=c == 0,
                            stop=c == DC - 1)
                    if c == DC - 1:
                        op.then_inc(s["g_mm"], 1)

                def logits_back():
                    hold(pe, s["gl_ready"], k - 1)
                    for t in range(2):
                        op = tr(vb[:, S + t * NE:S + t * NE + NE], gl[:, t * P:t * P + P], ident[0:NE, 0:NE])
                    op.then_inc(s["g_t"], 1)

                def queries(ch):
                    if ch == 0:
                        pe.wait_ge(s["cwb_ready"], k + 1)
                    for c in range(DC):
                        op = mm(qa[:, ch * S:ch * S + SQ], wq_s[:, c, ch * P:ch * P + P], xt[:, c, GLOB:S],
                                start=c == 0, stop=c == DC - 1)
                    if ch == DC - 1:
                        op.then_inc(s["q_t"], 1)

                def values():
                    pe.wait_ge(s["vt_ready"], k + 1)
                    pe.wait_ge(s["k_split"], k + 1)
                    for m, t0 in enumerate((0, P, GLOB)):
                        op = tr(va[:, m * P:m * P + P], vt[:, t0:t0 + P], ident[:])
                    op.then_inc(s["v_t"], 1)

                def context():
                    pe.wait_ge(s["v_ready"], k + 1)
                    pe.wait_ge(s["ctx_in"], k * 16 + 16)
                    for t in range(2):
                        op = tr(va[:, t * P:t * P + P], ctx_s[:, t * P:t * P + P], ident[:])
                    op.then_inc(s["c_t"], 1)

                def self_scores(u):
                    if u == 0:
                        pe.wait_ge(s["ks_in"], k * 96 + 96)
                        pe.wait_ge(s["qs_in"], k * 48 + 48)
                    q, blk = u // 2, u % 2
                    rows = SPLIT_ROWS + ALIBI_ROWS
                    if u >= 2:
                        pe.wait_ge(s["s_max"], k * AU + u - 1)
                    mm(abank[u % 2], identb[:], masks[:, blk, :], start=True, stop=False)
                    for h in range(4):
                        op = mm(abank[u % 2][:, h * P:h * P + P], qs[0:rows, q * 4 + h, blk * GLOB:blk * GLOB + P],
                                ks[0:rows, blk, q, :], start=False, stop=h == 3)
                    op.then_inc(s["s_unit"], 1)

                if x and not a:
                    pe.wait_ge(s["gate_up_in"], 2 * 16)
                    shared_gate_up(0, 0, qa)
                if x:
                    if a:
                        for ch in range(DC):
                            if AT_QUERY[ch] < 0:
                                queries(ch)
                    if g and not (isinstance(k, int) and k == 2):
                        pe.wait_ge(s["slot_ready"], k - 2)
                    pe.wait_ge(s["kxs_in"], k * 96)
                    pe.wait_ge(s["qxs_in"], k * 96)
                    for v in range(XU):
                        kv, t, half = v // 4, v // 2 % 2, v % 2
                        if v >= 2:
                            pe.wait_ge(s["x_max"], k * XU - XU + v - 1)
                        for h in range(2):
                            op = mm(xbank[v % 2][:, h * S:h * S + S],
                                    qxs[0:XSPLIT_ROWS, kv * 4 + half * 2 + h, t * P:t * P + P],
                                    kxs[0:XSPLIT_ROWS, kv, :], start=True, stop=True)
                        op.then_inc(s["xs_unit"], 1)
                        if a:
                            for ch in range(DC):
                                if v == AT_QUERY[ch]:
                                    queries(ch)
                            if v == AT_CONTEXT - 3:
                                values()
                            elif v == AT_CONTEXT:
                                context()
                            if v in AT_SELF:
                                self_scores(AT_SELF.index(v))
                        if g:
                            if v in (AT_THIRD, AT_THIRD + 1):
                                third_norm(v - AT_THIRD)
                            elif AT_LOGITS <= v < AT_LOGITS + DC:
                                logits(v - AT_LOGITS)
                            elif v == AT_LOGITS + DC + 1:
                                logits_back()
                    pe.wait_ge(s["x_max"], k * XU)
                    if g:
                        pe.wait_ge(s["th_ready"], k - 1)
                    for t in range(2):
                        op = tr(vb[0:XH, t * P:t * P + P], mxx[:, t * XH:t * XH + XH], ident[:])
                    op.then_inc(s["xm_t"], 1)
                else:
                    if a:
                        for ch in range(DC):
                            queries(ch)
                        values()
                        context()
                    if g:
                        third_norm(0)
                        third_norm(1)
                        for c in range(DC):
                            logits(c)
                        logits_back()
                if a:
                    for u in range(len(AT_SELF) if x else 0, AU):
                        self_scores(u)
                    pe.wait_ge(s["s_max"], k * AU + AU)
                    tr(pt[0:H, 0:P], mx[:, 0:H], ident[:])
                    tr(pt[0:H, 256:256 + P], mx[:, H:2 * H], ident[:]).then_inc(s["m_t"], 1)

                if x and not a:
                    pe.wait_ge(s["sh_h"], 1)
                    shared_gate_up(0, 1, qa)

                def xkeyed(v):
                    kv, t, half = v // 4, v // 2 % 2, v % 2
                    if v >= 2:
                        pe.wait_ge(s["xe_ready"], k * XU - XU + v - 1)
                    h = kv * 4 + half * 2
                    mm(xbank[v % 2], kxs[0:XSPLIT_ROWS + SHIFT_ROWS, kv, t * P:t * P + P],
                       qxs[0:XSPLIT_ROWS + SHIFT_ROWS, h:h + 2, :], start=True, stop=True).then_inc(s["xst_unit"], 1)

                def xweigh(v):
                    kv, t, half = v // 4, v // 2 % 2, v % 2
                    pe.wait_ge(s["xe_ready"], k * XU - XU + v + 1)
                    if v >= 8 and v % 8 == 0:
                        pe.wait_ge(s["ox_ready"], k * 4 - 4 + v // 8)
                    for h in range(2):
                        at_ = (half * 2 + h) * 32
                        op = mm(vb[at_:at_ + 32, kv % 2 * S:kv % 2 * S + S], vx[:, t, kv, :],
                                ex[v % 4][:, h * S:h * S + S], start=t == 0, stop=t == 1, tile_position=(0, at_))
                    op.then_inc(s["xpv_done"], 1)

                def cross(v):
                    xkeyed(v)
                    if v >= 2:
                        xweigh(v - 2)

                def keyed(u):
                    q, blk = u // 2, u % 2
                    if u >= 2:
                        pe.wait_ge(s["e_ready"], k * AU + u - 1)
                    rows = SPLIT_ROWS + ALIBI_ROWS + SHIFT_ROWS
                    mm(abank[u % 2], identb[:], masks[:, 1 - blk, :], start=True, stop=False)
                    mm(abank[u % 2], ks[0:rows, blk, q, :], qs[0:rows, q * 4:q * 4 + 4, blk * GLOB:blk * GLOB + P],
                       start=False, stop=True).then_inc(s["st_unit"], 1)

                def weigh(q):
                    pe.wait_ge(s["e_ready"], k * AU + 2 * q + 2)
                    if q >= 1:
                        pe.wait_ge(s["at_ready"], k * KVH + q)
                    far, near = (e4[(2 * q + m) % 4].rearrange("p (h n) -> p h n", h=4) for m in range(2))
                    vals = slice(q * HD, q * HD + HD)
                    for kind in range(6):
                        for h in range(4):
                            o = va[h * HD:h * HD + HD]
                            kw = dict(start=kind == 0, stop=kind == 5, skip_group_check=True,
                                      tile_position=(0, h * HD))
                            if kind == 0:
                                op = mm(o[:, 0:GLOB], vs[:, 0, vals], ones[:, 0:GLOB], **kw)
                            elif kind == 1:
                                op = mm(o[:, 0:GLOB], vs[:, 1, vals], ones[:, 0:GLOB], **kw)
                            elif kind == 2:
                                op = mm(o[:, GLOB:GLOB + P], vs[:, 1, vals], far[:, h, :], **kw)
                            elif kind == 3:
                                op = mm(o[:, P:S], vs[:, 2, vals], near[:, h, :], **kw)
                            elif kind == 4:
                                op = mm(o[:, S + GLOB:S + GLOB + P], ones[:, 0:HD], far[:, h, :], **kw)
                            else:
                                op = mm(o[:, S + P:2 * S], ones[:, 0:HD], near[:, h, :], **kw)
                    op.then_inc(s["pv_done"], 1)

                def project(t):
                    for q in range(DC):
                        op = mm(qa[:, t * D:t * D + D], at[:, q, t * P:t * P + P], wo_s[:, q, :],
                                start=q == 0, stop=q == DC - 1)
                    op.then_inc(s["wo_done"], 1)

                def cross_back(w):
                    half = w // 2
                    pe.wait_ge(s["ox_ready"], k * 4 - 4 + 2 * half + 2)
                    if w == 1:
                        pe.wait_ge(s["x2"], k * 3 - 3 + w)
                    for i, t in enumerate((w,) if w < 2 else (0, 1)):
                        for m in range(4):
                            at_, kv = i * 512 + m * P, half * 4 + m
                            op = tr(xo_bank[w][:, at_:at_ + P], ox[:, kv * S + t * P:kv * S + t * P + P], ident[:])
                    op.then_inc(s["xo_t"], 1)

                if x:
                    pe.wait_ge(s["xshift_in"], k * 32)
                    pe.wait_ge(s["vx_ready"], k)
                    for v in range(LEAD):
                        cross(v)
                for j in range(AU):
                    if a:
                        if j == 0:
                            pe.wait_ge(s["shift_in"], k * 32 + 32)
                            pe.wait_ge(s["c_rem"], k + 1)
                        keyed(j)
                    if x:
                        cross(LEAD + j)
                    if a and j % 2 == 0 and j >= 2:
                        weigh(j // 2 - 1)
                done = LEAD + AU
                if x:
                    cross(done)
                if a:
                    weigh(3)
                if x:
                    cross(done + 1)
                    cross(done + 2)
                    cross(done + 3)
                if a:
                    pe.wait_ge(s["at_ready"], k * KVH + KVH)
                    pe.wait_ge(s["e_ready"], k * AU + AU)
                    project(0)
                if x:
                    cross(done + 4)
                if a:
                    project(1)
                if x:
                    for v in range(done + 5, XU):
                        cross(v)
                        if v == AT_OUT:
                            cross_back(0)
                        elif v == AT_OUT + 6:
                            cross_back(1)
                        if a and v == AT_NORM:
                            pe.wait_ge(s["xn2"], k + 1)
                            transpose_norm(xn2, pt, "n_t")
                        if n and v == AT_FIRST:
                            pe.wait_ge(s["xn1"], k + 2)
                            transpose_norm(xn1, qa, "x_t")
                    xweigh(XU - 2)
                    xweigh(XU - 1)
                elif a:
                    pe.wait_ge(s["xn2"], k + 1)
                    transpose_norm(xn2, pt, "n_t")
                    pe.wait_ge(s["xn1"], k + 2)
                    transpose_norm(xn1, qa, "x_t")
                if not a and not x:
                    pe.wait_ge(s["sh_h"], 3)
                    shared_gate_up(0, 3, qa)
                if g:
                    pe.wait_ge(s["chosen"], k - 1)
                    count = xbank[0]
                    mm(count[:, 0:2 * NE], trib[:], chosen[:], start=True, stop=False, skip_group_check=True)
                    mm(count[:, NE:2 * NE], onesb[:], chosen[:, 0:NE], start=False, stop=False, skip_group_check=True)
                    mm(count[:, 2 * NE:3 * NE], onesb[:], chosen[:, 0:NE], start=False, stop=False,
                       skip_group_check=True)
                    mm(count[:, 2 * NE:3 * NE], onesb[:], chosen[:, NE:2 * NE], start=False, stop=True,
                       skip_group_check=True).then_inc(s["pos_t"], 1)
                if x:
                    if a:
                        pe.wait_ge(s["n_rem"], k + 1)
                    cross_back(2)
                    if not a:
                        pe.wait_ge(s["sh_h"], 2)
                        shared_gate_up(0, 2, qa)

            pe.wait_ge(s["ffn_in"], 16)

            @peeled(pe, N // NB)
            def _(n):
                if not isinstance(n, int):
                    for m in range(DC):
                        pe.wait_ge(s["sh_h"], n * DC + max(m - 1, 0))
                        shared_gate_up(n, m, duo[m % 2])
                pe.wait_ge(s["sh_h"], n * DC + DC)
                for t in range(4):
                    pe.wait_ge(s["res_final"], n * 4 + max(t - 1, 0))
                    for c in range(DC):
                        op = mm(pt[:, t % 2 * D:t % 2 * D + D], ht_sh[:, c, t * P:t * P + P], sd_s[:, c, :],
                                start=c == 0, stop=c == DC - 1)
                    op.then_inc(s["sh_down"], 1)
                if isinstance(n, int):
                    pe.wait_ge(s["slot_ready"], B)

            def bring(i, r):
                pe.wait_ge(s["xg_ready"], i * EU + r + 1)
                if not (isinstance(i, int) and i * EU + r < 2):
                    pe.wait_ge(s["xe_tr"], i * EU + r - 1)
                for c in range(DC):
                    op = tr(pt[:, r % 2 * 512 + c * P:r % 2 * 512 + c * P + P],
                            xg[r % 2][:, c, :], ident[:])
                op.then_inc(s["xe_t"], 1)

            def down(i, r):
                pe.wait_ge(s["ht_ready"], i * EU + r + 1)
                if not (isinstance(i, int) and i * EU + r < 2):
                    pe.wait_ge(s["y_ready"], i * EU + r - 1)
                for c in range(2):
                    op = mm(quad[2 + r % 2], hte[r % 2][:, c, :], h2[r % EU][:, c, :], start=c == 0, stop=c == 1)
                op.then_inc(s["down_done"], 1)

            pe.wait_ge(s["res_final"], N // NB * 4)
            bring(0, 0)

            @expert_rounds(pe)
            def _(i, first, last):
                for r in range(EU):
                    pe.wait_ge(wg_in[r], i * 48 + 48)
                    pe.wait_ge(s["xe_tr"], i * EU + r + 1)
                    if not first or r >= 2:
                        pe.wait_ge(s["h_done"], i * EU + r - 1)
                    for c in range(DC):
                        op = mm(quad[r % 2], xgt[r % 2][:, c, :], h13[r][:, c, :], start=c == 0, stop=c == DC - 1)
                    op.then_inc(s["up_done"], 1)
                    if not last or r + 1 < EU:
                        bring(i, r + 1)
                    if not first or r > 0:
                        down(i, r - 1)
                    pe.wait_ge(s["h_done"], i * EU + r + 1)
                    if not first or r >= 2:
                        pe.wait_ge(s["ht_ready"], i * EU + r - 1)
                    for c in range(2):
                        op = tr(pv[r % 2][:, c * P:c * P + P], he[r % 2].rearrange("p (n c) -> p c n", c=2)[:, c, :],
                                ident[:])
                    op.then_inc(s["ht_t"], 1)
                if last:
                    down(i, EU - 1)


_INS = ["x", "ctx_512", "L0_attn_Wq", "L0_attn_Wkv", "L0_attn_Wo", "L0_attn_bo", "L0_ffn_gate_w", "L0_ffn_gate_bias",
        "L0_ffn_w1", "L0_ffn_w2", "L0_ffn_w3", "L0_ffn_shared_gate", "L0_ffn_shared_up", "L0_ffn_shared_down"]


def kernel(**inputs):
    import numpy as _np
    import concourse.bacc as _bacc
    from concourse import mybir as _mybir
    from concourse.bass_utils import run_bass_kernel_spmd as _run

    nc = _bacc.Bacc("TRN2", target_bir_lowering=False, num_devices=1)
    arrays, args = {}, []
    given = {n: _np.asarray(inputs[n]) for n in _INS}
    given["L0_ffn_gate_w"] = given["L0_ffn_gate_w"].T
    given.update(constants())
    for name, a in given.items():
        a = _np.ascontiguousarray(a)
        arrays[f"in_{name}"] = a
        args.append(nc.dram_tensor(f"in_{name}", a.shape, _mybir.dt.from_np(a.dtype), kind="ExternalInput").ap())
    o = nc.dram_tensor("out_0", (B, S, D), _mybir.dt.float32, kind="ExternalOutput").ap()
    build(nc, *args, o)
    r = _run(nc, [arrays], core_ids=[0])
    return r.results[0]["out_0"]
```
